# Optimizing a Trainium2 kernel written in Bass

```python
import numpy as np
import jax
import jax.numpy as jnp

def _softmax(x, axis=-1):
    return jax.nn.softmax(x, axis=axis)

def _gelu(x):
    return jax.nn.gelu(x, approximate=True)

def _silu(x):
    return jax.nn.silu(x)

def _sigmoid(x):
    return jax.nn.sigmoid(x)

def _layernorm(x, axis=-1, eps=1e-05):
    m = jnp.mean(x, axis=axis, keepdims=True)
    v = jnp.var(x, axis=axis, keepdims=True)
    return (x - m) / jnp.sqrt(v + eps)

def _scatter_add(tgt, idx, src, axis=0):
    return tgt.at[idx].add(src)

def _segment_sum(src, seg, n):
    return jax.ops.segment_sum(src, seg, n)
kernel_name = 'mk_seq_preln_d2_jaxref_r8_d56496'

def setup_inputs(seed: int=0):
    np.random.seed(seed)
    _w = jnp.asarray

    def _L0_attn_setup():
        import jax, jax.numpy as jnp
        import numpy as np
        EPS = 1e-05
        H = 16

        def rms(x, w=None):
            y = x * jax.lax.rsqrt(jnp.mean(jnp.square(x), axis=-1, keepdims=True) + EPS)
            return y * w if w is not None else y

        def rotate_every_two(x):
            x1 = x[..., ::2]
            x2 = x[..., 1::2]
            return jnp.stack([-x2, x1], axis=-1).reshape(x.shape)

        def theta_shift(x, sin, cos):
            return x * cos + rotate_every_two(x) * sin

        def retnet_rel_pos(S, Dh):
            angle = 1.0 / 10000.0 ** jnp.linspace(0.0, 1.0, Dh // 2)
            angle = jnp.repeat(angle, 2)
            idx = jnp.arange(S, dtype=jnp.float32)
            sin = jnp.sin(idx[:, None] * angle[None, :])
            cos = jnp.cos(idx[:, None] * angle[None, :])
            decay = jnp.log(1.0 - 2.0 ** (-5.0 - jnp.arange(H, dtype=jnp.float32)))
            i = jnp.arange(S)[:, None]
            j = jnp.arange(S)[None, :]
            expnt = jnp.where(i >= j, (i - j).astype(jnp.float32)[None, :, :] * decay[:, None, None], -jnp.inf)
            mask = jnp.exp(expnt)
            mask = jnp.nan_to_num(mask)
            mask = mask / jnp.sqrt(jnp.sum(mask, axis=-1, keepdims=True))
            return (sin, cos, mask)
        key = jax.random.key(seed)
        B, S, E, F = (4, 128, 256, 1024)
        ks = jax.random.split(key, 12)
        sE = 1.0 / np.sqrt(E)
        sF = 1.0 / np.sqrt(F)
        return {'x': jax.random.normal(ks[0], (B, S, E), jnp.float32), 'q_w': jax.random.normal(ks[1], (E, E), jnp.float32) * sE, 'k_w': jax.random.normal(ks[2], (E, E), jnp.float32) * sE, 'v_w': jax.random.normal(ks[3], (E, E), jnp.float32) * sE, 'g_w': jax.random.normal(ks[4], (E, E), jnp.float32) * sE, 'out_w': jax.random.normal(ks[5], (E, E), jnp.float32) * sE, 'fc1_w': jax.random.normal(ks[6], (E, F), jnp.float32) * sE, 'fc1_b': jnp.zeros((F,), jnp.float32), 'fc2_w': jax.random.normal(ks[7], (F, E), jnp.float32) * sF, 'fc2_b': jnp.zeros((E,), jnp.float32), 'retn_norm_w': jnp.ones((E,), jnp.float32), 'final_norm_w': jnp.ones((E,), jnp.float32)}
    _L0_attn_in = _L0_attn_setup()

    def _L0_ffn_setup():
        import jax, jax.numpy as jnp
        import numpy as np
        HIDDEN = 256
        INTER = 1024
        SCALE = 64.0

        def fwht(x):
            orig_shape = x.shape
            n = orig_shape[-1]
            x = x.reshape(-1, n)
            h = 1
            while h < n:
                x = x.reshape(-1, n // (2 * h), 2, h)
                a, b = (x[:, :, 0, :], x[:, :, 1, :])
                x = jnp.stack([a + b, a - b], axis=2).reshape(-1, n)
                h *= 2
            return (x / jnp.sqrt(jnp.asarray(n, x.dtype))).reshape(orig_shape)
        key = jax.random.key(seed)
        ks = jax.random.split(key, 8)
        inp = jax.random.normal(ks[0], (4, 256, HIDDEN), dtype=jnp.float32)
        SU_ug = jnp.where(jax.random.bernoulli(ks[1], 0.5, (HIDDEN,)), 1.0, -1.0).astype(jnp.float32)
        SU_dp = jnp.where(jax.random.bernoulli(ks[2], 0.5, (INTER,)), 1.0, -1.0).astype(jnp.float32)
        Wscale_ug = jax.random.uniform(ks[3], (2 * INTER,), jnp.float32, 0.5, 1.5)
        Wscale_dp = jax.random.uniform(ks[4], (HIDDEN,), jnp.float32, 0.5, 1.5)
        W_up = jax.random.normal(ks[5], (INTER, HIDDEN), dtype=jnp.float32) * 0.02
        W_gate = jax.random.normal(ks[6], (INTER, HIDDEN), dtype=jnp.float32) * 0.02
        W_down = jax.random.normal(ks[7], (HIDDEN, INTER), dtype=jnp.float32) * 0.02
        return {'input': inp, 'SU_ug': SU_ug, 'SU_dp': SU_dp, 'Wscale_ug': Wscale_ug, 'Wscale_dp': Wscale_dp, 'W_up': W_up, 'W_gate': W_gate, 'W_down': W_down}
    _L0_ffn_in = _L0_ffn_setup()

    def _L1_attn_setup():
        import jax, jax.numpy as jnp
        import numpy as np
        HIDDEN = 256
        KEY = 256
        EPS = 1e-05
        key = jax.random.key(seed)
        k1, k2, k3 = jax.random.split(key, 3)
        B, S = (4, 256)
        x = jax.random.normal(k1, (B, S, HIDDEN), dtype=jnp.float32)
        bq = 1.0 / np.sqrt(HIDDEN)
        qkv = jax.random.uniform(k2, (HIDDEN, KEY * 3), minval=-bq, maxval=bq, dtype=jnp.float32)
        bo = 1.0 / np.sqrt(KEY)
        o_proj = jax.random.uniform(k3, (KEY, HIDDEN), minval=-bo, maxval=bo, dtype=jnp.float32)
        gamma = jnp.ones((HIDDEN,), dtype=jnp.float32)
        beta = jnp.zeros((HIDDEN,), dtype=jnp.float32)
        return {'x': x, 'qkv': qkv, 'o_proj': o_proj, 'gamma': gamma, 'beta': beta}
    _L1_attn_in = _L1_attn_setup()

    def _L1_ffn_setup():
        import jax, jax.numpy as jnp
        import numpy as np
        NUM_EXPERTS = 16
        TOP_K = 2
        HIDDEN = 256
        D_FF = 512
        BATCH, SEQ = (4, 256)

        def _moe_forward(hidden, router_w, W1, W2):
            B, S, D = hidden.shape
            x = hidden.reshape(-1, D)
            T = x.shape[0]
            logits = x @ router_w
            top_vals, top_ids = jax.lax.top_k(logits, TOP_K)
            probs = jax.nn.softmax(top_vals, axis=-1)
            combine = jnp.zeros((T, NUM_EXPERTS), dtype=x.dtype)
            combine = combine.at[jnp.arange(T)[:, None], top_ids].add(probs)
            out = jnp.zeros_like(x)
            for e in range(NUM_EXPERTS):
                h = jax.nn.silu(x @ W1[e]) @ W2[e]
                out = out + combine[:, e:e + 1] * h
            return out.reshape(B, S, D)
        key = jax.random.key(seed)
        k_h, k_r, k_w1, k_w2 = jax.random.split(key, 4)
        hidden = jax.random.normal(k_h, (BATCH, SEQ, HIDDEN), dtype=jnp.float32)
        router_w = jax.random.normal(k_r, (HIDDEN, NUM_EXPERTS), dtype=jnp.float32) * HIDDEN ** (-0.5)
        W1 = jax.random.normal(k_w1, (NUM_EXPERTS, HIDDEN, D_FF), dtype=jnp.float32) * HIDDEN ** (-0.5)
        W2 = jax.random.normal(k_w2, (NUM_EXPERTS, D_FF, HIDDEN), dtype=jnp.float32) * D_FF ** (-0.5)
        return {'hidden': hidden, 'router_w': router_w, 'W1': W1, 'W2': W2}
    _L1_ffn_in = _L1_ffn_setup()
    _d = {'L0_attn_x': _L0_attn_in['x'], 'L0_attn_q_w': _L0_attn_in['q_w'], 'L0_attn_k_w': _L0_attn_in['k_w'], 'L0_attn_v_w': _L0_attn_in['v_w'], 'L0_attn_g_w': _L0_attn_in['g_w'], 'L0_attn_out_w': _L0_attn_in['out_w'], 'L0_attn_fc1_w': _L0_attn_in['fc1_w'], 'L0_attn_fc1_b': _L0_attn_in['fc1_b'], 'L0_attn_fc2_w': _L0_attn_in['fc2_w'], 'L0_attn_fc2_b': _L0_attn_in['fc2_b'], 'L0_attn_retn_norm_w': _L0_attn_in['retn_norm_w'], 'L0_attn_final_norm_w': _L0_attn_in['final_norm_w'], 'L0_ffn_SU_ug': _L0_ffn_in['SU_ug'], 'L0_ffn_SU_dp': _L0_ffn_in['SU_dp'], 'L0_ffn_Wscale_ug': _L0_ffn_in['Wscale_ug'], 'L0_ffn_Wscale_dp': _L0_ffn_in['Wscale_dp'], 'L0_ffn_W_up': _L0_ffn_in['W_up'], 'L0_ffn_W_gate': _L0_ffn_in['W_gate'], 'L0_ffn_W_down': _L0_ffn_in['W_down'], 'L1_attn_qkv': _L1_attn_in['qkv'], 'L1_attn_o_proj': _L1_attn_in['o_proj'], 'L1_attn_gamma': _L1_attn_in['gamma'], 'L1_attn_beta': _L1_attn_in['beta'], 'L1_ffn_router_w': _L1_ffn_in['router_w'], 'L1_ffn_W1': _L1_ffn_in['W1'], 'L1_ffn_W2': _L1_ffn_in['W2']}
    _x0 = _d['L0_attn_x']
    _d['L0_attn_x'] = jax.random.normal(jax.random.fold_in(jax.random.key(seed), 1), (1, 1024, 256), dtype=_x0.dtype)
    del _x0
    return _d

def reference(L0_attn_x, L0_attn_q_w, L0_attn_k_w, L0_attn_v_w, L0_attn_g_w, L0_attn_out_w, L0_attn_fc1_w, L0_attn_fc1_b, L0_attn_fc2_w, L0_attn_fc2_b, L0_attn_retn_norm_w, L0_attn_final_norm_w, L0_ffn_SU_ug, L0_ffn_SU_dp, L0_ffn_Wscale_ug, L0_ffn_Wscale_dp, L0_ffn_W_up, L0_ffn_W_gate, L0_ffn_W_down, L1_attn_qkv, L1_attn_o_proj, L1_attn_gamma, L1_attn_beta, L1_ffn_router_w, L1_ffn_W1, L1_ffn_W2):

    def _L0_attn_ref(x, q_w, k_w, v_w, g_w, out_w, fc1_w, fc1_b, fc2_w, fc2_b, retn_norm_w, final_norm_w):
        import jax, jax.numpy as jnp
        import numpy as np
        EPS = 1e-05
        H = 16

        def rms(x, w=None):
            y = x * jax.lax.rsqrt(jnp.mean(jnp.square(x), axis=-1, keepdims=True) + EPS)
            return y * w if w is not None else y

        def rotate_every_two(x):
            x1 = x[..., ::2]
            x2 = x[..., 1::2]
            return jnp.stack([-x2, x1], axis=-1).reshape(x.shape)

        def theta_shift(x, sin, cos):
            return x * cos + rotate_every_two(x) * sin

        def retnet_rel_pos(S, Dh):
            angle = 1.0 / 10000.0 ** jnp.linspace(0.0, 1.0, Dh // 2)
            angle = jnp.repeat(angle, 2)
            idx = jnp.arange(S, dtype=jnp.float32)
            sin = jnp.sin(idx[:, None] * angle[None, :])
            cos = jnp.cos(idx[:, None] * angle[None, :])
            decay = jnp.log(1.0 - 2.0 ** (-5.0 - jnp.arange(H, dtype=jnp.float32)))
            i = jnp.arange(S)[:, None]
            j = jnp.arange(S)[None, :]
            expnt = jnp.where(i >= j, (i - j).astype(jnp.float32)[None, :, :] * decay[:, None, None], -jnp.inf)
            mask = jnp.exp(expnt)
            mask = jnp.nan_to_num(mask)
            mask = mask / jnp.sqrt(jnp.sum(mask, axis=-1, keepdims=True))
            return (sin, cos, mask)
        B, S, E = x.shape
        Dh = E // H
        scaling = Dh ** (-0.5)
        sin, cos, mask = retnet_rel_pos(S, Dh)
        residual = x
        h = rms(x, retn_norm_w)
        q = h @ q_w
        k = h @ k_w * scaling
        v = h @ v_w
        g = h @ g_w

        def split_heads(t):
            return t.reshape(B, S, H, Dh).transpose(0, 2, 1, 3)
        q, k, v_h = (split_heads(q), split_heads(k), split_heads(v))
        qr = theta_shift(q, sin, cos)
        kr = theta_shift(k, sin, cos)
        qk = jnp.einsum('bhsd,bhtd->bhst', qr, kr) * mask
        denom = jnp.clip(jnp.abs(jax.lax.stop_gradient(jnp.sum(qk, axis=-1, keepdims=True))), 1.0, None)
        qk = qk / denom
        o = jnp.einsum('bhst,bhtd->bhsd', qk, v_h)
        o = o.transpose(0, 2, 1, 3)
        o = rms(o)
        o = o.reshape(B, S, E)
        o = jax.nn.silu(g) * o
        o = o @ out_w
        x = residual + o
        residual = x
        h = rms(x, final_norm_w)
        h = jax.nn.gelu(h @ fc1_w + fc1_b)
        h = h @ fc2_w + fc2_b
        return residual + h

    def _L0_ffn_ref(input, SU_ug, SU_dp, Wscale_ug, Wscale_dp, W_up, W_gate, W_down):
        import jax, jax.numpy as jnp
        import numpy as np
        HIDDEN = 256
        INTER = 1024
        SCALE = 64.0

        def fwht(x):
            orig_shape = x.shape
            n = orig_shape[-1]
            x = x.reshape(-1, n)
            h = 1
            while h < n:
                x = x.reshape(-1, n // (2 * h), 2, h)
                a, b = (x[:, :, 0, :], x[:, :, 1, :])
                x = jnp.stack([a + b, a - b], axis=2).reshape(-1, n)
                h *= 2
            return (x / jnp.sqrt(jnp.asarray(n, x.dtype))).reshape(orig_shape)
        n = SU_ug.shape[0]
        x = input.reshape(-1, n)
        x = fwht(x * SU_ug) / SCALE
        x_up = x @ W_up.T * (Wscale_ug[:INTER] * SCALE)
        x_gate = x @ W_gate.T * (Wscale_ug[INTER:] * SCALE)
        x = jax.nn.silu(x_gate) * x_up
        x = fwht(x * SU_dp) / SCALE
        x = x @ W_down.T * (Wscale_dp * SCALE)
        return x.reshape(input.shape)

    def _L1_attn_ref(x, qkv, o_proj, gamma, beta):
        import jax, jax.numpy as jnp
        import numpy as np
        HIDDEN = 256
        KEY = 256
        EPS = 1e-05
        residual = x
        mu = jnp.mean(x, axis=-1, keepdims=True)
        var = jnp.mean((x - mu) ** 2, axis=-1, keepdims=True)
        x_norm = (x - mu) / jnp.sqrt(var + EPS) * gamma + beta
        q = x_norm @ qkv[:, :KEY]
        k = x_norm @ qkv[:, KEY:2 * KEY]
        v = x_norm @ qkv[:, 2 * KEY:]
        scale = 1.0 / jnp.sqrt(jnp.float32(KEY))
        scores = jnp.einsum('bsk,btk->bst', q, k) * scale
        S_len = x.shape[1]
        causal = jnp.tril(jnp.ones((S_len, S_len), dtype=bool))
        scores = jnp.where(causal[None], scores, -jnp.inf)
        attn = jax.nn.softmax(scores, axis=-1)
        out = attn @ v
        out = out @ o_proj
        return out + residual

    def _L1_ffn_ref(hidden, router_w, W1, W2):
        import jax, jax.numpy as jnp
        import numpy as np
        NUM_EXPERTS = 16
        TOP_K = 2
        HIDDEN = 256
        D_FF = 512
        BATCH, SEQ = (4, 256)

        def _moe_forward(hidden, router_w, W1, W2):
            B, S, D = hidden.shape
            x = hidden.reshape(-1, D)
            T = x.shape[0]
            logits = x @ router_w
            top_vals, top_ids = jax.lax.top_k(logits, TOP_K)
            probs = jax.nn.softmax(top_vals, axis=-1)
            combine = jnp.zeros((T, NUM_EXPERTS), dtype=x.dtype)
            combine = combine.at[jnp.arange(T)[:, None], top_ids].add(probs)
            out = jnp.zeros_like(x)
            for e in range(NUM_EXPERTS):
                h = jax.nn.silu(x @ W1[e]) @ W2[e]
                out = out + combine[:, e:e + 1] * h
            return out.reshape(B, S, D)
        return _moe_forward(hidden, router_w, W1, W2)
    x = L0_attn_x
    x = x + _L0_attn_ref(_layernorm(x, axis=-1), L0_attn_q_w, L0_attn_k_w, L0_attn_v_w, L0_attn_g_w, L0_attn_out_w, L0_attn_fc1_w, L0_attn_fc1_b, L0_attn_fc2_w, L0_attn_fc2_b, L0_attn_retn_norm_w, L0_attn_final_norm_w)
    x = x + _L0_ffn_ref(_layernorm(x, axis=-1), L0_ffn_SU_ug, L0_ffn_SU_dp, L0_ffn_Wscale_ug, L0_ffn_Wscale_dp, L0_ffn_W_up, L0_ffn_W_gate, L0_ffn_W_down)
    x = x + _L1_attn_ref(_layernorm(x, axis=-1), L1_attn_qkv, L1_attn_o_proj, L1_attn_gamma, L1_attn_beta)
    x = x + _L1_ffn_ref(_layernorm(x, axis=-1), L1_ffn_router_w, L1_ffn_W1, L1_ffn_W2)
    return x

_drawn_inputs = setup_inputs


def setup_inputs(seed=0):
    import zlib

    import numpy as np

    out = dict(_drawn_inputs(seed))
    spreads = {'L0_attn_fc1_b': (0.0, 0.1),
     'L0_attn_fc2_b': (0.0, 0.1),
     'L0_attn_retn_norm_w': (1.0, 0.2),
     'L0_attn_final_norm_w': (1.0, 0.2),
     'L1_attn_gamma': (1.0, 0.6),
     'L1_attn_beta': (0.0, 2.0)}
    factors = {'L0_ffn_Wscale_ug': 5.186,
     'L0_ffn_Wscale_dp': 6.52,
     'L0_ffn_W_up': 2.771,
     'L0_ffn_W_gate': 2.725,
     'L1_attn_qkv': 8.0,
     'L1_attn_o_proj': 8.0,
     'L1_ffn_router_w': 8.0,
     'L1_ffn_W1': 8.0,
     'L1_ffn_W2': 8.0}
    for name, (base, spread) in spreads.items():
        noise = np.random.default_rng([zlib.crc32(name.encode()), seed]).standard_normal(out[name].shape)
        drawn = base * np.exp(spread * noise) if base else spread * noise
        out[name] = jnp.asarray(drawn.astype(out[name].dtype))
    for name, factor in factors.items():
        out[name] = (out[name] * factor).astype(out[name].dtype)
    return out
```

```python
from contextlib import ExitStack

import numpy as np

import concourse.bass as bass
from concourse import mybir

F32 = mybir.dt.float32
I32 = mybir.dt.int32
U32 = mybir.dt.uint32
ALU = mybir.AluOpType
ACT = mybir.ActivationFunctionType
AX = mybir.AxisListType

P = 128
T, D = 1024, 256
C = T // P
KT = D // P
H, DH = 16, 16
HT = H // KT
F = 1024
FM = F // P
GC = 4
G = C // GC
GW = GC * P
E, FE = 16, 512
FEM = FE // P
EW = KT * FE + FEM * D
TILES = (2 * T) // P + E - 1
EPS = 1e-5
NEG = -3.0e38


def constant_columns():
    widths = [("ident", P), ("tril", P), ("below", P), ("had", P), ("hadneg", P), ("strict", P),
              ("ones", P), ("headmask", HT), ("cos", C * DH), ("sin", C * DH), ("growth", H),
              ("rowscale", C * H), ("stateblock", KT * HT * (DH + 1)), ("statedecay", KT),
              ("iota", E), ("tileno", TILES), ("half", 1)]
    at, out = 0, {}
    for name, w in widths:
        out[name] = (at, w)
        at += w
    return out, at

def constants():
    cols, n = constant_columns()
    out = np.zeros((P, n), np.float32)

    def put(name, a):
        at, w = cols[name]
        out[:, at:at + w] = np.asarray(a, np.float64).reshape(P, w).astype(np.float32)

    i = np.arange(P)
    put("ident", np.eye(P))
    put("tril", i[:, None] <= i[None, :])
    put("below", np.where(i[None, :] > i[:, None], NEG, 0.0))
    bits = np.array([[bin(a & b).count("1") for b in range(P)] for a in range(P)])
    put("had", (-1.0) ** bits)
    put("hadneg", -((-1.0) ** bits))
    put("strict", i[:, None] < i[None, :])
    put("ones", np.ones((P, P)))
    put("headmask", i[:, None] // DH == np.arange(HT)[None, :])
    angle = (np.float32(1.0) / np.float32(10000.0) ** np.linspace(0, 1, DH // 2, dtype=np.float32)).astype(np.float32)
    angle = np.repeat(angle, 2)
    phase = (np.arange(T, dtype=np.float32)[:, None] * angle[None, :]).astype(np.float32)
    sign = np.where(np.arange(DH) % 2 == 0, -1.0, 1.0)
    put("cos", np.cos(phase.astype(np.float64)).reshape(C, P, DH).transpose(1, 0, 2))
    put("sin", (np.sin(phase.astype(np.float64)) * sign).reshape(C, P, DH).transpose(1, 0, 2))
    gamma = 1.0 - 2.0 ** (-5.0 - np.arange(H))
    put("growth", gamma[None, :] ** (-i[:, None].astype(np.float64)))
    tok = np.arange(T, dtype=np.float64)[:, None]
    rows = (1.0 - gamma[None, :] ** (tok + 1)) / (1.0 - gamma[None, :])
    scale = gamma[None, :] ** (tok % P) / np.sqrt(rows) * DH ** -0.5
    put("rowscale", scale.reshape(C, P, H).transpose(1, 0, 2))
    block = np.zeros((P, KT, HT, DH + 1))
    decay = np.zeros((P, KT))
    for k in range(KT):
        for p in range(P):
            g = gamma[k * HT + p // DH] ** P
            block[p, k, p // DH, :] = g
            decay[p, k] = g
    put("stateblock", block)
    put("statedecay", decay)
    put("iota", np.tile(np.arange(E), (P, 1)))
    put("tileno", np.tile(np.arange(TILES), (P, 1)))
    put("half", np.full((P, 1), -0.5))
    return out

def vector_columns():
    widths = [("retn_w", KT), ("final_w", KT), ("fc1_b", FM), ("su_ug", KT), ("scale_up", FM),
              ("scale_gate", FM), ("su_dp", FM), ("gamma", KT), ("beta", KT), ("fc2_b", D), ("scale_dp", D)]
    at, out = 0, {}
    for name, w in widths:
        out[name] = (at, w)
        at += w
    return out, at


def psum_plan():
    order = []

    def job(bank, *name):
        order.append((name, bank))

    def project(c):
        job(0, "qk", c)
        job(1, "vg", c)

    job(6, "xt", 0)
    project(0)
    job(6, "xt", 1)
    job(2, "qkt", 0)
    for c in range(C):
        if c + 1 < C:
            project(c + 1)
        if c + 2 < C:
            job(6, "xt", c + 2)
        for n in range(4):
            job(3 + n % 2, "p", c, n)
        if c:
            job(7, "ot", c - 1)
        if c + 1 < C:
            job(2, "qkt", c + 1)
        if c:
            job(7, "y", c - 1)
        job(5, "o", c)
        job(6, "st", c)
    for n in range(4):
        job(n, "wd", n)
    job(7, "ot", C - 1)
    for m in range(KT):
        job(3 + m, "m", m)
    for m in range(KT):
        job(5 + m, "vo", m)
    job(7, "y", C - 1)
    for g in range(G):
        for c in range(GC * g, GC * g + GC):
            job(c % 2, "bt", c)
        for m in range(FM):
            job(2 + m % 2, "fc1", g, m)
    for c in range(C):
        job(4 + c % 2, "fc2", c)
    for g in range(G):
        for c in range(GC * g, GC * g + GC):
            job(c % 2, "ct", c)
        for m in range(KT):
            job(6 + m, "had", g, m)
        for m in range(FM):
            job(2 + m % 2, "gate", g, m)
            job(4 + m % 2, "up", g, m)
    for c in range(C):
        job(6 + c % 2, "down", c)
    for g in range(G):
        for c in range(GC * g, GC * g + GC):
            job(c % 2, "dt", c)
        for m in range(KT):
            job(2 + m, "qm", g, m)
        for c in range(GC * g, GC * g + GC):
            job(4 + c % 2, "v", c)

    def scores(c):
        for b in range(c // GC + 1):
            job(2 * (c % 2) + b, "sc", c, b)

    scores(0)
    for c in range(C):
        if c + 1 < C:
            scores(c + 1)
        for b in range(c // GC + 1):
            job(4 + b, "pt", c, b)
        if c:
            job(7, "zt", c - 1)
        job(6, "pv", c)
        if c:
            job(7, "lg", c - 1)
    job(7, "zt", C - 1)
    job(7, "lg", C - 1)
    job(0, "rank")
    fills, plan = [0] * 8, {}
    for name, bank in order:
        fills[bank] += 1
        plan[name] = (bank, fills[bank])
    return plan, fills

def build(nc, x_in, const_in, vec_in, qkvg_in, out_w_in, fc1_in, fc2_in, upgate_in, down_in, wqt_in, wkt_in,
          wvt_in, o_in, router_in, experts_in, out, upto=9):
    ccol, cn = constant_columns()
    vcol, vn = vector_columns()
    plan, fills = psum_plan()

    with ExitStack() as ctx:
        def sb(name, *shape, dt=F32):
            return ctx.enter_context(nc.sbuf_tensor(name, [P, *shape], dt))

        def sem(name):
            return ctx.enter_context(nc.semaphore(name))

        cst = sb("cst", cn)
        vec = sb("vec", vn)

        def const(name, *dims):
            at, w = ccol[name]
            return cst[:, at:at + w]

        def vector(name):
            at, w = vcol[name]
            return vec[:, at:at + w]

        ident, tril, below = const("ident"), const("tril"), const("below")
        had, hadneg, strict, ones = const("had"), const("hadneg"), const("strict"), const("ones")
        headmask = const("headmask")
        cos = const("cos").rearrange("p (c d) -> p c d", c=C)
        sin = const("sin").rearrange("p (c d) -> p c d", c=C)
        growth = const("growth")
        rowscale = const("rowscale").rearrange("p (c h) -> p c h", c=C)
        stateblock, statedecay = const("stateblock"), const("statedecay")

        x = sb("x", C, D)
        y = sb("y", C, D)
        xn = sb("xn", C, D)
        featT = sb("featT", KT, T)
        raw = sb("raw", C, 2)
        bn = sb("bn", 2, 6)
        ssq = sb("ssq", C)
        rstd = sb("rstd", C)
        rs2 = sb("rs2", C)
        tmp1 = sb("tmp1", C)
        tmp2 = sb("tmp2", C)

        experts = sb("experts", E * EW)
        region = [experts[:, 0:E // 2 * EW], experts[:, E // 2 * EW:]]
        used = [0, 0]

        def carve(r, *shape):
            n = int(np.prod(shape))
            ap = region[r][:, used[r]:used[r] + n]
            used[r] += n
            assert used[r] <= E // 2 * EW
            if len(shape) == 2:
                ap = ap.rearrange("p (a b) -> p a b", a=shape[0])
            elif len(shape) == 3:
                ap = ap.rearrange("p (a b c) -> p a b c", a=shape[0], b=shape[1])
            return ap

        w_qkvg = carve(0, KT, 4 * D)
        w_out = carve(0, KT, D)
        hT = carve(0, 2, KT, P)
        rotc = carve(0, 2 * D)
        rots = carve(0, 2 * D)
        qk = carve(0, 2, 2 * D)
        qkT = carve(0, 2, 4, P)
        qx = carve(0, KT, HT * P)
        pT = carve(0, H, P)
        va = carve(0, 2, H * (DH + 1))
        sg = carve(0, 2, D)
        state = carve(0, KT, HT * (DH + 1))
        statetmp = carve(0, KT, HT * (DH + 1))
        den = carve(0, H)
        rden = carve(0, H)
        wrow = carve(0, H)
        o1 = carve(0, D)
        osq = carve(0, D)
        oss = carve(0, H)
        ors = carve(0, H)
        o2 = carve(0, D)
        o3 = carve(0, 2, D)
        oT = carve(0, KT, P)
        sqj = carve(0, D)
        x1i = y
        halfs = sb("halfs", H)

        hidT = carve(1, FM, T)
        w_ug = carve(1, KT, 2 * F)
        uT = carve(1, KT, T)
        w_down = carve(1, FM, D)
        wdA = hidT[:, 0:2, :].rearrange("p a (b n) -> p (a b) n", n=D)
        wdB = hidT[:, 2:4, :].rearrange("p a (b n) -> p (a b) n", n=D)

        ffw = sb("ffw", 2 * KT * F)
        w_fc1 = ffw[:, 0:KT * F].rearrange("p (k n) -> p k n", k=KT)
        w_fc2 = ffw[:, KT * F:].rearrange("p (m n) -> p m n", m=FM)
        qT = ffw[:, 0:KT * T].rearrange("p (k n) -> p k n", k=KT)
        v = ffw[:, KT * T:].rearrange("p (c n) -> p c n", c=C)
        attn = sb("attn", 3 * T)
        prob = attn[:, 0:2 * T].rearrange("p (b n) -> p b n", b=2)
        probT = attn[:, 2 * T:].rearrange("p (j n) -> p j n", j=C)
        w_at = attn[:, 0:3 * KT * D].rearrange("p (a k n) -> p a k n", a=3, k=KT)
        silu_g = sb("silu_g", 2, GW)
        w_o = carve(0, KT, D)
        w_m = sb("w_m", KT, D)
        w_vo = sb("w_vo", KT, D)
        w_r = sb("w_r", KT, E)
        scpar = sb("scpar", FM)
        scup = sb("scup", FM)
        rmax = sb("rmax", 2)
        rsum = sb("rsum", C, 2)
        rmaxp = sb("rmaxp", 2)
        rinv = sb("rinv", C)
        flat_y = y[:].rearrange("p c d -> p (c d)")
        zT = flat_y[:, 0:D].rearrange("p (k n) -> p k n", k=KT)
        oh = flat_y[:, D:D + 3 * C * E].rearrange("p (a n) -> p a n", a=3)
        tot, pick = (flat_y[:, at:at + 2 * C * E].rearrange("p (a n) -> p a n", a=2) for at in (3 * D, 4 * D))
        within, posn = flat_y[:, 5 * D:5 * D + C * E], flat_y[:, 5 * D + C * E:6 * D]
        lgs = sb("lgs", C, E)
        top = sb("top", C, 8)
        topi = sb("topi", C, 8, dt=U32)
        topf = sb("topf", C, 2)
        dv8 = sb("dv8", C)
        ex8 = sb("ex8", C)
        p1 = sb("p1", C)
        p2 = sb("p2", C)
        ends = sb("ends", 2, E)
        ntile = sb("ntile", E)
        ntile_i = sb("ntile_i", E, dt=I32)
        base = sb("base", E)
        slotf = sb("slotf", 2, C)
        slots = sb("slots", 2, C, dt=U32)
        texp = sb("texp", TILES)
        texp_i = sb("texp_i", TILES, dt=I32)
        def two(ap):
            return ap.rearrange("p (b n) -> p b n", b=2)

        mh = two(attn[:, 0:2 * FE])
        mhT = two(attn[:, 2 * FE:4 * FE])
        mx = two(attn[:, 4 * FE:4 * FE + 2 * D])
        my = two(attn[:, 4 * FE + 2 * D:4 * FE + 4 * D])
        mxT = two(silu_g[:, 0, :])
        tcmp = silu_g[:, 1, 0:TILES * E]
        zeros = silu_g[:, 0, 0:D]

        psum = ctx.enter_context(nc.psum_tensor("psum", [P, 8, 512], F32))

        zpad = nc.dram_tensor("sorted_tokens", [TILES * P, D], F32, kind="Internal").ap()
        yout = nc.dram_tensor("sorted_outputs", [TILES * P, D], F32, kind="Internal").ap()

        full = [sem(f"psum_full{b}") for b in range(8)]
        drained = [sem(f"psum_drained{b}") for b in range(8)]
        s_cst, s_x, s_qkvg, s_outw, s_vec = sem("const_loaded"), sem("x_loaded"), sem("qkvg_loaded"), sem("outw_loaded"), sem("vec_loaded")
        s_fc, s_down, s_ug, s_at, s_o = sem("fc_loaded"), sem("down_loaded"), sem("upgate_loaded"), sem("attw_loaded"), sem("o_loaded")
        s_exp = [sem("experts_lo_loaded"), sem("experts_hi_loaded")]
        s_zero = sem("pad_zeroed")
        s_dv = sem("vector_steps")
        s_pl = sem("pool_steps")
        s_ac = sem("scalar_steps")
        s_init = sem("buffers_set")
        s_par = sem("ffn_scales_ready")
        s_stat = sem("stats_ready")
        s_xn = [sem(f"normalised{ph}") for ph in range(5)]
        s_y = sem("layernorm_ready")
        s_xr = [sem("ffn_residual"), sem("attn_residual")]
        s_oss = sem("head_squares")
        s_qk = sem("rotated")
        s_va = sem("values_ready")
        s_qx = sem("queries_spread")
        s_state = sem("state_ready")
        s_ors = sem("head_rms_ready")
        s_o3 = sem("gated_ready")
        s_bfly = sem("butterflies")
        s_mx = sem("rowmax_ready")
        s_gap = sem("logit_gap_ready")
        s_e8 = sem("gap_exp_ready")
        s_oh = sem("onehot_ready")
        s_slot = sem("slots_ready")
        s_te = sem("tile_experts_ready")
        s_scat = sem("tokens_scattered")
        s_ld = [sem("tile_loaded0"), sem("tile_loaded1")]
        s_st = [sem("tile_stored0"), sem("tile_stored1")]
        s_txf, s_txd = sem("tile_xT_full"), sem("tile_xT_drained")
        s_hf, s_hd = sem("tile_h_full"), sem("tile_h_drained")
        s_thf, s_thd = sem("tile_hT_full"), sem("tile_hT_drained")
        s_yf, s_yd = sem("tile_y_full"), sem("tile_y_drained")
        s_gat = [sem(f"gathered{c}") for c in range(C)]
        s_res = sem("result_ready")
        s_out = sem("result_stored")

        def bank(job):
            b, _ = plan[job]
            return psum[:, b, :]

        def filled(eng, job):
            b, n = plan[job]
            eng.wait_ge(full[b], n)
            return psum[:, b, :]

        def emptied(eng, job):
            b, n = plan[job]
            eng.wait_ge(drained[b], n)

        gate = E // 2 * EW
        nphase = upto

        block = ctx.enter_context(nc.Block())

        @block.sync
        def _(sp):
            for n in range(4):
                sp.dma_start(x[:, 2 * n:2 * n + 2, :],
                             x_in.rearrange("(c p) d -> p c d", p=P)[:, 2 * n:2 * n + 2, :]).then_inc(s_x, 16)
                sp.wait_ge(s_x, 16 * (n + 1))
                if n == 0:
                    sp.dma_start(cst[:], const_in).then_inc(s_cst, 16)
                    sp.dma_start(w_qkvg, qkvg_in).then_inc(s_qkvg, 16)
            sp.dma_start(w_out, out_w_in).then_inc(s_outw, 16)
            sp.dma_start(wdA, down_in).then_inc(s_down, 16)
            sp.dma_start(w_at[:, 0], wqt_in).then_inc(s_at, 16)
            sp.dma_start(w_at[:, 1], wkt_in).then_inc(s_at, 16)
            sp.dma_start(w_at[:, 2], wvt_in).then_inc(s_at, 16)
            sp.dma_start(w_o, o_in).then_inc(s_at, 16)
            sp.dma_start(w_fc1, fc1_in).then_inc(s_fc, 16)
            sp.dma_start(w_fc2, fc2_in).then_inc(s_fc, 16)
            sp.dma_start(w_ug, upgate_in).then_inc(s_ug, 16)
            sp.dma_start(w_r[:], router_in).then_inc(s_o, 16)
            if nphase >= 5:
                sp.wait_ge(full[plan[("y", C - 1)][0]], plan[("y", C - 1)][1])
                sp.wait_ge(s_xn[1], C)
                for e in range(E // 2):
                    sp.dma_start(region[0][:, e * EW:(e + 1) * EW], experts_in[e]).then_inc(s_exp[0], 16)
                sp.wait_ge(full[plan[("down", C - 1)][0]], plan[("down", C - 1)][1])
                for e in range(E // 2):
                    sp.dma_start(region[1][:, e * EW:(e + 1) * EW], experts_in[E // 2 + e]).then_inc(s_exp[1], 16)
                sp.wait_ge(s_scat, 32 * C)

                def load(t, par):
                    sp.dma_start(mx[:, par, :], zpad[bass.ds(t * P, P), :]).then_inc(s_ld[par], 16)

                def store(t, par):
                    sp.wait_ge(s_yd, t + 1)
                    sp.dma_start(yout[bass.ds(t * P, P), :], my[:, par, :]).then_inc(s_st[par], 16)

                load(0, 0)
                load(1, 1)

                def step(t, par):
                    sp.wait_ge(s_txf, t + 1)
                    load(t + 2, par)
                    store(t, par)

                step(0, 0)
                step(1, 1)
                with sp.Fori(2, TILES - 3, 2) as t:
                    step(t, 0)
                    step(t + 1, 1)
                step(TILES - 3, 0)
                store(TILES - 2, 1)
                store(TILES - 1, 0)
                for c in range(C):
                    sp.wait_ge(s_res, c + 1)
                    sp.dma_start(out.rearrange("(c p) d -> p c d", p=P)[:, c, :], x[:, c, :]).then_inc(s_out, 16)
                sp.wait_ge(s_out, 16 * C)
            else:
                src = {1: y, 2: x, 3: xn, 4: x}[nphase]
                sp.wait_ge(s_xn[nphase], C)
                sp.dma_start(out.rearrange("(c p) d -> p c d", p=P), src[:]).then_inc(s_out, 16)
                sp.wait_ge(s_out, 16)

        @block.gpsimd
        def _(pool):
            steps = [0]

            def link(ins):
                steps[0] += 1
                ins.then_inc(s_pl, 1)
                pool.wait_ge(s_pl, steps[0])

            def power(dst, src):
                return pool.tensor_tensor(dst, src, halfs[:, 0:dst.shape[1]], ALU.pow)

            def norm(ph, c, double, residual):
                col = slice(c, c + 1)
                pool.wait_ge(s_stat, ph * C + c + 1)
                link(pool.tensor_scalar(tmp1[:, col], raw[:, c, 1:2], EPS, None, ALU.add))
                link(power(rstd[:, col], tmp1[:, col]))
                s = rstd
                if double:
                    link(pool.tensor_scalar(tmp1[:, col], raw[:, c, 1:2], rstd[:, col], rstd[:, col],
                                            ALU.mult, ALU.mult))
                    link(pool.tensor_scalar(tmp1[:, col], tmp1[:, col], EPS, None, ALU.add))
                    link(power(tmp2[:, col], tmp1[:, col]))
                    link(pool.tensor_tensor(rs2[:, col], rstd[:, col], tmp2[:, col], ALU.mult))
                    s = rs2
                pool.tensor_scalar(xn[:, c, :], x[:, c, :], raw[:, c, 0:1], s[:, col],
                                   ALU.subtract, ALU.mult).then_inc(s_xn[(0, 2, 3, 4)[ph]], 1)
                if double:
                    ins = pool.tensor_scalar(y[:, c, :], x[:, c, :], raw[:, c, 0:1], rstd[:, col],
                                             ALU.subtract, ALU.mult)
                    if residual:
                        link(ins)
                        pool.tensor_tensor(x[:, c, :], x[:, c, :], y[:, c, :], ALU.add).then_inc(s_xr[1], 1)
                    else:
                        ins.then_inc(s_y, 1)

            def head_rms(c):
                pool.wait_ge(s_oss, c + 1)
                link(pool.tensor_scalar(oss, oss, 1.0 / DH, EPS, ALU.mult, ALU.add))
                pool.tensor_tensor(ors, oss, halfs[:], ALU.pow).then_inc(s_ors, 1)

            def ffn_norm(c):
                col = slice(c, c + 1)
                pool.wait_ge(s_ac, c + 1)
                link(pool.tensor_scalar(tmp1[:, col], ssq[:, col], 1.0 / D, EPS, ALU.mult, ALU.add))
                link(power(rs2[:, col], tmp1[:, col]))
                pool.tensor_scalar(xn[:, c, :], x1i[:, c, :], rs2[:, col], None, ALU.mult).then_inc(s_xn[1], 1)
                link(pool.tensor_tensor(x[:, c, :], x[:, c, :], x1i[:, c, :], ALU.add))
                pool.tensor_tensor(x[:, c, :], x[:, c, :], vector("fc2_b"), ALU.add).then_inc(s_xr[0], 1)

            def butterfly(stage, half):
                src, dst = ((wdA, wdB), (wdB, wdA), (wdA, wdB))[stage]
                a = src.rearrange("p (o t i) n -> p o t (i n)", t=2, i=1 << stage)
                b = dst.rearrange("p (o t i) n -> p o t (i n)", t=2, i=1 << stage)
                return pool.tensor_tensor(b[:, :, half], a[:, :, 0], a[:, :, 1], (ALU.add, ALU.subtract)[half])

            link(pool.memset(halfs[:], -0.5))
            link(pool.memset(state, 0.0))
            pool.memset(zeros, 0.0).then_inc(s_init, 1)
            pool.wait_ge(s_cst, 16)
            for n in range(2):
                va_n = va[:, n].rearrange("p (h e) -> p h e", e=DH + 1)
                pool.tensor_copy(va_n[:, :, DH], growth).then_inc(s_init, 1)
            pool.wait_ge(s_init, 3)
            if nphase >= 5:
                for n in range(TILES):
                    pool.dma_start(zpad[n * P:(n + 1) * P, :], zeros).then_inc(s_zero, 16)
            norm(0, 0, True, False)
            norm(0, 1, True, False)
            pool.wait_ge(s_vec, 16)
            for c in range(C):
                emptied(pool, ("qk", c))
                if c >= 2:
                    filled(pool, ("st", c - 2))
                pool.tensor_tensor(qk[:, c % 2, :], rotc, rots, ALU.add).then_inc(s_qk, 1)
                if c + 2 < C:
                    norm(0, c + 2, True, False)
                if c >= 2:
                    ffn_norm(c - 2)
                if c >= 1:
                    head_rms(c - 1)
                if 1 <= c < 7:
                    if c == 1:
                        pool.wait_ge(s_down, 16)
                    ins = butterfly((c - 1) // 2, (c - 1) % 2)
                    if c == 6:
                        ins.then_inc(s_bfly, 1)
                    else:
                        link(ins)
            head_rms(C - 1)
            ffn_norm(C - 2)
            ffn_norm(C - 1)
            if nphase >= 5:
                pool.wait_ge(s_zero, 16 * TILES)
            for c in range(C):
                norm(1, c, False, False)
            if nphase >= 3:
                for c in range(C):
                    norm(2, c, True, True)
            if nphase >= 4:
                for c in range(C):
                    norm(3, c, False, False)
            if nphase >= 5:
                pool.wait_ge(s_slot, 1)
                pool.wait_ge(s_zero, 16 * TILES)
                for c in range(C):
                    for k in range(2):
                        pool.indirect_dma_start(
                            out=zpad, out_offset=bass.IndirectOffsetOnAxis(ap=slots[:, k, c:c + 1], axis=0),
                            in_=xn[:, c, :], in_offset=None).then_inc(s_scat, 16)
                for par in range(2):
                    pool.wait_ge(s_st[par], 16 * len(range(par, TILES, 2)))
                for c in range(C):
                    for k, dst in enumerate((xn, y)):
                        pool.indirect_dma_start(
                            out=dst[:, c, :], out_offset=None, in_=yout,
                            in_offset=bass.IndirectOffsetOnAxis(ap=slots[:, k, c:c + 1], axis=0)).then_inc(s_gat[c], 16)

        @block.scalar
        def _(act):
            act.dma_start(vec[:], vec_in).then_inc(s_vec, 16)
            act.wait_ge(s_vec, 16)

            def drain(job, dst, scale=1.0, func=ACT.Copy, src=None):
                b, _ = plan[job]
                p_ = filled(act, job)
                act.activation(dst, src(p_) if src else p_[:, 0:dst.free_size()], func, scale=scale).then_inc(drained[b], 1)

            def drain2(job, dst, name, bias=None):
                b, _ = plan[job]
                p_ = filled(act, job)
                for k in range(KT):
                    kw = {"bias": vector(bias)[:, k:k + 1]} if bias else {}
                    ins = act.activation(dst[:, k, :], p_[:, k * P:(k + 1) * P], ACT.Identity,
                                         scale=vector(name)[:, k:k + 1], **kw)
                ins.then_inc(drained[b], 1)

            def xt(c):
                drain2(("xt", c), hT[:, c % 2], "retn_w")

            def gate_g(c):
                act.wait_ge(s_va, c + 1)
                if c >= 2:
                    act.wait_ge(s_o3, c - 1)
                b, _ = plan[("vg", c)]
                act.activation(sg[:, c % 2, :], bank(("vg", c))[:, D:2 * D], ACT.Silu).then_inc(drained[b], 1)

            def ot(c):
                drain(("ot", c), oT.rearrange("p k n -> p (k n)"))

            def square(c):
                emptied(act, ("y", c))
                act.activation(sqj, x1i[:, c, :], ACT.Square, accum_out=ssq[:, c:c + 1]).then_inc(s_ac, 1)

            def qkt(c):
                drain(("qkt", c), qkT[:, c % 2].rearrange("p a n -> p (a n)"))

            xt(0)
            xt(1)
            gate_g(0)
            qkt(0)
            for c in range(C):
                if c + 2 < C:
                    xt(c + 2)
                if c + 1 < C:
                    gate_g(c + 1)
                if c:
                    ot(c - 1)
                if c + 1 < C:
                    qkt(c + 1)
                if c:
                    square(c - 1)
            ot(C - 1)
            for m in range(KT):
                drain(("m", m), w_m[:, m, :], scale=float(D) ** -0.5)
            for m in range(KT):
                drain(("vo", m), w_vo[:, m, :])
            square(C - 1)
            for g in range(G):
                for c in range(GC * g, GC * g + GC):
                    drain2(("bt", c), featT[:, :, c * P:(c + 1) * P], "final_w")
                for m in range(FM):
                    b, _ = plan[("fc1", g, m)]
                    act.activation(hidT[:, m, g * GW:(g + 1) * GW], filled(act, ("fc1", g, m)),
                                   ACT.Gelu_apprx_tanh, bias=vector("fc1_b")[:, m:m + 1]).then_inc(drained[b], 1)
            if nphase < 3:
                return
            for g in range(G):
                for c in range(GC * g, GC * g + GC):
                    drain2(("ct", c), featT[:, :, c * P:(c + 1) * P], "su_ug")
                for m in range(KT):
                    drain(("had", g, m), uT[:, m, g * GW:(g + 1) * GW])
                act.wait_ge(s_par, 2)
                for m in range(FM):
                    n = g * FM + m
                    if n >= 2:
                        emptied(act, ("up", (n - 2) // FM, (n - 2) % FM))
                    b, _ = plan[("gate", g, m)]
                    act.activation(silu_g[:, n % 2, :], filled(act, ("gate", g, m)), ACT.Silu,
                                   scale=scpar[:, m:m + 1]).then_inc(drained[b], 1)
            if nphase < 4:
                return
            for g in range(G):
                for c in range(GC * g, GC * g + GC):
                    drain2(("dt", c), featT[:, :, c * P:(c + 1) * P], "gamma", "beta")
                for m in range(KT):
                    drain(("qm", g, m), qT[:, m, g * GW:(g + 1) * GW])
                for c in range(GC * g, GC * g + GC):
                    drain(("v", c), v[:, c, :])
            if nphase < 4:
                return

            def exps(c):
                act.wait_ge(s_mx, c + 1)
                if c >= 2:
                    for b_ in range((c - 2) // GC + 1):
                        filled(act, ("pt", c - 2, b_))
                for b_ in range(c // GC + 1):
                    n = min(GW, (c + 1) * P - b_ * GW)
                    act.activation(prob[:, c % 2, b_ * GW:b_ * GW + n], bank(("sc", c, b_))[:, 0:n], ACT.Exp,
                                   bias=rmax[:, c % 2:c % 2 + 1], accum_out=rsum[:, c, b_:b_ + 1]
                                   ).then_inc(drained[plan[("sc", c, b_)][0]], 1)

            def zt(c):
                if c == 0:
                    act.wait_ge(s_xr[1], C)
                drain(("zt", c), zT.rearrange("p k n -> p (k n)"))

            exps(0)
            for c in range(C):
                if c + 1 < C:
                    exps(c + 1)
                if c:
                    zt(c - 1)
            zt(C - 1)
            act.wait_ge(s_gap, 1)
            act.activation(ex8[:], dv8[:], ACT.Exp).then_inc(s_e8, 1)
            if nphase < 5:
                return

            def tile_xT(t, par):
                act.wait_ge(s_txf, t + 1)
                act.activation(mxT[:, par, :], psum[:, par, 0:KT * P], ACT.Copy).then_inc(s_txd, 1)

            def tile_silu(t, par):
                act.wait_ge(s_hf, t + 1)
                act.activation(mh[:, par, :], psum[:, 2 + par, :], ACT.Silu).then_inc(s_hd, 1)

            def step(t, par):
                tile_silu(t + 1, 1 - par)
                tile_xT(t + 2, par)

            tile_xT(0, 0)
            tile_silu(0, 0)
            tile_xT(1, 1)
            step(0, 0)
            step(1, 1)
            with act.Fori(2, TILES - 3, 2) as t:
                step(t, 0)
                step(t + 1, 1)
            step(TILES - 3, 0)
            tile_silu(TILES - 1, 0)

        @block.tensor
        def _(pe):
            def fill(job):
                b, n = plan[job]
                if n > 1:
                    pe.wait_ge(drained[b], n - 1)
                return psum[:, b, :]

            def done(ins, job):
                ins.then_inc(full[plan[job][0]], 1)

            def turn(job, src):
                d = fill(job)
                for k in range(src.shape[1] // P):
                    ins = pe.transpose(d[:, k * P:(k + 1) * P], src[:, k * P:(k + 1) * P], ident)
                done(ins, job)

            def product(job, pairs, n):
                d = fill(job)
                for i, (w, m) in enumerate(pairs):
                    ins = pe.matmul(d[:, 0:n], w, m, start=(i == 0), stop=(i == len(pairs) - 1))
                done(ins, job)

            def xt(c):
                pe.wait_ge(s_xn[0], c + 1)
                turn(("xt", c), xn[:, c, :])

            def project(c):
                emptied(pe, ("xt", c))
                for half, name in enumerate(("qk", "vg")):
                    product((name, c), [(hT[:, c % 2, k, :], w_qkvg[:, k, half * 2 * D:(half + 1) * 2 * D])
                                        for k in range(KT)], 2 * D)

            def qkt(c):
                pe.wait_ge(s_qk, c + 1)
                turn(("qkt", c), qk[:, c % 2, :])

            def scores(c):
                pe.wait_ge(s_qx, c + 1)
                for n in range(4):
                    k, h = n // 2, (n % 2) * 4
                    product(("p", c, n), [(qkT[:, c % 2, 2 + k, :], qx[:, k, h * P:(h + 4) * P])], 4 * P)

            def retain(c):
                w = DH + 1
                d = fill(("o", c))
                emptied(pe, ("qkt", c))
                if c:
                    pe.wait_ge(s_state, c)
                else:
                    pe.wait_ge(s_init, 3)
                for k in range(KT):
                    pe.matmul(d[:, k * HT * w:(k + 1) * HT * w], qkT[:, c % 2, k, :], state[:, k, :],
                              start=(k == 0), stop=False, skip_group_check=True)
                for h in range(H):
                    if h % 4 == 0:
                        emptied(pe, ("p", c, h // 4))
                    if h == 0:
                        pe.wait_ge(s_va, c + 1)
                    ins = pe.matmul(d[:, h * w:(h + 1) * w], pT[:, h, :], va[:, c % 2, h * w:(h + 1) * w],
                                    start=False, stop=(h == H - 1), skip_group_check=True)
                done(ins, ("o", c))
                d = fill(("st", c))
                for k in range(KT):
                    ins = pe.matmul(d[:, k * HT * w:(k + 1) * HT * w], qk[:, c % 2, D + k * P:D + (k + 1) * P],
                                    va[:, c % 2, k * HT * w:(k + 1) * HT * w], start=True, stop=True)
                done(ins, ("st", c))

            def ot(c):
                pe.wait_ge(s_o3, c + 1)
                turn(("ot", c), o3[:, c % 2, :])

            def yproj(c):
                emptied(pe, ("ot", c))
                product(("y", c), [(oT[:, k, :], w_out[:, k, :]) for k in range(KT)], D)

            pe.wait_ge(s_cst, 16)
            xt(0)
            pe.wait_ge(s_qkvg, 16)
            project(0)
            xt(1)
            qkt(0)
            for c in range(C):
                if c + 1 < C:
                    project(c + 1)
                if c + 2 < C:
                    xt(c + 2)
                scores(c)
                if c:
                    ot(c - 1)
                if c + 1 < C:
                    qkt(c + 1)
                if c:
                    if c == 1:
                        pe.wait_ge(s_outw, 16)
                    yproj(c - 1)
                retain(c)
            pe.wait_ge(s_bfly, 1)
            for n in range(4):
                product(("wd", n), [(had, wdB[:, 2 * n:2 * n + 2, :].rearrange("p a n -> p (a n)"))], 512)
            ot(C - 1)
            pe.wait_ge(s_at, 64)
            for m in range(KT):
                product(("m", m), [(w_at[:, 0, k, m * P:(m + 1) * P], w_at[:, 1, k, :]) for k in range(KT)], D)
            for m in range(KT):
                product(("vo", m), [(w_at[:, 2, k, m * P:(m + 1) * P], w_o[:, k, :]) for k in range(KT)], D)
            yproj(C - 1)

            pe.wait_ge(s_fc, 32)
            for g in range(G):
                for c in range(GC * g, GC * g + GC):
                    pe.wait_ge(s_xn[1], c + 1)
                    turn(("bt", c), xn[:, c, :])
                for m in range(FM):
                    if m == 0:
                        for c in (GC * g + GC - 2, GC * g + GC - 1):
                            emptied(pe, ("bt", c))
                    product(("fc1", g, m), [(w_fc1[:, k, m * P:(m + 1) * P], featT[:, k, g * GW:(g + 1) * GW])
                                            for k in range(KT)], GW)
            for c in range(C):
                for m in (FM - 2, FM - 1):
                    emptied(pe, ("fc1", c // GC, m))
                product(("fc2", c), [(hidT[:, m, c * P:(c + 1) * P], w_fc2[:, m, :]) for m in range(FM)], D)
            if nphase < 3:
                return
            pe.wait_ge(s_ug, 16)
            for g in range(G):
                for c in range(GC * g, GC * g + GC):
                    pe.wait_ge(s_xn[2], c + 1)
                    turn(("ct", c), xn[:, c, :])
                for c in (GC * g + GC - 2, GC * g + GC - 1):
                    emptied(pe, ("ct", c))
                cols = slice(g * GW, (g + 1) * GW)
                for m in range(KT):
                    product(("had", g, m), [(had, featT[:, 0, cols]), (had if m == 0 else hadneg, featT[:, 1, cols])], GW)
                for m in range(KT):
                    emptied(pe, ("had", g, m))
                for m in range(FM):
                    for name, at in (("gate", F), ("up", 0)):
                        product((name, g, m), [(w_ug[:, k, at + m * P:at + (m + 1) * P], uT[:, k, cols])
                                               for k in range(KT)], GW)
            for c in range(C):
                for m in (FM - 2, FM - 1):
                    emptied(pe, ("up", c // GC, m))
                if c == 0:
                    for n in range(4):
                        emptied(pe, ("wd", n))
                product(("down", c), [(hidT[:, m, c * P:(c + 1) * P], w_down[:, m, :]) for m in range(FM)], D)
            if nphase < 4:
                return
            for g in range(G):
                for c in range(GC * g, GC * g + GC):
                    pe.wait_ge(s_xn[3], c + 1)
                    turn(("dt", c), xn[:, c, :])
                for c in (GC * g + GC - 2, GC * g + GC - 1):
                    emptied(pe, ("dt", c))
                for m in range(KT):
                    product(("qm", g, m), [(w_m[:, k, m * P:(m + 1) * P], featT[:, k, g * GW:(g + 1) * GW])
                                           for k in range(KT)], GW)
                for c in range(GC * g, GC * g + GC):
                    product(("v", c), [(featT[:, k, c * P:(c + 1) * P], w_vo[:, k, :]) for k in range(KT)], D)

            def att_scores(c):
                if c % GC == 0:
                    for m in range(KT):
                        emptied(pe, ("qm", c // GC, m))
                for b in range(c // GC + 1):
                    n = min(GW, (c + 1) * P - b * GW)
                    product(("sc", c, b), [(qT[:, k, c * P:(c + 1) * P], featT[:, k, b * GW:b * GW + n])
                                           for k in range(KT)], n)

            def prob_turn(c):
                for b in range(c // GC + 1):
                    emptied(pe, ("sc", c, b))
                    n = min(GW, (c + 1) * P - b * GW)
                    turn(("pt", c, b), prob[:, c % 2, b * GW:b * GW + n])

            def att_out(c):
                for b in range(c // GC + 1):
                    emptied(pe, ("pt", c, b))
                if c % GC == 0:
                    for cc in range(c, c + GC):
                        emptied(pe, ("v", cc))
                product(("pv", c), [(probT[:, j, :], v[:, j, :]) for j in range(c + 1)], D)

            def zt(c):
                pe.wait_ge(s_xn[4], c + 1)
                turn(("zt", c), xn[:, c, :])

            def logits(c):
                emptied(pe, ("zt", c))
                product(("lg", c), [(zT[:, k, :], w_r[:, k, :]) for k in range(KT)], E)

            att_scores(0)
            for c in range(C):
                if c + 1 < C:
                    att_scores(c + 1)
                prob_turn(c)
                if c:
                    zt(c - 1)
                att_out(c)
                if c:
                    if c == 1:
                        pe.wait_ge(s_o, 16)
                    logits(c - 1)
            zt(C - 1)
            logits(C - 1)
            if nphase < 5:
                return
            pe.wait_ge(s_oh, 1)
            d = fill(("rank",))
            pe.matmul(d[:, 0:C * E], strict, oh[:, 2, :], start=True, stop=True)
            done(pe.matmul(d[:, C * E:2 * C * E], ones, oh[:, 2, :], start=True, stop=True), ("rank",))

            for b in range(8):
                pe.wait_ge(drained[b], fills[b])
            pe.wait_ge(s_te, 1)
            for n in range(2):
                pe.wait_ge(s_exp[n], 16 * (E // 2))

            def expert(t):
                return pe.value_load(texp_i[0:1, bass.ds(t, 1)], min_val=0, max_val=(E - 1) * EW)

            def tile_turn(t, par, loads):
                pe.wait_ge(s_ld[par], loads)
                for k in range(KT):
                    ins = pe.transpose(psum[:, par, k * P:(k + 1) * P], mx[:, par, k * P:(k + 1) * P], ident)
                ins.then_inc(s_txf, 1)

            def tile_up(t, par, at):
                pe.wait_ge(s_txd, t + 1)
                for k in range(KT):
                    ins = pe.matmul(psum[:, 2 + par, :], mxT[:, par, k * P:(k + 1) * P],
                                    experts[:, bass.ds(at + k * FE, FE)], start=(k == 0), stop=(k == KT - 1))
                ins.then_inc(s_hf, 1)

            def tile_hT(t, par):
                pe.wait_ge(s_hd, t + 1)
                if not (isinstance(t, int) and t < 2):
                    pe.wait_ge(s_thd, t - 1)
                for m in range(FEM):
                    ins = pe.transpose(psum[:, 4 + par, m * P:(m + 1) * P], mh[:, par, m * P:(m + 1) * P], ident)
                ins.then_inc(s_thf, 1)

            def tile_down(t, par, at):
                pe.wait_ge(s_thd, t + 1)
                if not (isinstance(t, int) and t < 2):
                    pe.wait_ge(s_yd, t - 1)
                for m in range(FEM):
                    ins = pe.matmul(psum[:, 6 + par, 0:D], mhT[:, par, m * P:(m + 1) * P],
                                    experts[:, bass.ds(at + KT * FE + m * D, D)], start=(m == 0), stop=(m == FEM - 1))
                ins.then_inc(s_yf, 1)

            def step(t, par, loads):
                tile_hT(t, par)
                tile_up(t + 1, 1 - par, expert(t + 1))
                tile_down(t, par, expert(t))
                if loads is not None:
                    tile_turn(t + 2, par, loads)

            tile_turn(0, 0, 16)
            tile_up(0, 0, expert(0))
            tile_turn(1, 1, 16)
            step(0, 0, 32)
            step(1, 1, 32)
            with pe.Fori(2, TILES - 3, 2) as t:
                for u in range(2):
                    step(t + u, u, t * 8 + 32)
            step(TILES - 3, 0, 8 * (TILES - 3) + 32)
            step(TILES - 2, 1, None)
            tile_hT(TILES - 1, 0)
            tile_down(TILES - 1, 0, expert(TILES - 1))

        @block.vector
        def _(dve):
            steps = [0]

            def link(ins):
                steps[0] += 1
                ins.then_inc(s_dv, 1)
                dve.wait_ge(s_dv, steps[0])

            def wide(ap, n):
                return ap.unsqueeze(2).to_broadcast([P, ap.shape[1], n])

            def over(ap, n):
                return ap.unsqueeze(1).to_broadcast([P, n, ap.shape[1]])

            def stats(c):
                link(dve.bn_stats(bn[:, c % 2, :], x[:, c, :]))
                dve.bn_aggr(raw[:, c, :], bn[:, c % 2, :]).then_inc(s_stat, 1)

            def rotate(c):
                if c:
                    dve.wait_ge(s_qk, c)
                q = filled(dve, ("qk", c)).rearrange("p (h d) -> p h d", d=DH)
                dve.tensor_tensor(rotc.rearrange("p (h d) -> p h d", d=DH), q, over(cos[:, c, :], 2 * H), ALU.mult)
                q2 = q.rearrange("p h (i two) -> p h i two", two=2)
                r2 = rots.rearrange("p (h i two) -> p h i two", two=2, i=DH // 2)
                s2 = sin[:, c, :].rearrange("p (i two) -> p i two", two=2)
                for side in range(2):
                    ins = dve.tensor_tensor(r2[:, :, :, side], q2[:, :, :, 1 - side],
                                            over(s2[:, :, side], 2 * H), ALU.mult)
                ins.then_inc(drained[plan[("qk", c)][0]], 1)

            def values(c):
                if c >= 2:
                    filled(dve, ("st", c - 2))
                src = filled(dve, ("vg", c))[:, 0:D].rearrange("p (h d) -> p h d", d=DH)
                dst = va[:, c % 2, :].rearrange("p (h e) -> p h e", e=DH + 1)[:, :, 0:DH]
                dve.tensor_tensor(dst, src, wide(growth, DH), ALU.mult).then_inc(s_va, 1)

            def causal(c):
                if c:
                    filled(dve, ("o", c - 1))
                for n in range(4):
                    src = filled(dve, ("p", c, n)).rearrange("p (h s) -> p h s", s=P)
                    dve.tensor_tensor(pT[:, 4 * n:4 * n + 4, :], src, over(tril, 4), ALU.mult
                                      ).then_inc(drained[plan[("p", c, n)][0]], 1)

            def spread(c):
                emptied(dve, ("qkt", c))
                for k in range(KT):
                    ins = dve.tensor_tensor(qx[:, k, :].rearrange("p (h s) -> p h s", s=P),
                                            over(qkT[:, c % 2, k, :], HT), wide(headmask, P), ALU.mult)
                ins.then_inc(s_qx, 1)

            def inner_residual(c):
                dve.wait_ge(s_y, c + 1)
                dve.tensor_tensor(x1i[:, c, :], y[:, c, :], filled(dve, ("y", c))[:, 0:D], ALU.add
                                  ).then_inc(drained[plan[("y", c)][0]], 1)

            def update_state(c):
                n = KT * HT * (DH + 1)
                src = filled(dve, ("st", c))[:, 0:n]
                flat = statetmp.rearrange("p k n -> p (k n)")
                dve.tensor_tensor(flat, src, stateblock, ALU.mult).then_inc(drained[plan[("st", c)][0]], 1)
                emptied(dve, ("st", c))
                for k in range(KT):
                    ins = dve.scalar_tensor_tensor(state[:, k, :], state[:, k, :], statedecay[:, k:k + 1],
                                                   statetmp[:, k, :], ALU.mult, ALU.add)
                ins.then_inc(s_state, 1)

            def weigh(c):
                d = filled(dve, ("o", c))[:, 0:H * (DH + 1)].rearrange("p (h e) -> p h e", e=DH + 1)
                link(dve.tensor_tensor(den, d[:, :, DH], rowscale[:, c, :], ALU.mult))
                link(dve.scalar_tensor_tensor(den, den, -1.0, den, ALU.mult, ALU.max))
                link(dve.tensor_scalar(den, den, 1.0, None, ALU.max))
                link(dve.reciprocal(rden, den))
                link(dve.tensor_tensor(wrow, rden, rowscale[:, c, :], ALU.mult))
                dve.tensor_tensor(o1.rearrange("p (h d) -> p h d", d=DH), d[:, :, 0:DH], wide(wrow, DH), ALU.mult
                                  ).then_inc(drained[plan[("o", c)][0]], 1)
                emptied(dve, ("o", c))
                link(dve.tensor_tensor(osq, o1, o1, ALU.mult))
                if c:
                    dve.wait_ge(s_ors, c)
                dve.tensor_reduce(oss, osq.rearrange("p (h d) -> p h d", d=DH), AX.X, ALU.add).then_inc(s_oss, 1)

            def gated(c):
                dve.wait_ge(s_ors, c + 1)
                link(dve.tensor_tensor(o2.rearrange("p (h d) -> p h d", d=DH),
                                       o1.rearrange("p (h d) -> p h d", d=DH), wide(ors, DH), ALU.mult))
                emptied(dve, ("vg", c))
                dve.tensor_tensor(o3[:, c % 2, :], o2, sg[:, c % 2, :], ALU.mult).then_inc(s_o3, 1)

            for c in range(C):
                if c % 2 == 0:
                    dve.wait_ge(s_x, 16 * (c // 2 + 1))
                stats(c)
            dve.wait_ge(s_vec, 16)
            dve.wait_ge(s_cst, 16)
            dve.scalar_tensor_tensor(scup[:], vector("scale_up"), D ** -0.5, vector("su_dp"), ALU.mult, ALU.mult
                                     ).then_inc(s_par, 1)
            dve.tensor_scalar(scpar[:], vector("scale_gate"), D ** -0.5, None, ALU.mult).then_inc(s_par, 1)
            rotate(0)
            values(0)
            spread(0)
            for c in range(C):
                if c + 1 < C:
                    rotate(c + 1)
                    values(c + 1)
                causal(c)
                if c + 1 < C:
                    spread(c + 1)
                if c:
                    inner_residual(c - 1)
                weigh(c)
                update_state(c)
                gated(c)
            for n in range(4):
                src = filled(dve, ("wd", n)).rearrange("p (a n) -> p a n", n=D)
                dve.scalar_tensor_tensor(w_down[:, 2 * n:2 * n + 2, :], src, F ** -0.5, over(vector("scale_dp"), 2),
                                         ALU.mult, ALU.mult).then_inc(drained[plan[("wd", n)][0]], 1)
            inner_residual(C - 1)

            def add_residual(job, c):
                dve.tensor_tensor(x[:, c, :], x[:, c, :], filled(dve, job)[:, 0:D], ALU.add
                                  ).then_inc(drained[plan[job][0]], 1)
                emptied(dve, job)
                stats(c)

            for c in range(C):
                dve.wait_ge(s_xr[0], c + 1)
                add_residual(("fc2", c), c)
            if nphase < 3:
                return
            for g in range(G):
                for m in range(FM):
                    emptied(dve, ("gate", g, m))
                    dve.scalar_tensor_tensor(hidT[:, m, g * GW:(g + 1) * GW], filled(dve, ("up", g, m)),
                                             scup[:, m:m + 1], silu_g[:, m % 2, :], ALU.mult, ALU.mult
                                             ).then_inc(drained[plan[("up", g, m)][0]], 1)
            for c in range(C):
                add_residual(("down", c), c)
            if nphase < 4:
                return

            def row_max(c):
                for b in range(c // GC + 1):
                    filled(dve, ("sc", c, b))
                b0 = 2 * (c % 2)
                flat = psum[:, b0:b0 + 2, :].rearrange("p b n -> p (b n)")
                diag = flat[:, c * P:(c + 1) * P]
                link(dve.tensor_tensor(diag, diag, below, ALU.add))
                link(dve.tensor_reduce(rmaxp[:, c % 2:c % 2 + 1], flat[:, 0:(c + 1) * P], AX.X, ALU.max))
                dve.tensor_scalar(rmax[:, c % 2:c % 2 + 1], rmaxp[:, c % 2:c % 2 + 1], -1.0, None, ALU.mult
                                  ).then_inc(s_mx, 1)

            def probs_out(c):
                for b in range(c // GC + 1):
                    n = min(GW, (c + 1) * P - b * GW)
                    dst = probT[:, b * GC:b * GC + n // P, :].rearrange("p j n -> p (j n)")
                    dve.tensor_copy(dst, filled(dve, ("pt", c, b))[:, 0:n]).then_inc(drained[plan[("pt", c, b)][0]], 1)

            def attended(c):
                col = slice(c, c + 1)
                if c >= GC:
                    link(dve.tensor_tensor(rsum[:, c, 0:1], rsum[:, c, 0:1], rsum[:, c, 1:2], ALU.add))
                link(dve.reciprocal(rinv[:, col], rsum[:, c, 0:1]))
                dve.wait_ge(s_xr[1], c + 1)
                job = ("pv", c)
                dve.scalar_tensor_tensor(x[:, c, :], filled(dve, job)[:, 0:D], rinv[:, col], x[:, c, :],
                                         ALU.mult, ALU.add).then_inc(drained[plan[job][0]], 1)
                emptied(dve, job)
                stats(c)

            def choose(c):
                job = ("lg", c)
                if c == 0:
                    dve.wait_ge(s_xr[1], C)
                dve.tensor_copy(lgs[:, c, :], filled(dve, job)[:, 0:E]).then_inc(drained[plan[job][0]], 1)
                emptied(dve, job)
                link(dve.max(top[:, c, :], lgs[:, c, :]))
                link(dve.max_index(topi[:, c, :], top[:, c, :], lgs[:, c, :]))
                link(dve.tensor_copy(topf[:, c, :], topi[:, c, 0:2]))
                for k in range(2):
                    link(dve.tensor_scalar(oh[:, k, c * E:(c + 1) * E], const("iota"), topf[:, c, k:k + 1], None,
                                           ALU.is_equal))

            row_max(0)
            for c in range(C):
                if c + 1 < C:
                    row_max(c + 1)
                probs_out(c)
                attended(c)
                if c:
                    choose(c - 1)
            choose(C - 1)
            dve.tensor_tensor(oh[:, 2, :], oh[:, 0, :], oh[:, 1, :], ALU.add).then_inc(s_oh, 1)
            dve.tensor_tensor(dv8[:], top[:, :, 1], top[:, :, 0], ALU.subtract).then_inc(s_gap, 1)
            if nphase < 5:
                return
            n = C * E
            job = ("rank",)
            src = filled(dve, job)
            link(dve.tensor_copy(tot[:, 0, :], src[:, n:2 * n]))
            dve.tensor_tensor(within, src[:, 0:n], tot[:, 0, :], ALU.subtract).then_inc(drained[plan[job][0]], 1)
            emptied(dve, job)
            for i, sh in enumerate((E, 2 * E, 4 * E)):
                a, b = tot[:, i % 2, :], tot[:, 1 - i % 2, :]
                dve.tensor_copy(b[:, 0:sh], a[:, 0:sh])
                link(dve.tensor_tensor(b[:, sh:n], a[:, sh:n], a[:, 0:n - sh], ALU.add))
            upto_c = tot[:, 1, :]
            count = tot[:, 1, n - E:n]
            link(dve.tensor_scalar(ntile_i[:], count, float(P - 1), None, ALU.add))
            link(dve.tensor_scalar(ntile_i[:], ntile_i[:], 7, None, ALU.logical_shift_right))
            link(dve.tensor_copy(ntile[:], ntile_i[:]))
            link(dve.tensor_copy(ends[:, 0, :], ntile[:]))
            for i, sh in enumerate((1, 2, 4, 8)):
                a, b = ends[:, i % 2, :], ends[:, 1 - i % 2, :]
                dve.tensor_copy(b[:, 0:sh], a[:, 0:sh])
                link(dve.tensor_tensor(b[:, sh:E], a[:, sh:E], a[:, 0:E - sh], ALU.add))
            last = ends[:, 0, :]
            link(dve.tensor_tensor(base[:], last, ntile[:], ALU.subtract))
            link(dve.tensor_tensor(posn, within, upto_c, ALU.add))
            link(dve.tensor_scalar(base[:], base[:], float(P), None, ALU.mult))
            pv_ = posn.rearrange("p (c e) -> p c e", e=E)
            link(dve.tensor_tensor(pv_, pv_, over(base[:], C), ALU.add))
            for k in range(2):
                link(dve.tensor_tensor(pick[:, k, :], posn, oh[:, k, :], ALU.mult))
                link(dve.tensor_reduce(slotf[:, k, :], pick[:, k, :].rearrange("p (c e) -> p c e", e=E), AX.X, ALU.add))
            dve.tensor_copy(slots[:], slotf[:]).then_inc(s_slot, 1)
            tc = tcmp.rearrange("p (t e) -> p t e", e=E)
            link(dve.tensor_tensor(tc, over(last, TILES), wide(const("tileno"), E), ALU.is_le))
            link(dve.tensor_reduce(texp[:], tc, AX.X, ALU.add))
            dve.tensor_scalar(texp_i[:], texp[:], float(E - 1), float(EW), ALU.min, ALU.mult).then_inc(s_te, 1)
            dve.wait_ge(s_e8, 1)
            link(dve.tensor_scalar(p2[:], ex8[:], 1.0, None, ALU.add))
            link(dve.reciprocal(p1[:], p2[:]))
            link(dve.tensor_tensor(p2[:], ex8[:], p1[:], ALU.mult))

            def step(t, par, stores):
                dve.wait_ge(s_thf, t + 1)
                dve.tensor_copy(mhT[:, par, :], psum[:, 4 + par, :]).then_inc(s_thd, 1)
                if stores is not None:
                    dve.wait_ge(s_st[par], stores)
                dve.wait_ge(s_yf, t + 1)
                dve.tensor_copy(my[:, par, :], psum[:, 6 + par, 0:D]).then_inc(s_yd, 1)

            step(0, 0, None)
            step(1, 1, None)
            with dve.Fori(2, TILES - 3, 2) as t:
                for u in range(2):
                    step(t + u, u, t * 8)
            step(TILES - 3, 0, 8 * (TILES - 3))
            step(TILES - 2, 1, 8 * (TILES - 3))
            step(TILES - 1, 0, 8 * (TILES - 1))
            for c in range(C):
                dve.wait_ge(s_gat[c], 32)
                link(dve.scalar_tensor_tensor(x[:, c, :], xn[:, c, :], p1[:, c:c + 1], x[:, c, :], ALU.mult, ALU.add))
                dve.scalar_tensor_tensor(x[:, c, :], y[:, c, :], p2[:, c:c + 1], x[:, c, :], ALU.mult, ALU.add
                                         ).then_inc(s_res, 1)


def kernel(upto=9, **inputs):
    import numpy as _np
    import concourse.bacc as _bacc
    from concourse import mybir as _mybir
    from concourse.bass_utils import run_bass_kernel_spmd as _run

    a = {k: _np.asarray(v) for k, v in inputs.items()}

    def rows(w):
        return _np.ascontiguousarray(w.reshape(-1, P, w.shape[-1]).transpose(1, 0, 2))

    def column(vec):
        return vec.reshape(-1, P).T

    def spread_row(vec):
        return _np.broadcast_to(vec[None, :], (P, vec.shape[0]))

    qkv = a["L1_attn_qkv"]
    su_ug, ws_ug = a["L0_ffn_SU_ug"], a["L0_ffn_Wscale_ug"]
    vectors = _np.concatenate([
        column(a["L0_attn_retn_norm_w"]), column(a["L0_attn_final_norm_w"]), column(a["L0_attn_fc1_b"]),
        column(su_ug), column(ws_ug[:F]), column(ws_ug[F:]), column(a["L0_ffn_SU_dp"]),
        column(a["L1_attn_gamma"]), column(a["L1_attn_beta"]), spread_row(a["L0_attn_fc2_b"]),
        spread_row(a["L0_ffn_Wscale_dp"])], axis=1)
    arrays = {
        "x_in": a["L0_attn_x"].reshape(T, D),
        "const_in": constants(),
        "vec_in": vectors,
        "qkvg_in": rows(_np.concatenate([a["L0_attn_q_w"], a["L0_attn_k_w"], a["L0_attn_v_w"], a["L0_attn_g_w"]], axis=1)),
        "out_w_in": rows(a["L0_attn_out_w"]),
        "fc1_in": rows(a["L0_attn_fc1_w"]),
        "fc2_in": rows(a["L0_attn_fc2_w"]),
        "upgate_in": rows(_np.concatenate([a["L0_ffn_W_up"].T, a["L0_ffn_W_gate"].T], axis=1)),
        "down_in": rows(a["L0_ffn_W_down"].T),
        "wqt_in": rows(qkv[:, :D].T),
        "wkt_in": rows(qkv[:, D:2 * D].T),
        "wvt_in": rows(qkv[:, 2 * D:].T),
        "o_in": rows(a["L1_attn_o_proj"]),
        "router_in": rows(a["L1_ffn_router_w"]),
        "experts_in": _np.concatenate([
            a["L1_ffn_W1"].reshape(E, KT, P, FE).transpose(0, 2, 1, 3).reshape(E, P, KT * FE),
            a["L1_ffn_W2"].reshape(E, FEM, P, D).transpose(0, 2, 1, 3).reshape(E, P, FEM * D)], axis=2),
    }
    nc = _bacc.Bacc("TRN2", target_bir_lowering=False, num_devices=1)
    arrays = {k: _np.ascontiguousarray(v) for k, v in arrays.items()}
    args = {k: nc.dram_tensor(k, v.shape, _mybir.dt.from_np(v.dtype), kind="ExternalInput").ap()
            for k, v in arrays.items()}
    out = nc.dram_tensor("out", (T, D), F32, kind="ExternalOutput").ap()
    build(nc, out=out, upto=upto, **args)
    r = _run(nc, [arrays], core_ids=[0])
    return r.results[0]["out"].reshape(1, T, D)
```

```python
from contextlib import ExitStack

import numpy as np

import concourse.bass as bass
from concourse import mybir

F32 = mybir.dt.float32
I32 = mybir.dt.int32
U32 = mybir.dt.uint32
ALU = mybir.AluOpType
ACT = mybir.ActivationFunctionType
AX = mybir.AxisListType

P = 128
T, D = 1024, 256
C = T // P
KT = D // P
H, DH = 16, 16
HT = H // KT
F = 1024
FM = F // P
GC = 4
G = C // GC
GW = GC * P
E, FE = 16, 512
FEM = FE // P
EW = KT * FE + FEM * D
TILES = (2 * T) // P + E - 1
AHEAD = 3
LOADS = 4
HEAD = 2
LOOPED = HEAD + (TILES - LOADS - HEAD) // LOADS * LOADS
EPS = 1e-5
NEG = -3.0e38


def constant_columns():
    widths = [("ident", P), ("tril", P), ("below", P), ("had", P), ("hadneg", P), ("strict", P),
              ("ones", P), ("headmask", HT), ("cos", C * DH), ("sin", C * DH), ("growth", H),
              ("rowscale", C * H), ("stateblock", KT * HT * (DH + 1)), ("statedecay", KT),
              ("iota", P), ("tileno", TILES),
              ("token1", C), ("spare", 1)]
    at, out = 0, {}
    for name, w in widths:
        out[name] = (at, w)
        at += w
    return out, at

def constants():
    cols, n = constant_columns()
    out = np.zeros((P, n), np.float32)

    def put(name, a):
        at, w = cols[name]
        out[:, at:at + w] = np.asarray(a, np.float64).reshape(P, w).astype(np.float32)

    i = np.arange(P)
    put("ident", np.eye(P))
    put("tril", i[:, None] <= i[None, :])
    put("below", np.where(i[None, :] > i[:, None], NEG, 0.0))
    bits = np.array([[bin(a & b).count("1") for b in range(P)] for a in range(P)])
    put("had", (-1.0) ** bits)
    put("hadneg", -((-1.0) ** bits))
    put("strict", i[:, None] < i[None, :])
    put("ones", np.ones((P, P)))
    put("headmask", i[:, None] // DH == np.arange(HT)[None, :])
    angle = (np.float32(1.0) / np.float32(10000.0) ** np.linspace(0, 1, DH // 2, dtype=np.float32)).astype(np.float32)
    angle = np.repeat(angle, 2)
    phase = (np.arange(T, dtype=np.float32)[:, None] * angle[None, :]).astype(np.float32)
    sign = np.where(np.arange(DH) % 2 == 0, -1.0, 1.0)
    put("cos", np.cos(phase.astype(np.float64)).reshape(C, P, DH).transpose(1, 0, 2))
    put("sin", (np.sin(phase.astype(np.float64)) * sign).reshape(C, P, DH).transpose(1, 0, 2))
    gamma = 1.0 - 2.0 ** (-5.0 - np.arange(H))
    put("growth", gamma[None, :] ** (-i[:, None].astype(np.float64)))
    tok = np.arange(T, dtype=np.float64)[:, None]
    rows = (1.0 - gamma[None, :] ** (tok + 1)) / (1.0 - gamma[None, :])
    scale = gamma[None, :] ** (tok % P) / np.sqrt(rows) * DH ** -0.5
    put("rowscale", scale.reshape(C, P, H).transpose(1, 0, 2))
    block = np.zeros((P, KT, HT, DH + 1))
    decay = np.zeros((P, KT))
    for k in range(KT):
        for p in range(P):
            g = gamma[k * HT + p // DH] ** P
            block[p, k, p // DH, :] = g
            decay[p, k] = g
    put("stateblock", block)
    put("statedecay", decay)
    put("iota", np.tile(np.arange(P), (P, 1)))
    put("tileno", np.tile(np.arange(TILES), (P, 1)))
    put("token1", i[:, None] + P * np.arange(C)[None, :] + 1)
    put("spare", T + 1 + i[:, None])
    return out

def vector_columns():
    widths = [("retn_w", KT), ("final_w", KT), ("fc1_b", FM), ("su_ug", KT), ("scale_up", FM),
              ("scale_gate", FM), ("su_dp", FM), ("gamma", KT), ("beta", KT), ("fc2_b", D), ("scale_dp", D)]
    at, out = 0, {}
    for name, w in widths:
        out[name] = (at, w)
        at += w
    return out, at


def score_banks(c):
    return [c] if c < GC else [2 * (c % 2), 2 * (c % 2) + 1]

def turn_bank(c, b):
    return 4 + (c % 2 if c < GC else b)

def psum_plan():
    order = []

    def job(bank, *name):
        order.append((name, bank))

    def project(c):
        job(0, "qk", c)
        job(1, "vg", c)

    job(2, "xt", 0)
    project(0)
    job(2, "qkt", 0)
    job(2, "xt", 1)
    project(1)
    job(2, "xt", 2)
    for c in range(C):
        for n in range(4):
            job((3, 4, 7, 3)[n], "p", c, n)
        if c + 1 < C:
            job(2, "qkt", c + 1)
        job(5, "o", c)
        if c + 2 < C:
            project(c + 2)
        else:
            for m in range(KT):
                job(m, ("m", "vo")[c + 2 - C], m)
        if c + 1 < C:
            job(6, "st", c)
        if c:
            job(7, "ot", c - 1)
            job(7, "y", c - 1)
        if c + 3 < C:
            job(2, "xt", c + 3)
    for c in range(GC):
        job(c % 2, "bt", c)
    for g in range(G):
        for m in range(FM):
            job(2 + m % 2, "fc1", g, m)
            if (g, m) == (0, 1):
                job(7, "ot", C - 1)
            if (g, m) == (0, 2):
                job(7, "y", C - 1)
            if g == 0 and m >= FM - GC:
                job(m % 2, "bt", GC + m - (FM - GC))
    for n in range(4):
        job(4 + n, "wd", n)
    for c in range(C):
        job(4 + c % 2, "fc2", c)
        if c >= AHEAD:
            job(c % 2, "ct", c - AHEAD)
    for g in range(G):
        if g == 0:
            for m in range(KT):
                job(6 + m, "had", g, m)
        for m in range(FM):
            if g == 0 and m < AHEAD:
                job(m % 2, "ct", C - AHEAD + m)
            job(2 + m % 2, "gate", g, m)
            job(4 + m % 2, "up", g, m)
            if g == 0 and m == FM - 2:
                for k in range(KT):
                    job(6 + k, "had", 1, k)
    for c in range(C):
        job(6 + c % 2, "down", c)
        if c >= AHEAD:
            job(c % 2, "dt", c - AHEAD)
    for m in range(KT):
        job(2 + m, "qm", 0, m)
    job(7, "dt", C - 3)
    for c in range(GC):
        job(4 + c % 2, "v", c)
    job(6, "dt", C - 2)
    job(7, "dt", C - 1)

    def scores(c):
        for b in range(c // GC + 1):
            job(score_banks(c)[b], "sc", c, b)

    scores(0)
    scores(1)
    for m in range(KT):
        job(2 + m, "qm", 1, m)
    for c in range(C):
        for b in range(c // GC + 1):
            job(turn_bank(c, b), "pt", c, b)
        if c + 2 < C:
            scores(c + 2)
        if c < GC:
            job(7, "v", c + GC)
        if c:
            job(7, "zt", c - 1)
        job(6, "pv", c)
        if c:
            job(7, "lg", c - 1)
    job(7, "zt", C - 1)
    job(7, "lg", C - 1)
    job(0, "rank")
    job(1, "map")
    fills, plan = [0] * 8, {}
    for name, bank in order:
        fills[bank] += 1
        plan[name] = (bank, fills[bank])
    return plan, fills

def build(nc, x_in, const_in, vec_in, qkvg_in, out_w_in, fc1_in, fc2_in, upgate_in, down_in, wqt_in, wkt_in,
          wvt_in, o_in, router_in, experts_in, out, upto=9):
    ccol, cn = constant_columns()
    vcol, vn = vector_columns()
    plan, fills = psum_plan()

    with ExitStack() as ctx:
        def sb(name, *shape, dt=F32):
            return ctx.enter_context(nc.sbuf_tensor(name, [P, *shape], dt))

        def sem(name):
            return ctx.enter_context(nc.semaphore(name))

        cst = sb("cst", cn)
        vec = sb("vec", vn)

        def const(name, *dims):
            at, w = ccol[name]
            return cst[:, at:at + w]

        def vector(name):
            at, w = vcol[name]
            return vec[:, at:at + w]

        ident, tril, below = const("ident"), const("tril"), const("below")
        had, hadneg, strict, ones = const("had"), const("hadneg"), const("strict"), const("ones")
        headmask = const("headmask")
        cos = const("cos").rearrange("p (c d) -> p c d", c=C)
        sin = const("sin").rearrange("p (c d) -> p c d", c=C)
        growth = const("growth")
        rowscale = const("rowscale").rearrange("p (c h) -> p c h", c=C)
        stateblock, statedecay = const("stateblock"), const("statedecay")

        x = sb("x", C, D)
        y = sb("y", C, D)
        xn = sb("xn", C, D)
        featT = sb("featT", KT, T)
        raw = sb("raw", C, 2)
        bn = sb("bn", 2, 6)
        ssq = sb("ssq", C)
        rstd = sb("rstd", C)
        rs2 = sb("rs2", C)
        rs2f = sb("rs2f", C)
        tmp1 = sb("tmp1", C)
        tmp2 = sb("tmp2", C)
        shift = sb("shift", C)
        shift2 = sb("shift2", C)

        experts = sb("experts", E * EW)
        region = [experts[:, 0:E // 2 * EW], experts[:, E // 2 * EW:]]
        used = [0, 0]

        def carve(r, *shape):
            n = int(np.prod(shape))
            ap = region[r][:, used[r]:used[r] + n]
            used[r] += n
            assert used[r] <= E // 2 * EW
            if len(shape) == 2:
                ap = ap.rearrange("p (a b) -> p a b", a=shape[0])
            elif len(shape) == 3:
                ap = ap.rearrange("p (a b c) -> p a b c", a=shape[0], b=shape[1])
            return ap

        w_qkvg = carve(0, KT, 4 * D)
        w_out = carve(0, KT, D)
        hT = carve(0, 2, KT, P)
        rotc = carve(0, 2 * D)
        rots = carve(0, 2 * D)
        qk = carve(0, 2, 2 * D)
        qkT = carve(0, 2, 4, P)
        qx = carve(0, KT, HT * P)
        pT = carve(0, H, P)
        va = carve(0, 2, H * (DH + 1))
        sg = carve(0, 3, D)
        state = carve(0, KT, HT * (DH + 1))
        statetmp = carve(0, KT, HT * (DH + 1))
        den = carve(0, H)
        rden = carve(0, H)
        wrow = carve(0, H)
        o1 = carve(0, D)
        osq = carve(0, D)
        oss = carve(0, H)
        ors = carve(0, H)
        o2 = osq
        o3 = carve(0, 2, D)
        oT = carve(0, KT, P)
        sqj = carve(0, D)
        x1i = y
        halfs = sb("halfs", H)

        hidT = carve(1, FM, T)
        w_ug = carve(1, KT, 2 * F)
        uT = carve(1, KT, T)
        w_down = carve(1, FM, D)
        wdA = carve(0, FM, D)
        wdB = uT.rearrange("p a (b n) -> p (a b) n", n=D)

        ffw = sb("ffw", 2 * KT * F)
        w_fc1 = ffw[:, 0:KT * F].rearrange("p (k n) -> p k n", k=KT)
        w_fc2 = ffw[:, KT * F:].rearrange("p (m n) -> p m n", m=FM)
        qT = ffw[:, 0:KT * T].rearrange("p (k n) -> p k n", k=KT)
        v = ffw[:, KT * T:].rearrange("p (c n) -> p c n", c=C)
        attn = sb("attn", 3 * T)
        prob = attn[:, 0:2 * T].rearrange("p (b n) -> p b n", n=GW)
        probT = attn[:, 2 * T:].rearrange("p (j n) -> p j n", j=C)
        w_at = attn[:, 0:3 * KT * D].rearrange("p (a k n) -> p a k n", a=3, k=KT)
        silu_g = sb("silu_g", 2, GW)
        w_o = carve(0, KT, D)
        w_m = sb("w_m", KT, D)
        w_vo = sb("w_vo", KT, D)
        w_r = sb("w_r", KT, E)
        w_spare = uT[:, 0, 0:D]
        scpar = sb("scpar", FM)
        scup = sb("scup", FM)
        rmax = sb("rmax", C)
        rsum = sb("rsum", C, 2)
        rmaxp = sb("rmaxp", C)
        rinv = sb("rinv", C)
        flat_y = y[:].rearrange("p c d -> p (c d)")
        zT = flat_y[:, 0:D].rearrange("p (k n) -> p k n", k=KT)
        oh = flat_y[:, D:D + 3 * C * E].rearrange("p (a n) -> p a n", a=3)
        tot, pick = (flat_y[:, at:at + 2 * C * E].rearrange("p (a n) -> p a n", a=2) for at in (3 * D, 4 * D))
        within, posn = flat_y[:, 5 * D:5 * D + C * E], flat_y[:, 5 * D + C * E:6 * D]
        lgs = sb("lgs", C, E)
        top = sb("top", C, 8)
        topi = sb("topi", C, 8, dt=U32)
        topf = sb("topf", C, 2)
        dv8 = sb("dv8", C)
        ex8 = sb("ex8", C)
        p12 = sb("p12", 2, C)
        ends = sb("ends", 2, E)
        ntile = sb("ntile", E)
        ntile_i = sb("ntile_i", E, dt=I32)
        base = sb("base", E)
        slotf = sb("slotf", 2 * C)
        slot_i = sb("slot_i", 3, 2 * C, dt=I32)
        rowf = sb("rowf", 2 * C)
        tilef = sb("tilef", 2 * C)
        id1, weight, idtmp, source, target, texp, texp_i = (
            flat_y[:, 6 * D + i * 32:6 * D + i * 32 + TILES] for i in range(7))
        source, target, texp_i = source.bitcast(U32), target.bitcast(U32), texp_i.bitcast(I32)
        source_span = flat_y[:, 6 * D + 3 * 32:6 * D + 3 * 32 + TILES + LOADS].bitcast(U32)
        source_t = sb("source_t", LOADS, dt=U32)
        target_t = sb("target_t", 2, dt=U32)
        def two(ap):
            return ap.rearrange("p (b n) -> p b n", b=2)

        mh = two(attn[:, 0:2 * FE])
        mhT = two(attn[:, 2 * FE:4 * FE])
        mx = xn
        my = two(attn[:, 4 * FE:4 * FE + 2 * D])
        mxT = two(silu_g[:, 0, :])
        tcmp = silu_g[:, 1, 0:TILES * E]
        onerow = featT[:].rearrange("p k n -> p (k n)").rearrange("p (a n) -> p a n", n=P)
        onetile = ffw[:, 0:2 * C * TILES].rearrange("p (a n) -> p a n", n=TILES)
        idpair = ffw[:, KT * T:KT * T + 2 * C * 2 * TILES].rearrange("p (a b n) -> p a b n", b=2, n=TILES)

        psum = ctx.enter_context(nc.psum_tensor("psum", [P, 8, 512], F32))

        ztok = nc.dram_tensor("router_input", [T, D], F32, kind="Internal").ap()

        full = [sem(f"psum_full{b}") for b in range(8)]
        drained = [sem(f"psum_drained{b}") for b in range(8)]
        s_cst, s_qkvg, s_outw, s_vec = sem("const_loaded"), sem("qkvg_loaded"), sem("outw_loaded"), sem("vec_loaded")
        s_fc, s_down, s_ug, s_at, s_o = sem("fc_loaded"), sem("down_loaded"), sem("upgate_loaded"), sem("attw_loaded"), sem("o_loaded")
        s_exp = [sem("experts_lo_loaded"), sem("experts_hi_loaded")]
        s_x = [sem(f"x_loaded{n}") for n in range(4)]
        s_scale = sem("norm_scales")
        s_spare = sem("spare_rows_zeroed")
        s_ztok = sem("router_input_stored")
        s_x3 = sem("residual_stored")
        s_p = sem("gate_weights_ready")
        s_map = sem("place_factors_ready")
        s_src = sem("tile_sources_ready")
        s_add = sem("tile_added")
        s_dv = sem("vector_steps")
        s_pl = sem("pool_steps")
        s_ac = sem("scalar_steps")
        s_init = sem("buffers_set")
        s_par = sem("ffn_scales_ready")
        s_stat = sem("stats_ready")
        s_xn = [sem(f"normalised{ph}") for ph in range(5)]
        s_y = sem("layernorm_ready")
        s_xr = [sem("ffn_residual"), sem("attn_residual")]
        s_oss = sem("head_squares")
        s_qk = sem("rotated")
        s_va = sem("values_ready")
        s_qx = [sem(f"queries_spread{k}") for k in range(KT)]
        s_state = sem("state_ready")
        s_ors = sem("head_rms_ready")
        s_o3 = sem("gated_ready")
        s_bfly = sem("butterflies")
        s_mx = sem("rowmax_ready")
        s_gap = sem("logit_gap_ready")
        s_e8 = sem("gap_exp_ready")
        s_oh = sem("onehot_ready")
        s_te = sem("tile_experts_ready")
        s_ld = [sem(f"tile_loaded{n}") for n in range(LOADS)]
        s_txf, s_txd = sem("tile_xT_full"), sem("tile_xT_drained")
        s_hf, s_hd = sem("tile_h_full"), sem("tile_h_drained")
        s_thf, s_thd = sem("tile_hT_full"), sem("tile_hT_drained")
        s_yf, s_yd = sem("tile_y_full"), sem("tile_y_drained")
        s_out = sem("result_stored")

        def turned(c):
            return GC * (c % 2) if c < GC else 0

        def bank(job):
            b, _ = plan[job]
            return psum[:, b, :]

        def filled(eng, job):
            b, n = plan[job]
            eng.wait_ge(full[b], n)
            return psum[:, b, :]

        def emptied(eng, job):
            b, n = plan[job]
            eng.wait_ge(drained[b], n)

        gate = E // 2 * EW
        nphase = upto

        block = ctx.enter_context(nc.Block())

        @block.sync
        def _(sp):
            xs = x_in.rearrange("(c p) d -> p c d", p=P)
            for n in range(4):
                sp.dma_start(x[:, 2 * n:2 * n + 2, :], xs[:, 2 * n:2 * n + 2, :]).then_inc(s_x[n], 16)
                if n == 0:
                    sp.dma_start(cst[:], const_in).then_inc(s_cst, 16)
                    sp.dma_start(w_qkvg, qkvg_in).then_inc(s_qkvg, 16)
            sp.dma_start(w_out, out_w_in).then_inc(s_outw, 16)
            sp.dma_start(wdA, down_in).then_inc(s_down, 16)
            sp.dma_start(w_at[:, 0], wqt_in).then_inc(s_at, 16)
            sp.dma_start(w_at[:, 1], wkt_in).then_inc(s_at, 16)
            sp.dma_start(w_at[:, 2], wvt_in).then_inc(s_at, 16)
            sp.dma_start(w_o, o_in).then_inc(s_at, 16)
            sp.dma_start(w_fc1, fc1_in).then_inc(s_fc, 16)
            sp.dma_start(w_fc2, fc2_in).then_inc(s_fc, 16)
            sp.dma_start(w_ug, upgate_in).then_inc(s_ug, 16)
            sp.dma_start(w_r[:], router_in).then_inc(s_o, 16)
            if nphase >= 5:
                sp.wait_ge(full[plan[("y", C - 1)][0]], plan[("y", C - 1)][1])
                sp.wait_ge(s_xn[1], C)
                sp.wait_ge(s_bfly, 1)
                for e in range(E // 2):
                    sp.dma_start(region[0][:, e * EW:(e + 1) * EW], experts_in[e]).then_inc(s_exp[0], 16)
                sp.wait_ge(full[plan[("down", C - 1)][0]], plan[("down", C - 1)][1])
                for e in range(E // 2):
                    sp.dma_start(region[1][:, e * EW:(e + 1) * EW], experts_in[E // 2 + e]).then_inc(s_exp[1], 16)
                for c in range(C):
                    sp.wait_ge(s_xn[4], c + 1)
                    sp.dma_start(ztok[c * P:(c + 1) * P, :], xn[:, c, :]).then_inc(s_ztok, 16)
                    sp.dma_start(out[c * P:(c + 1) * P, :], x[:, c, :]).then_inc(s_x3, 16)
            else:
                src = {1: y, 2: x, 3: xn, 4: x}[nphase]
                sp.wait_ge(s_xn[nphase], C)
                sp.dma_start(out[0:T, :].rearrange("(c p) d -> p c d", p=P), src[:]).then_inc(s_out, 16)
                sp.wait_ge(s_out, 16)

        @block.gpsimd
        def _(pool):
            steps = [0]

            def link(ins):
                steps[0] += 1
                ins.then_inc(s_pl, 1)
                pool.wait_ge(s_pl, steps[0])

            def power(dst, src):
                return pool.tensor_tensor(dst, src, halfs[:, 0:dst.shape[1]], ALU.pow)

            def norm(ph, c, double):
                col = slice(c, c + 1)
                pool.wait_ge(s_stat, ph * C + c + 1)
                ins = pool.tensor_scalar(tmp1[:, col], raw[:, c, 1:2], EPS, None, ALU.add)
                if double:
                    ins = pool.tensor_scalar(tmp2[:, col], raw[:, c, 1:2], 1.0 + EPS, EPS * EPS, ALU.mult, ALU.add)
                link(ins)
                ins = power(rstd[:, col], tmp1[:, col])
                if double:
                    ins = power(rs2[:, col], tmp2[:, col])
                link(ins)
                ins = pool.tensor_scalar(shift[:, col], raw[:, c, 0:1], rstd[:, col], -1.0, ALU.mult, ALU.mult)
                if double:
                    ins = pool.tensor_scalar(shift2[:, col], raw[:, c, 0:1], rs2[:, col], -1.0, ALU.mult, ALU.mult)
                ins.then_inc(s_scale, 1)

            def attention_residual(c):
                pool.wait_ge(s_y, C + c + 1)
                pool.tensor_tensor(x[:, c, :], x[:, c, :], y[:, c, :], ALU.add).then_inc(s_xr[1], 1)

            def head_rms(c):
                pool.wait_ge(s_oss, c + 1)
                link(pool.tensor_scalar(oss, oss, 1.0 / DH, EPS, ALU.mult, ALU.add))
                pool.tensor_tensor(ors, oss, halfs[:], ALU.pow).then_inc(s_ors, 1)

            def ffn_norm(c):
                col = slice(c, c + 1)
                pool.wait_ge(s_ac, c + 1)
                link(pool.tensor_scalar(tmp1[:, col], ssq[:, col], 1.0 / D, EPS, ALU.mult, ALU.add))
                power(rs2f[:, col], tmp1[:, col]).then_inc(s_scale, 1)
                link(pool.tensor_tensor(x[:, c, :], x[:, c, :], x1i[:, c, :], ALU.add))
                pool.tensor_tensor(x[:, c, :], x[:, c, :], vector("fc2_b"), ALU.add).then_inc(s_xr[0], 1)

            def butterfly(stage, half):
                src, dst = ((wdA, wdB), (wdB, wdA), (wdA, wdB))[stage]
                a = src.rearrange("p (o t i) n -> p o t (i n)", t=2, i=1 << stage)
                b = dst.rearrange("p (o t i) n -> p o t (i n)", t=2, i=1 << stage)
                return pool.tensor_tensor(b[:, :, half], a[:, :, 0], a[:, :, 1], (ALU.add, ALU.subtract)[half])

            link(pool.memset(halfs[:], -0.5))
            link(pool.memset(state, 0.0))
            pool.memset(w_spare, 0.0).then_inc(s_init, 1)
            pool.wait_ge(s_cst, 16)
            for n in range(2):
                va_n = va[:, n].rearrange("p (h e) -> p h e", e=DH + 1)
                pool.tensor_copy(va_n[:, :, DH], growth).then_inc(s_init, 1)
            pool.wait_ge(s_init, 3)
            pool.dma_start(out[T:T + P, :], w_spare).then_inc(s_spare, 16)
            def rotated(c):
                emptied(pool, ("qk", c))
                if c >= 2:
                    filled(pool, ("st", c - 2))
                pool.tensor_tensor(qk[:, c % 2, :], rotc, rots, ALU.add).then_inc(s_qk, 1)

            for c in range(3):
                norm(0, c, True)
            pool.wait_ge(s_vec, 16)
            rotated(0)
            rotated(1)
            norm(0, 3, True)
            for c in range(C):
                if c:
                    head_rms(c - 1)
                if c + 4 < C:
                    norm(0, c + 4, True)
                if c >= 2:
                    ffn_norm(c - 2)
                if c + 2 < C:
                    rotated(c + 2)
            head_rms(C - 1)
            ffn_norm(C - 2)
            ffn_norm(C - 1)
            pool.wait_ge(s_spare, 16)
            pool.wait_ge(s_down, 16)
            for n in range(6):
                ins = butterfly(n // 2, n % 2)
                if n == 5:
                    ins.then_inc(s_bfly, 1)
                else:
                    link(ins)
            for c in range(C):
                norm(1, c, False)
            if nphase >= 3:
                for c in range(C):
                    norm(2, c, True)
                    if c:
                        attention_residual(c - 1)
                attention_residual(C - 1)
            if nphase >= 4:
                for c in range(C):
                    norm(3, c, False)
            if nphase >= 5:
                pool.wait_ge(s_ztok, 16 * C)
                pool.wait_ge(s_x3, 16 * C)
                pool.wait_ge(s_spare, 16)

                def gather(t, n):
                    pool.wait_ge(s_src, t + 1)
                    pool.indirect_dma_start(
                        out=mx[:, n, :], out_offset=None, in_=ztok,
                        in_offset=bass.IndirectOffsetOnAxis(ap=source_t[:, n:n + 1], axis=0)).then_inc(s_ld[n], 16)

                def step(t, u, last=False):
                    par, n = u % 2, u % LOADS
                    if not last:
                        pool.wait_ge(s_txf, t + 1)
                        gather(t + LOADS, n)
                    pool.wait_ge(s_yd, t + 1)
                    if t:
                        pool.wait_ge(s_add, t * 16)
                    pool.indirect_dma_start(
                        out=out, out_offset=bass.IndirectOffsetOnAxis(ap=target_t[:, par:par + 1], axis=0),
                        in_=my[:, par, :], in_offset=None, compute_op=ALU.add, bounds_check=T + P - 1
                    ).then_inc(s_add, 16)

                for n in range(LOADS):
                    gather(n, n)
                for t in range(TILES):
                    step(t, t, last=t + LOADS >= TILES)
                pool.wait_ge(s_add, 16 * TILES)

        @block.scalar
        def _(act):
            act.dma_start(vec[:], vec_in).then_inc(s_vec, 16)
            act.wait_ge(s_vec, 16)

            def drain(job, dst, scale=1.0, func=ACT.Copy, src=None):
                b, _ = plan[job]
                p_ = filled(act, job)
                act.activation(dst, src(p_) if src else p_[:, 0:dst.free_size()], func, scale=scale).then_inc(drained[b], 1)

            def drain2(job, dst, name, bias=None):
                b, _ = plan[job]
                p_ = filled(act, job)
                for k in range(KT):
                    kw = {"bias": vector(bias)[:, k:k + 1]} if bias else {}
                    ins = act.activation(dst[:, k, :], p_[:, k * P:(k + 1) * P], ACT.Identity,
                                         scale=vector(name)[:, k:k + 1], **kw)
                ins.then_inc(drained[b], 1)

            def normal(ph, c, n, double):
                col = slice(c, c + 1)
                act.wait_ge(s_scale, n)
                a, b = (rs2, shift2) if double else (rstd, shift)
                act.activation(xn[:, c, :], x[:, c, :], ACT.Identity, scale=a[:, col], bias=b[:, col]
                               ).then_inc(s_xn[ph], 1)
                if double:
                    act.activation(y[:, c, :], x[:, c, :], ACT.Identity, scale=rstd[:, col], bias=shift[:, col]
                                   ).then_inc(s_y, 1)

            def xt(c):
                drain2(("xt", c), hT[:, c % 2], "retn_w")

            def ffn_in(c):
                act.wait_ge(s_scale, min(C, c + 7) + c + 1)
                act.activation(xn[:, c, :], x1i[:, c, :], ACT.Copy, scale=rs2f[:, c:c + 1]).then_inc(s_xn[1], 1)

            def gate_g(c):
                act.wait_ge(s_va, c + 1)
                if c >= 3:
                    act.wait_ge(s_o3, c - 2)
                b, _ = plan[("vg", c)]
                act.activation(sg[:, c % 3, :], bank(("vg", c))[:, D:2 * D], ACT.Silu).then_inc(drained[b], 1)

            def ot(c):
                drain(("ot", c), oT.rearrange("p k n -> p (k n)"))

            def square(c):
                emptied(act, ("y", c))
                act.activation(sqj, x1i[:, c, :], ACT.Square, accum_out=ssq[:, c:c + 1]).then_inc(s_ac, 1)

            def qkt(c):
                drain(("qkt", c), qkT[:, c % 2].rearrange("p a n -> p (a n)"))
                emptied(act, ("qkt", c))
                for h in range(HT):
                    ins = act.activation(qx[:, 1, h * P:(h + 1) * P], qkT[:, c % 2, 1, :], ACT.Copy,
                                         scale=headmask[:, h:h + 1])
                ins.then_inc(s_qx[1], 1)

            def block_input(c):
                normal(0, c, c + 1 + max(0, c - 6), True)

            block_input(0)
            xt(0)
            block_input(1)
            act.wait_ge(s_cst, 16)
            qkt(0)
            gate_g(0)
            xt(1)
            block_input(2)
            gate_g(1)
            xt(2)
            for c in range(C):
                if c >= 2:
                    square(c - 2)
                if c + 3 < C:
                    block_input(c + 3)
                if c + 1 < C:
                    qkt(c + 1)
                if c >= 3:
                    ffn_in(c - 3)
                if c:
                    ot(c - 1)
                if c + 2 < C:
                    gate_g(c + 2)
                elif c == C - 2:
                    for m in range(KT):
                        drain(("m", m), w_m[:, m, :], scale=float(D) ** -0.5)
                else:
                    for m in range(KT):
                        drain(("vo", m), w_vo[:, m, :])
                if c + 3 < C:
                    xt(c + 3)
            square(C - 2)
            ffn_in(C - 3)

            def bt(c):
                drain2(("bt", c), featT[:, :, c * P:(c + 1) * P], "final_w")

            def ct(c):
                drain2(("ct", c), featT[:, :, c * P:(c + 1) * P], "su_ug")

            def dt(c):
                drain2(("dt", c), featT[:, :, c * P:(c + 1) * P], "gamma", "beta")

            def hadamard(g):
                for m in range(KT):
                    drain(("had", g, m), uT[:, m, g * GW:(g + 1) * GW])

            def queries(g):
                for m in range(KT):
                    drain(("qm", g, m), qT[:, m, g * GW:(g + 1) * GW])

            for c in range(GC):
                bt(c)
            for g in range(G):
                for m in range(FM):
                    b, _ = plan[("fc1", g, m)]
                    act.activation(hidT[:, m, g * GW:(g + 1) * GW], filled(act, ("fc1", g, m)),
                                   ACT.Gelu_apprx_tanh, bias=vector("fc1_b")[:, m:m + 1]).then_inc(drained[b], 1)
                    if (g, m) == (0, 1):
                        ot(C - 1)
                    if (g, m) == (0, 2):
                        ffn_in(C - 2)
                    if (g, m) == (0, 3):
                        square(C - 1)
                    if (g, m) == (0, FM - 2):
                        ffn_in(C - 1)
                    if g == 0 and m >= FM - GC:
                        bt(GC + m - (FM - GC))
            if nphase < 3:
                return
            for c in range(C):
                normal(2, c, 2 * C + c + 1, False)
                if c >= AHEAD:
                    ct(c - AHEAD)
            hadamard(0)
            act.wait_ge(s_par, 2)
            for g in range(G):
                for m in range(FM):
                    if g == 0 and m < AHEAD:
                        ct(C - AHEAD + m)
                    n = g * FM + m
                    if n >= 2:
                        emptied(act, ("up", (n - 2) // FM, (n - 2) % FM))
                    b, _ = plan[("gate", g, m)]
                    act.activation(silu_g[:, n % 2, :], filled(act, ("gate", g, m)), ACT.Silu,
                                   scale=scpar[:, m:m + 1]).then_inc(drained[b], 1)
                    if g == 0 and m == FM - 2:
                        hadamard(1)
            if nphase < 4:
                return
            for c in range(C):
                normal(3, c, 3 * C + c + 1, True)
                if c >= AHEAD:
                    dt(c - AHEAD)
            queries(0)
            dt(C - 3)
            for c in range(GC):
                drain(("v", c), v[:, c, :])
            dt(C - 2)
            dt(C - 1)

            def exps(c):
                act.wait_ge(s_mx, c + 1)
                if c >= GC + 2:
                    for b_ in range(2):
                        filled(act, ("pt", c - 2, b_))
                elif c >= GC:
                    for c_ in score_banks(c):
                        filled(act, ("pt", c_, 0))
                for b_ in range(c // GC + 1):
                    n = min(GW, (c + 1) * P - b_ * GW)
                    act.activation(prob[:, score_banks(c)[b_], 0:n], bank(("sc", c, b_))[:, 0:n], ACT.Exp,
                                   bias=rmax[:, c:c + 1], accum_out=rsum[:, c, b_:b_ + 1]
                                   ).then_inc(drained[plan[("sc", c, b_)][0]], 1)

            def zt(c):
                normal(4, c, 4 * C + c + 1, False)
                if c == 0:
                    act.wait_ge(s_xr[1], C)
                drain(("zt", c), zT.rearrange("p k n -> p (k n)"))

            exps(0)
            queries(1)
            for c in range(C):
                if c + 1 < C:
                    exps(c + 1)
                if c < GC:
                    drain(("v", c + GC), v[:, c + GC, :])
                if c:
                    zt(c - 1)
            zt(C - 1)
            act.wait_ge(s_gap, 1)
            act.activation(ex8[:], dv8[:], ACT.Exp).then_inc(s_e8, 1)
            if nphase < 5:
                return

            def tile_xT(t, par):
                act.wait_ge(s_txf, t + 1)
                act.activation(mxT[:, par, :], psum[:, par, 0:KT * P], ACT.Copy).then_inc(s_txd, 1)

            def tile_silu(t, par):
                act.wait_ge(s_hf, t + 1)
                act.activation(mh[:, par, :], psum[:, 2 + par, :], ACT.Silu).then_inc(s_hd, 1)

            def step(t, par):
                tile_silu(t + 1, 1 - par)
                tile_xT(t + 2, par)

            tile_xT(0, 0)
            tile_silu(0, 0)
            tile_xT(1, 1)
            step(0, 0)
            step(1, 1)
            with act.Fori(2, TILES - 3, 2) as t:
                step(t, 0)
                step(t + 1, 1)
            step(TILES - 3, 0)
            tile_silu(TILES - 1, 0)

        @block.tensor
        def _(pe):
            def fill(job):
                b, n = plan[job]
                if n > 1:
                    pe.wait_ge(drained[b], n - 1)
                return psum[:, b, :]

            def done(ins, job):
                ins.then_inc(full[plan[job][0]], 1)

            def turn(job, src):
                d = fill(job)
                for k in range(src.shape[1] // P):
                    ins = pe.transpose(d[:, k * P:(k + 1) * P], src[:, k * P:(k + 1) * P], ident)
                done(ins, job)

            def product(job, pairs, n):
                d = fill(job)
                for i, (w, m) in enumerate(pairs):
                    ins = pe.matmul(d[:, 0:n], w, m, start=(i == 0), stop=(i == len(pairs) - 1))
                done(ins, job)

            def xt(c):
                pe.wait_ge(s_xn[0], c + 1)
                turn(("xt", c), xn[:, c, :])

            def project(c):
                emptied(pe, ("xt", c))
                for half, name in enumerate(("qk", "vg")):
                    d = fill((name, c))
                    for k in range(KT):
                        ins = pe.matmul(d, hT[:, c % 2, k, :], w_qkvg[:, k, half * 2 * D:(half + 1) * 2 * D],
                                        start=(k == 0), stop=(k == KT - 1))
                        if k == KT - 1:
                            done(ins, (name, c))
                        yield

            def weight_product(name, left, right):
                if name == "m":
                    pe.wait_ge(s_at, 64)
                for m in range(KT):
                    d = fill((name, m))
                    for k in range(KT):
                        ins = pe.matmul(d[:, 0:D], left[:, k, m * P:(m + 1) * P], right[:, k, :],
                                        start=(k == 0), stop=(k == KT - 1))
                        if k == KT - 1:
                            done(ins, (name, m))
                        yield

            def qkt(c):
                pe.wait_ge(s_qk, c + 1)
                turn(("qkt", c), qk[:, c % 2, :])

            def scores(c):
                for k in range(KT):
                    pe.wait_ge(s_qx[k], c + 1)
                for n in range(4):
                    k, h = n // 2, (n % 2) * 4
                    product(("p", c, n), [(qkT[:, c % 2, 2 + k, :], qx[:, k, h * P:(h + 4) * P])], 4 * P)

            def retain(c, others):
                w = DH + 1
                d = fill(("o", c))
                if c == 0:
                    pe.wait_ge(s_init, 3)
                for h in range(H):
                    if h % 4 == 0:
                        next(others)
                        emptied(pe, ("p", c, h // 4))
                    if h == 0:
                        pe.wait_ge(s_va, c + 1)
                    pe.matmul(d[:, h * w:(h + 1) * w], pT[:, h, :], va[:, c % 2, h * w:(h + 1) * w],
                              start=(h == 0), stop=False, skip_group_check=True)
                if c:
                    pe.wait_ge(s_state, c)
                for k in range(KT):
                    ins = pe.matmul(d[:, k * HT * w:(k + 1) * HT * w], qkT[:, c % 2, k, :], state[:, k, :],
                                    start=False, stop=(k == KT - 1), skip_group_check=True)
                done(ins, ("o", c))
                if c == C - 1:
                    return
                d = fill(("st", c))
                for k in range(KT):
                    ins = pe.matmul(d[:, k * HT * w:(k + 1) * HT * w], qk[:, c % 2, D + k * P:D + (k + 1) * P],
                                    va[:, c % 2, k * HT * w:(k + 1) * HT * w], start=True, stop=True)
                done(ins, ("st", c))

            def ot(c):
                pe.wait_ge(s_o3, c + 1)
                turn(("ot", c), o3[:, c % 2, :])

            def yproj(c):
                emptied(pe, ("ot", c))
                product(("y", c), [(oT[:, k, :], w_out[:, k, :]) for k in range(KT)], D)

            pe.wait_ge(s_cst, 16)
            xt(0)
            pe.wait_ge(s_qkvg, 16)
            for _ in project(0):
                pass
            qkt(0)
            xt(1)
            for _ in project(1):
                pass
            xt(2)
            for c in range(C):
                scores(c)
                if c + 1 < C:
                    qkt(c + 1)
                if c + 2 < C:
                    retain(c, project(c + 2))
                elif c == C - 2:
                    retain(c, weight_product("m", w_at[:, 0], w_at[:, 1]))
                else:
                    retain(c, weight_product("vo", w_at[:, 2], w_o))
                if c:
                    ot(c - 1)
                    if c == 1:
                        pe.wait_ge(s_outw, 16)
                    yproj(c - 1)
                if c + 3 < C:
                    xt(c + 3)

            pe.wait_ge(s_fc, 32)
            def features(name, phase, c):
                pe.wait_ge(s_xn[phase], c + 1)
                turn((name, c), xn[:, c, :])

            def group(g):
                return slice(g * GW, (g + 1) * GW)

            for c in range(GC):
                features("bt", 1, c)
            for g in range(G):
                for c in (GC * g + GC - 2, GC * g + GC - 1):
                    emptied(pe, ("bt", c))
                for m in range(FM):
                    product(("fc1", g, m), [(w_fc1[:, k, m * P:(m + 1) * P], featT[:, k, group(g)])
                                            for k in range(KT)], GW)
                    if (g, m) == (0, 1):
                        ot(C - 1)
                    if (g, m) == (0, 2):
                        yproj(C - 1)
                    if g == 0 and m >= FM - GC:
                        features("bt", 1, GC + m - (FM - GC))
            pe.wait_ge(s_bfly, 1)
            for n in range(4):
                product(("wd", n), [(had, wdB[:, 2 * n:2 * n + 2, :].rearrange("p a n -> p (a n)"))], 512)
            for c in range(C):
                for m in (FM - 2, FM - 1):
                    emptied(pe, ("fc1", c // GC, m))
                product(("fc2", c), [(hidT[:, m, c * P:(c + 1) * P], w_fc2[:, m, :]) for m in range(FM)], D)
                if c >= AHEAD:
                    features("ct", 2, c - AHEAD)
            if nphase < 3:
                return
            def hadamard(g):
                for c in (GC * g + GC - 2, GC * g + GC - 1):
                    emptied(pe, ("ct", c))
                for m in range(KT):
                    product(("had", g, m), [(had, featT[:, 0, group(g)]),
                                            (had if m == 0 else hadneg, featT[:, 1, group(g)])], GW)

            pe.wait_ge(s_ug, 16)
            hadamard(0)
            for g in range(G):
                for m in range(FM):
                    if g == 0 and m < AHEAD:
                        features("ct", 2, C - AHEAD + m)
                    if m == 0:
                        for k in range(KT):
                            emptied(pe, ("had", g, k))
                    for name, at in (("gate", F), ("up", 0)):
                        product((name, g, m), [(w_ug[:, k, at + m * P:at + (m + 1) * P], uT[:, k, group(g)])
                                               for k in range(KT)], GW)
                    if g == 0 and m == FM - 2:
                        hadamard(1)
            for c in range(C):
                for m in (FM - 2, FM - 1):
                    emptied(pe, ("up", c // GC, m))
                if c == 0:
                    for n in range(4):
                        emptied(pe, ("wd", n))
                product(("down", c), [(hidT[:, m, c * P:(c + 1) * P], w_down[:, m, :]) for m in range(FM)], D)
                if c >= AHEAD:
                    features("dt", 3, c - AHEAD)
            if nphase < 4:
                return
            def queries(g):
                for c in range(GC * g, GC * g + GC):
                    emptied(pe, ("dt", c))
                for m in range(KT):
                    product(("qm", g, m), [(w_m[:, k, m * P:(m + 1) * P], featT[:, k, group(g)])
                                           for k in range(KT)], GW)

            def values(c):
                product(("v", c), [(featT[:, k, c * P:(c + 1) * P], w_vo[:, k, :]) for k in range(KT)], D)

            def att_scores(c):
                if c % GC == 0:
                    for m in range(KT):
                        emptied(pe, ("qm", c // GC, m))
                for b in range(c // GC + 1):
                    n = min(GW, (c + 1) * P - b * GW)
                    product(("sc", c, b), [(qT[:, k, c * P:(c + 1) * P], featT[:, k, b * GW:b * GW + n])
                                           for k in range(KT)], n)

            def prob_turn(c):
                for b in range(c // GC + 1):
                    emptied(pe, ("sc", c, b))
                    n = min(GW, (c + 1) * P - b * GW)
                    turn(("pt", c, b), prob[:, score_banks(c)[b], 0:n])

            def att_out(c):
                for b in range(c // GC + 1):
                    emptied(pe, ("pt", c, b))
                if c % GC == 0:
                    for cc in range(c, c + GC):
                        emptied(pe, ("v", cc))
                product(("pv", c), [(probT[:, turned(c) + j, :], v[:, j, :]) for j in range(c + 1)], D)

            def zt(c):
                pe.wait_ge(s_xn[4], c + 1)
                turn(("zt", c), xn[:, c, :])

            def logits(c):
                emptied(pe, ("zt", c))
                product(("lg", c), [(zT[:, k, :], w_r[:, k, :]) for k in range(KT)], E)

            queries(0)
            features("dt", 3, C - 3)
            for c in range(GC):
                values(c)
            features("dt", 3, C - 2)
            features("dt", 3, C - 1)
            att_scores(0)
            att_scores(1)
            queries(1)
            for c in range(C):
                prob_turn(c)
                if c + 2 < C:
                    att_scores(c + 2)
                if c < GC:
                    values(c + GC)
                if c:
                    zt(c - 1)
                att_out(c)
                if c:
                    if c == 1:
                        pe.wait_ge(s_o, 16)
                    logits(c - 1)
            zt(C - 1)
            logits(C - 1)
            if nphase < 5:
                return
            pe.wait_ge(s_oh, 1)
            d = fill(("rank",))
            pe.matmul(d[:, 0:C * E], strict, oh[:, 2, :], start=True, stop=True)
            done(pe.matmul(d[:, C * E:2 * C * E], ones, oh[:, 2, :], start=True, stop=True), ("rank",))

            d = fill(("map",))
            for a in range(2 * C):
                if a % 4 == 0:
                    pe.wait_ge(s_map, a // 4 + 1)
                ins = pe.matmul(d[:, 0:2 * TILES], onerow[:, a, :], idpair[:, a].rearrange("p b n -> p (b n)"),
                                start=(a == 0), stop=(a == 2 * C - 1))
            done(ins, ("map",))
            for b in range(8):
                pe.wait_ge(drained[b], fills[b])
            pe.wait_ge(s_te, 1)
            for n in range(2):
                pe.wait_ge(s_exp[n], 16 * (E // 2))

            def expert(t):
                return pe.value_load(texp_i[0:1, bass.ds(t, 1)], min_val=0, max_val=(E - 1) * EW)

            def tile_turn(t, u, loads):
                par, n = u % 2, u % LOADS
                pe.wait_ge(s_ld[n], loads)
                for k in range(KT):
                    ins = pe.transpose(psum[:, par, k * P:(k + 1) * P], mx[:, n, k * P:(k + 1) * P], ident)
                ins.then_inc(s_txf, 1)

            def tile_up(t, par, at):
                pe.wait_ge(s_txd, t + 1)
                for k in range(KT):
                    ins = pe.matmul(psum[:, 2 + par, :], mxT[:, par, k * P:(k + 1) * P],
                                    experts[:, bass.ds(at + k * FE, FE)], start=(k == 0), stop=(k == KT - 1))
                ins.then_inc(s_hf, 1)

            def tile_hT(t, par):
                pe.wait_ge(s_hd, t + 1)
                if not (isinstance(t, int) and t < 2):
                    pe.wait_ge(s_thd, t - 1)
                for m in range(FEM):
                    ins = pe.transpose(psum[:, 4 + par, m * P:(m + 1) * P], mh[:, par, m * P:(m + 1) * P], ident)
                ins.then_inc(s_thf, 1)

            def tile_down(t, par, at):
                pe.wait_ge(s_thd, t + 1)
                if not (isinstance(t, int) and t < 2):
                    pe.wait_ge(s_yd, t - 1)
                for m in range(FEM):
                    ins = pe.matmul(psum[:, 6 + par, 0:D], mhT[:, par, m * P:(m + 1) * P],
                                    experts[:, bass.ds(at + KT * FE + m * D, D)], start=(m == 0), stop=(m == FEM - 1))
                ins.then_inc(s_yf, 1)

            def step(t, u, loads):
                par = u % 2
                tile_hT(t, par)
                tile_up(t + 1, 1 - par, expert(t + 1))
                tile_down(t, par, expert(t))
                if loads is not None:
                    tile_turn(t + 2, u + 2, loads)

            def load_count(t):
                return (t // LOADS + 1) * 16

            tile_turn(0, 0, 16)
            tile_up(0, 0, expert(0))
            tile_turn(1, 1, 16)
            for t in range(HEAD):
                step(t, t, load_count(t + 2))
            with pe.Fori(HEAD, LOOPED, LOADS) as t:
                for n in range(HEAD, HEAD + LOADS):
                    step(t + (n - HEAD), n, t * (16 // LOADS) + (load_count(n + 2) - HEAD * 16 // LOADS))
            for t in range(LOOPED, TILES - 1):
                step(t, t, load_count(t + 2) if t + 2 < TILES else None)
            tile_hT(TILES - 1, 0)
            tile_down(TILES - 1, 0, expert(TILES - 1))

        @block.vector
        def _(dve):
            steps = [0]

            def link(ins):
                steps[0] += 1
                ins.then_inc(s_dv, 1)
                dve.wait_ge(s_dv, steps[0])

            def wide(ap, n):
                return ap.unsqueeze(2).to_broadcast([P, ap.shape[1], n])

            def over(ap, n):
                return ap.unsqueeze(1).to_broadcast([P, n, ap.shape[1]])

            def stats(c):
                link(dve.bn_stats(bn[:, c % 2, :], x[:, c, :]))
                dve.bn_aggr(raw[:, c, :], bn[:, c % 2, :]).then_inc(s_stat, 1)

            def rotate(c):
                if c:
                    dve.wait_ge(s_qk, c)
                q = filled(dve, ("qk", c)).rearrange("p (h d) -> p h d", d=DH)
                dve.tensor_tensor(rotc.rearrange("p (h d) -> p h d", d=DH), q, over(cos[:, c, :], 2 * H), ALU.mult)
                q2 = q.rearrange("p h (i two) -> p h i two", two=2)
                r2 = rots.rearrange("p (h i two) -> p h i two", two=2, i=DH // 2)
                s2 = sin[:, c, :].rearrange("p (i two) -> p i two", two=2)
                for side in range(2):
                    ins = dve.tensor_tensor(r2[:, :, :, side], q2[:, :, :, 1 - side],
                                            over(s2[:, :, side], 2 * H), ALU.mult)
                ins.then_inc(drained[plan[("qk", c)][0]], 1)

            def values(c):
                if c >= 2:
                    filled(dve, ("st", c - 2))
                src = filled(dve, ("vg", c))[:, 0:D].rearrange("p (h d) -> p h d", d=DH)
                dst = va[:, c % 2, :].rearrange("p (h e) -> p h e", e=DH + 1)[:, :, 0:DH]
                dve.tensor_tensor(dst, src, wide(growth, DH), ALU.mult).then_inc(s_va, 1)

            def causal(c):
                if c:
                    filled(dve, ("o", c - 1))
                for n in range(4):
                    src = filled(dve, ("p", c, n)).rearrange("p (h s) -> p h s", s=P)
                    dve.tensor_tensor(pT[:, 4 * n:4 * n + 4, :], src, over(tril, 4), ALU.mult
                                      ).then_inc(drained[plan[("p", c, n)][0]], 1)

            def spread(c):
                emptied(dve, ("qkt", c))
                dve.tensor_tensor(qx[:, 0, :].rearrange("p (h s) -> p h s", s=P), over(qkT[:, c % 2, 0, :], HT),
                                  wide(headmask, P), ALU.mult).then_inc(s_qx[0], 1)

            def inner_residual(c):
                dve.wait_ge(s_y, c + 1)
                dve.tensor_tensor(x1i[:, c, :], y[:, c, :], filled(dve, ("y", c))[:, 0:D], ALU.add
                                  ).then_inc(drained[plan[("y", c)][0]], 1)

            def update_state(c):
                n = KT * HT * (DH + 1)
                src = filled(dve, ("st", c))[:, 0:n]
                flat = statetmp.rearrange("p k n -> p (k n)")
                dve.tensor_tensor(flat, src, stateblock, ALU.mult).then_inc(drained[plan[("st", c)][0]], 1)
                emptied(dve, ("st", c))
                for k in range(KT):
                    ins = dve.scalar_tensor_tensor(state[:, k, :], state[:, k, :], statedecay[:, k:k + 1],
                                                   statetmp[:, k, :], ALU.mult, ALU.add)
                ins.then_inc(s_state, 1)

            def weigh(c):
                d = filled(dve, ("o", c))[:, 0:H * (DH + 1)].rearrange("p (h e) -> p h e", e=DH + 1)
                link(dve.tensor_tensor(den, d[:, :, DH], rowscale[:, c, :], ALU.mult))
                link(dve.scalar_tensor_tensor(den, den, -1.0, den, ALU.mult, ALU.max))
                link(dve.tensor_scalar(den, den, 1.0, None, ALU.max))
                link(dve.reciprocal(rden, den))
                link(dve.tensor_tensor(wrow, rden, rowscale[:, c, :], ALU.mult))
                dve.tensor_tensor(o1.rearrange("p (h d) -> p h d", d=DH), d[:, :, 0:DH], wide(wrow, DH), ALU.mult
                                  ).then_inc(drained[plan[("o", c)][0]], 1)
                emptied(dve, ("o", c))
                link(dve.tensor_tensor(osq, o1, o1, ALU.mult))
                if c:
                    dve.wait_ge(s_ors, c)
                dve.tensor_reduce(oss, osq.rearrange("p (h d) -> p h d", d=DH), AX.X, ALU.add).then_inc(s_oss, 1)

            def gated(c):
                dve.wait_ge(s_ors, c + 1)
                link(dve.tensor_tensor(o2.rearrange("p (h d) -> p h d", d=DH),
                                       o1.rearrange("p (h d) -> p h d", d=DH), wide(ors, DH), ALU.mult))
                emptied(dve, ("vg", c))
                dve.tensor_tensor(o3[:, c % 2, :], o2, sg[:, c % 3, :], ALU.mult).then_inc(s_o3, 1)

            for c in range(C):
                if c % 2 == 0:
                    dve.wait_ge(s_x[c // 2], 16)
                stats(c)
            dve.wait_ge(s_vec, 16)
            dve.wait_ge(s_cst, 16)
            dve.scalar_tensor_tensor(scup[:], vector("scale_up"), D ** -0.5, vector("su_dp"), ALU.mult, ALU.mult
                                     ).then_inc(s_par, 1)
            dve.tensor_scalar(scpar[:], vector("scale_gate"), D ** -0.5, None, ALU.mult).then_inc(s_par, 1)
            for c in range(2):
                rotate(c)
                values(c)
                if c == 0:
                    spread(0)
            for c in range(C):
                if c:
                    weigh(c - 1)
                causal(c)
                if c:
                    update_state(c - 1)
                    gated(c - 1)
                if c + 1 < C:
                    spread(c + 1)
                if c + 2 < C:
                    rotate(c + 2)
                    values(c + 2)
                if c:
                    inner_residual(c - 1)
            weigh(C - 1)
            gated(C - 1)
            inner_residual(C - 1)
            for n in range(4):
                src = filled(dve, ("wd", n)).rearrange("p (a n) -> p a n", n=D)
                dve.scalar_tensor_tensor(w_down[:, 2 * n:2 * n + 2, :], src, F ** -0.5, over(vector("scale_dp"), 2),
                                         ALU.mult, ALU.mult).then_inc(drained[plan[("wd", n)][0]], 1)

            def add_residual(job, c):
                dve.tensor_tensor(x[:, c, :], x[:, c, :], filled(dve, job)[:, 0:D], ALU.add
                                  ).then_inc(drained[plan[job][0]], 1)
                emptied(dve, job)
                stats(c)

            for c in range(C):
                dve.wait_ge(s_xr[0], c + 1)
                add_residual(("fc2", c), c)
            if nphase < 3:
                return
            for g in range(G):
                for m in range(FM):
                    emptied(dve, ("gate", g, m))
                    dve.scalar_tensor_tensor(hidT[:, m, g * GW:(g + 1) * GW], filled(dve, ("up", g, m)),
                                             scup[:, m:m + 1], silu_g[:, m % 2, :], ALU.mult, ALU.mult
                                             ).then_inc(drained[plan[("up", g, m)][0]], 1)
            for c in range(C):
                add_residual(("down", c), c)
            if nphase < 4:
                return

            def row_max(c):
                for b in range(c // GC + 1):
                    filled(dve, ("sc", c, b))
                banks = score_banks(c)
                flat = psum[:, banks[0]:banks[-1] + 1, :].rearrange("p b n -> p (b n)")
                diag = flat[:, c * P:(c + 1) * P]
                link(dve.tensor_tensor(diag, diag, below, ALU.add))
                link(dve.tensor_reduce(rmaxp[:, c:c + 1], flat[:, 0:(c + 1) * P], AX.X, ALU.max))
                dve.tensor_scalar(rmax[:, c:c + 1], rmaxp[:, c:c + 1], -1.0, None, ALU.mult
                                  ).then_inc(s_mx, 1)

            def probs_out(c):
                for b in range(c // GC + 1):
                    n = min(GW, (c + 1) * P - b * GW)
                    at = turned(c) + b * GC
                    dst = probT[:, at:at + n // P, :].rearrange("p j n -> p (j n)")
                    dve.tensor_copy(dst, filled(dve, ("pt", c, b))[:, 0:n]).then_inc(drained[plan[("pt", c, b)][0]], 1)

            def attended(c):
                col = slice(c, c + 1)
                if c >= GC:
                    link(dve.tensor_tensor(rsum[:, c, 0:1], rsum[:, c, 0:1], rsum[:, c, 1:2], ALU.add))
                link(dve.reciprocal(rinv[:, col], rsum[:, c, 0:1]))
                dve.wait_ge(s_xr[1], c + 1)
                job = ("pv", c)
                dve.scalar_tensor_tensor(x[:, c, :], filled(dve, job)[:, 0:D], rinv[:, col], x[:, c, :],
                                         ALU.mult, ALU.add).then_inc(drained[plan[job][0]], 1)
                emptied(dve, job)
                stats(c)

            def choose(c):
                job = ("lg", c)
                if c == 0:
                    dve.wait_ge(s_xr[1], C)
                dve.tensor_copy(lgs[:, c, :], filled(dve, job)[:, 0:E]).then_inc(drained[plan[job][0]], 1)
                emptied(dve, job)
                link(dve.max(top[:, c, :], lgs[:, c, :]))
                link(dve.max_index(topi[:, c, :], top[:, c, :], lgs[:, c, :]))
                link(dve.tensor_copy(topf[:, c, :], topi[:, c, 0:2]))
                for k in range(2):
                    link(dve.tensor_scalar(oh[:, k, c * E:(c + 1) * E], const("iota")[:, 0:E], topf[:, c, k:k + 1], None,
                                           ALU.is_equal))

            row_max(0)
            row_max(1)
            for c in range(C):
                probs_out(c)
                if c + 2 < C:
                    row_max(c + 2)
                attended(c)
                if c:
                    choose(c - 1)
            choose(C - 1)
            dve.tensor_tensor(oh[:, 2, :], oh[:, 0, :], oh[:, 1, :], ALU.add).then_inc(s_oh, 1)
            dve.tensor_tensor(dv8[:], top[:, :, 1], top[:, :, 0], ALU.subtract).then_inc(s_gap, 1)
            if nphase < 5:
                return
            dve.wait_ge(s_e8, 1)
            link(dve.tensor_scalar(p12[:, 1, :], ex8[:], 1.0, None, ALU.add))
            link(dve.reciprocal(p12[:, 0, :], p12[:, 1, :]))
            link(dve.tensor_tensor(p12[:, 1, :], ex8[:], p12[:, 0, :], ALU.mult))
            n = C * E
            job = ("rank",)
            src = filled(dve, job)
            link(dve.tensor_copy(tot[:, 0, :], src[:, n:2 * n]))
            dve.tensor_tensor(within, src[:, 0:n], tot[:, 0, :], ALU.subtract).then_inc(drained[plan[job][0]], 1)
            emptied(dve, job)
            for i, sh in enumerate((E, 2 * E, 4 * E)):
                a, b = tot[:, i % 2, :], tot[:, 1 - i % 2, :]
                dve.tensor_copy(b[:, 0:sh], a[:, 0:sh])
                link(dve.tensor_tensor(b[:, sh:n], a[:, sh:n], a[:, 0:n - sh], ALU.add))
            upto_c = tot[:, 1, :]
            count = tot[:, 1, n - E:n]
            link(dve.tensor_scalar(ntile_i[:], count, float(P - 1), None, ALU.add))
            link(dve.tensor_scalar(ntile_i[:], ntile_i[:], 7, None, ALU.logical_shift_right))
            link(dve.tensor_copy(ntile[:], ntile_i[:]))
            link(dve.tensor_copy(ends[:, 0, :], ntile[:]))
            for i, sh in enumerate((1, 2, 4, 8)):
                a, b = ends[:, i % 2, :], ends[:, 1 - i % 2, :]
                dve.tensor_copy(b[:, 0:sh], a[:, 0:sh])
                link(dve.tensor_tensor(b[:, sh:E], a[:, sh:E], a[:, 0:E - sh], ALU.add))
            last = ends[:, 0, :]
            link(dve.tensor_tensor(base[:], last, ntile[:], ALU.subtract))
            link(dve.tensor_tensor(posn, within, upto_c, ALU.add))
            link(dve.tensor_scalar(base[:], base[:], float(P), None, ALU.mult))
            pv_ = posn.rearrange("p (c e) -> p c e", e=E)
            link(dve.tensor_tensor(pv_, pv_, over(base[:], C), ALU.add))
            for k in range(2):
                link(dve.tensor_tensor(pick[:, k, :], posn, oh[:, k, :], ALU.mult))
                link(dve.tensor_reduce(slotf[:, k * C:(k + 1) * C], pick[:, k, :].rearrange("p (c e) -> p c e", e=E),
                                       AX.X, ALU.add))
            link(dve.tensor_copy(slot_i[:, 0, :], slotf[:]))
            dve.tensor_scalar(slot_i[:, 1, :], slot_i[:, 0, :], P - 1, None, ALU.bitwise_and)
            link(dve.tensor_scalar(slot_i[:, 2, :], slot_i[:, 0, :], 7, None, ALU.logical_shift_right))
            dve.tensor_copy(rowf[:], slot_i[:, 1, :])
            link(dve.tensor_copy(tilef[:], slot_i[:, 2, :]))
            link(dve.tensor_tensor(onetile, over(const("tileno"), 2 * C), wide(tilef[:], TILES), ALU.is_equal))
            for k in range(2):
                dve.tensor_tensor(idpair[:, k * C:(k + 1) * C, 0, :], onetile[:, k * C:(k + 1) * C, :],
                                  wide(const("token1"), TILES), ALU.mult)
            dve.tensor_tensor(idpair[:, :, 1, :], onetile, wide(p12[:].rearrange("p k c -> p (k c)"), TILES), ALU.mult)
            for n in range(4):
                dve.tensor_tensor(onerow[:, 4 * n:4 * n + 4, :], over(const("iota"), 4),
                                  wide(rowf[:, 4 * n:4 * n + 4], P), ALU.is_equal).then_inc(s_map, 1)
            tc = tcmp.rearrange("p (t e) -> p t e", e=E)
            link(dve.tensor_tensor(tc, over(last, TILES), wide(const("tileno"), E), ALU.is_le))
            link(dve.tensor_reduce(texp, tc, AX.X, ALU.add))
            dve.tensor_scalar(texp_i, texp, float(E - 1), float(EW), ALU.min, ALU.mult).then_inc(s_te, 1)
            job = ("map",)
            src = filled(dve, job)
            dve.tensor_copy(weight, src[:, TILES:2 * TILES])
            dve.tensor_copy(id1, src[:, 0:TILES]).then_inc(drained[plan[job][0]], 1)
            emptied(dve, job)
            link(dve.tensor_scalar(source, id1, -1.0, 0.0, ALU.add, ALU.max))
            for t in range(LOADS):
                dve.tensor_copy(source_t[:, t:t + 1], source[:, t:t + 1]).then_inc(s_src, 1)
            link(dve.tensor_scalar(idtmp, id1, 0.0, const("spare"), ALU.is_equal, ALU.mult))
            link(dve.scalar_tensor_tensor(target, idtmp, -1.0, id1, ALU.add, ALU.add))

            def step(t, u, last=False):
                par, n = u % 2, u % LOADS
                dve.wait_ge(s_thf, t + 1)
                dve.tensor_copy(mhT[:, par, :], psum[:, 4 + par, :]).then_inc(s_thd, 1)
                if not last:
                    dve.tensor_copy(source_t[:, n:n + 1], source_span[:, bass.ds(t + LOADS, 1)]).then_inc(s_src, 1)
                if not (isinstance(t, int) and t < 2):
                    dve.wait_ge(s_add, t * 16 - 16)
                dve.tensor_copy(target_t[:, par:par + 1], target[:, bass.ds(t, 1)])
                dve.wait_ge(s_yf, t + 1)
                dve.tensor_scalar(my[:, par, :], psum[:, 6 + par, 0:D], weight[:, bass.ds(t, 1)], None, ALU.mult
                                  ).then_inc(s_yd, 1)

            for t in range(HEAD):
                step(t, t)
            with dve.Fori(HEAD, LOOPED, LOADS) as t:
                for n in range(HEAD, HEAD + LOADS):
                    step(t + (n - HEAD), n)
            for t in range(LOOPED, TILES):
                step(t, t, last=t + LOADS >= TILES)



def kernel(upto=9, **inputs):
    import numpy as _np
    import concourse.bacc as _bacc
    from concourse import mybir as _mybir
    from concourse.bass_utils import run_bass_kernel_spmd as _run

    a = {k: _np.asarray(v) for k, v in inputs.items()}

    def rows(w):
        return _np.ascontiguousarray(w.reshape(-1, P, w.shape[-1]).transpose(1, 0, 2))

    def column(vec):
        return vec.reshape(-1, P).T

    def spread_row(vec):
        return _np.broadcast_to(vec[None, :], (P, vec.shape[0]))

    qkv = a["L1_attn_qkv"]
    su_ug, ws_ug = a["L0_ffn_SU_ug"], a["L0_ffn_Wscale_ug"]
    vectors = _np.concatenate([
        column(a["L0_attn_retn_norm_w"]), column(a["L0_attn_final_norm_w"]), column(a["L0_attn_fc1_b"]),
        column(su_ug), column(ws_ug[:F]), column(ws_ug[F:]), column(a["L0_ffn_SU_dp"]),
        column(a["L1_attn_gamma"]), column(a["L1_attn_beta"]), spread_row(a["L0_attn_fc2_b"]),
        spread_row(a["L0_ffn_Wscale_dp"])], axis=1)
    arrays = {
        "x_in": a["L0_attn_x"].reshape(T, D),
        "const_in": constants(),
        "vec_in": vectors,
        "qkvg_in": rows(_np.concatenate([a["L0_attn_q_w"], a["L0_attn_k_w"], a["L0_attn_v_w"], a["L0_attn_g_w"]], axis=1)),
        "out_w_in": rows(a["L0_attn_out_w"]),
        "fc1_in": rows(a["L0_attn_fc1_w"]),
        "fc2_in": rows(a["L0_attn_fc2_w"]),
        "upgate_in": rows(_np.concatenate([a["L0_ffn_W_up"].T, a["L0_ffn_W_gate"].T], axis=1)),
        "down_in": rows(a["L0_ffn_W_down"].T),
        "wqt_in": rows(qkv[:, :D].T),
        "wkt_in": rows(qkv[:, D:2 * D].T),
        "wvt_in": rows(qkv[:, 2 * D:].T),
        "o_in": rows(a["L1_attn_o_proj"]),
        "router_in": rows(a["L1_ffn_router_w"]),
        "experts_in": _np.concatenate([
            a["L1_ffn_W1"].reshape(E, KT, P, FE).transpose(0, 2, 1, 3).reshape(E, P, KT * FE),
            a["L1_ffn_W2"].reshape(E, FEM, P, D).transpose(0, 2, 1, 3).reshape(E, P, FEM * D)], axis=2),
    }
    nc = _bacc.Bacc("TRN2", target_bir_lowering=False, num_devices=1)
    arrays = {k: _np.ascontiguousarray(v) for k, v in arrays.items()}
    args = {k: nc.dram_tensor(k, v.shape, _mybir.dt.from_np(v.dtype), kind="ExternalInput").ap()
            for k, v in arrays.items()}
    out = nc.dram_tensor("out", (T + P, D), F32, kind="ExternalOutput").ap()
    build(nc, out=out, upto=upto, **args)
    r = _run(nc, [arrays], core_ids=[0])
    return r.results[0]["out"][:T].reshape(1, T, D)
```

```python
from contextlib import ExitStack

import numpy as np

import concourse.bass as bass
from concourse import mybir

F32 = mybir.dt.float32
F32R = mybir.dt.float32r
BF16 = mybir.dt.bfloat16
I32 = mybir.dt.int32
U32 = mybir.dt.uint32
ALU = mybir.AluOpType
ACT = mybir.ActivationFunctionType
AX = mybir.AxisListType

P = 128
T, D = 1024, 256
C = T // P
KT = D // P
H, DH = 16, 16
HT = H // KT
F = 1024
FM = F // P
GC = 4
G = C // GC
GW = GC * P
E, FE = 16, 512
FEM = FE // P
EW = KT * FE + FEM * D
TILES = (2 * T) // P + E - 1
WHOLE = 2
AHEAD = 2
LOADS = 4
HEAD = 2
LOOPED = HEAD + (TILES - LOADS - HEAD) // LOADS * LOADS
TURNS = {1: GC, 3: GC + 1, 5: GC + 2, 6: GC + 3}
LAST_TURN = max(TURNS)
EPS = 1e-5
NEG = -3.0e38


def constant_columns():
    widths = [("ident", P), ("tril", P), ("below", P), ("had", P), ("hadneg", P), ("strict", P),
              ("ones", P), ("headmask", HT), ("cos", C * DH), ("sin", C * DH), ("growth", H),
              ("rowscale", C * H), ("stateblock", KT * HT * (DH + 1)), ("statedecay", KT),
              ("iota", P), ("tileno", TILES),
              ("row1", 1), ("chunk_at", 2 * C), ("spare", 1)]
    at, out = 0, {}
    for name, w in widths:
        out[name] = (at, w)
        at += w
    return out, at

def constants():
    cols, n = constant_columns()
    out = np.zeros((P, n), np.float32)

    def put(name, a):
        at, w = cols[name]
        out[:, at:at + w] = np.asarray(a, np.float64).reshape(P, w).astype(np.float32)

    i = np.arange(P)
    put("ident", np.eye(P))
    put("tril", i[:, None] <= i[None, :])
    put("below", np.where(i[None, :] > i[:, None], NEG, 0.0))
    bits = np.array([[bin(a & b).count("1") for b in range(P)] for a in range(P)])
    put("had", (-1.0) ** bits)
    put("hadneg", -((-1.0) ** bits))
    put("strict", i[:, None] < i[None, :])
    put("ones", np.ones((P, P)))
    put("headmask", i[:, None] // DH == np.arange(HT)[None, :])
    angle = (np.float32(1.0) / np.float32(10000.0) ** np.linspace(0, 1, DH // 2, dtype=np.float32)).astype(np.float32)
    angle = np.repeat(angle, 2)
    phase = (np.arange(T, dtype=np.float32)[:, None] * angle[None, :]).astype(np.float32)
    sign = np.where(np.arange(DH) % 2 == 0, -1.0, 1.0)
    put("cos", np.cos(phase.astype(np.float64)).reshape(C, P, DH).transpose(1, 0, 2))
    put("sin", (np.sin(phase.astype(np.float64)) * sign).reshape(C, P, DH).transpose(1, 0, 2))
    gamma = 1.0 - 2.0 ** (-5.0 - np.arange(H))
    put("growth", gamma[None, :] ** (-i[:, None].astype(np.float64)))
    tok = np.arange(T, dtype=np.float64)[:, None]
    rows = (1.0 - gamma[None, :] ** (tok + 1)) / (1.0 - gamma[None, :])
    scale = gamma[None, :] ** (tok % P) / np.sqrt(rows) * DH ** -0.5
    put("rowscale", scale.reshape(C, P, H).transpose(1, 0, 2))
    block = np.zeros((P, KT, HT, DH + 1))
    decay = np.zeros((P, KT))
    for k in range(KT):
        for p in range(P):
            g = gamma[k * HT + p // DH] ** P
            block[p, k, p // DH, :] = g
            decay[p, k] = g
    put("stateblock", block)
    put("statedecay", decay)
    put("iota", np.tile(np.arange(P), (P, 1)))
    put("tileno", np.tile(np.arange(TILES), (P, 1)))
    put("row1", i[:, None] + 1)
    put("chunk_at", np.tile(np.arange(C) * P, (P, 2)))
    put("spare", T + 1 + i[:, None])
    return out

def vector_columns():
    widths = [("retn_w", KT), ("final_w", KT), ("fc1_b", FM), ("su_ug", KT), ("scale_up", FM),
              ("scale_gate", FM), ("su_dp", FM), ("gamma", KT), ("beta", KT), ("fc2_b", D), ("scale_dp", D)]
    at, out = 0, {}
    for name, w in widths:
        out[name] = (at, w)
        at += w
    return out, at


def score_banks(c):
    return [c] if c < GC else [2 * (c % 2), 2 * (c % 2) + 1]

def turn_bank(c, b):
    return 4 + (c % 2 if c < GC else b)

def psum_plan():
    order = []

    def job(bank, *name):
        order.append((name, bank))

    def project(c):
        job(0, "qk", c)
        job(1, "vg", c)

    job(2, "xt", 0)
    project(0)
    job(2, "xt", 1)
    job(2, "qkt", 0)
    project(1)
    job(2, "xt", 2)
    for c in range(C):
        for n in range(4):
            job((3, 4, 7, 1)[n], "p", c, n)
        if c + 1 < C:
            job(2, "qkt", c + 1)
        job(5, "o", c)
        if c + 2 < C:
            project(c + 2)
        else:
            for m in range(KT):
                job(m, ("m", "vo")[c + 2 - C], m)
        if c + 1 < C:
            job(6, "st", c)
        if c:
            job(7, "ot", c - 1)
            job(7, "y", c - 1)
        if c + 3 < C:
            job(2, "xt", c + 3)
        elif c < C - 1:
            job(2, "bt", c + 3 - C)
        else:
            job(2, "bt", 2)
            job(6, "bt", 3)
    job(4, "wd", 0)
    for g in range(G):
        for m in range(FM):
            job(2 + m % 2, "fc1", g, m)
            if (g, m) == (0, 2):
                job(5, "wd", 1)
                job(7, "ot", C - 1)
            if (g, m) == (0, 3):
                job(7, "y", C - 1)
            if g == 0 and m in TURNS:
                job(TURNS[m] % 2, "bt", TURNS[m])
    for n in (2, 3):
        job(4 + n, "wd", n)
    for c in range(C):
        job(4 + c % 2, "fc2", c)
        if c >= AHEAD:
            job(c % 2, "ct", c - AHEAD)
        if c == C - 2:
            for m in range(KT):
                job(6 + m, "had", 0, m)
    for g in range(G):
        for m in range(FM):
            if g == 0 and m < AHEAD:
                job(m % 2, "ct", C - AHEAD + m)
            job(2 + m % 2, "gate", g, m)
            job(4 + m % 2, "up", g, m)
            if g == 0 and m == FM - 2:
                for k in range(KT):
                    job(6 + k, "had", 1, k)
    for c in range(C):
        job(6 + c % 2, "down", c)
        if c >= AHEAD:
            job(c % 2, "dt", c - AHEAD)
    for m in range(KT):
        job(2 + m, "qm", 0, m)
    for c in range(GC):
        job(4 + c % 2, "v", c)
    job(6, "dt", C - 2)
    job(7, "dt", C - 1)

    def scores(c):
        for b in range(c // GC + 1):
            job(score_banks(c)[b], "sc", c, b)

    scores(0)
    scores(1)
    for m in range(KT):
        job(2 + m, "qm", 1, m)
    for c in range(C):
        for b in range(c // GC + 1):
            job(turn_bank(c, b), "pt", c, b)
        if c >= 2:
            job(7, "lg", c - 2)
        if c + 2 < C:
            scores(c + 2)
        if c < GC:
            job(7, "v", c + GC)
        job(6, "pv", c)
        if c:
            job(7, "zt", c - 1)
    job(7, "lg", C - 2)
    job(7, "zt", C - 1)
    job(7, "lg", C - 1)
    job(0, "rank")
    job(1, "map")
    job(7, "weights")
    fills, plan = [0] * 8, {}
    for name, bank in order:
        fills[bank] += 1
        plan[name] = (bank, fills[bank])
    return plan, fills

def build(nc, x_in, const_in, vec_in, qkvg_in, out_w_in, fc1_in, fc2_in, upgate_in, down_in, wqt_in, wkt_in,
          wvt_in, o_in, router_in, experts_in, out):
    ccol, cn = constant_columns()
    vcol, vn = vector_columns()
    plan, fills = psum_plan()

    shared = {"cst": (cn,), "featT": (KT, T), "experts": (E * EW,), "ffw": (2 * KT * F,), "attn": (3 * T,)}
    in_experts = {"hid_lo": FM * T, "ug_lo": 2 * KT * F, "ug_hi": 2 * KT * F,
                  "hid_hi": FM * T, "fc_hi": 2 * KT * F, "u_hi": KT * T, "down_hi": FM * D}
    assert sum(in_experts.values()) == E * EW
    with ExitStack() as rounded_ctx:
        def rounded_name(name, *shape):
            return rounded_ctx.enter_context(nc.sbuf_tensor(name + "_rounded", [P, *shape], F32R))

        rounded = {}
        for name, shape in shared.items():
            if name == "experts":
                for part, n in in_experts.items():
                    rounded[part] = rounded_name(part, n)
            else:
                rounded[name] = rounded_name(name, *shape)

    with ExitStack() as ctx:
        plain = {name: ctx.enter_context(nc.sbuf_tensor(name, [P, *shape], F32)) for name, shape in shared.items()}

        def sb(name, *shape, dt=F32):
            if name in plain:
                return plain[name]
            return ctx.enter_context(nc.sbuf_tensor(name, [P, *shape], dt))

        def sem(name):
            return ctx.enter_context(nc.semaphore(name))

        cst = sb("cst", cn)
        vec = sb("vec", vn)

        def const(name, *dims):
            at, w = ccol[name]
            return cst[:, at:at + w]

        def vector(name):
            at, w = vcol[name]
            return vec[:, at:at + w]

        ident, tril, below = const("ident"), const("tril"), const("below")
        had, hadneg, strict, ones = const("had"), const("hadneg"), const("strict"), const("ones")
        had_r, hadneg_r = (rounded["cst"][:, ccol[name][0]:ccol[name][0] + P] for name in ("had", "hadneg"))
        headmask = const("headmask")
        cos = const("cos").rearrange("p (c d) -> p c d", c=C)
        sin = const("sin").rearrange("p (c d) -> p c d", c=C)
        growth = const("growth")
        rowscale = const("rowscale").rearrange("p (c h) -> p c h", c=C)
        stateblock, statedecay = const("stateblock"), const("statedecay")

        x = sb("x", C, D)
        y = sb("y", C, D)
        xn = sb("xn", C, D)
        featT = sb("featT", KT, T)
        raw = sb("raw", C, 2)
        bn = sb("bn", 2, 6)
        unread = sb("unread", 2)
        ssq = sb("ssq", C)
        rstd = sb("rstd", C)
        rs2 = sb("rs2", C)
        rs2f = sb("rs2f", C)
        tmp1 = sb("tmp1", C)
        tmp2 = sb("tmp2", C)
        shift = sb("shift", C)
        shift2 = sb("shift2", C)

        experts = sb("experts", E * EW)
        region = [experts[:, 0:E // 2 * EW], experts[:, E // 2 * EW:]]
        used = [0, 0]

        def carve(r, *shape):
            n = int(np.prod(shape))
            ap = region[r][:, used[r]:used[r] + n]
            used[r] += n
            assert used[r] <= E // 2 * EW
            if len(shape) == 2:
                ap = ap.rearrange("p (a b) -> p a b", a=shape[0])
            elif len(shape) == 3:
                ap = ap.rearrange("p (a b c) -> p a b c", a=shape[0], b=shape[1])
            return ap

        w_qkvg = carve(0, KT, 4 * D)
        rotc = carve(0, 2 * D)
        rots = carve(0, 2 * D)
        qk = carve(0, 2, 2 * D)
        qkT = carve(0, 2, 4, P)
        qx = carve(0, KT, HT * P)
        pT = carve(0, H, P)
        assert used[0] >= FM * T
        w_out = carve(0, KT, D)
        hT = carve(0, 2, KT, P)
        va = carve(0, 2, H * (DH + 1))
        sg = carve(0, 3, D)
        state = carve(0, KT, HT * (DH + 1))
        statetmp = carve(0, KT, HT * (DH + 1))
        den = carve(0, H)
        rden = carve(0, H)
        wrow = carve(0, H)
        o1 = carve(0, D)
        osq = carve(0, D)
        oss = carve(0, H)
        ors = carve(0, H)
        o2 = osq
        o3 = carve(0, 2, D)
        oT = carve(0, KT, P)
        sqj = carve(0, D)
        x1i = y
        halfs = sb("halfs", H)

        wdA = carve(0, FM, D)

        def split(name, at, parts, n):
            return rounded[name][:, at:at + parts * n].rearrange("p (a n) -> p a n", a=parts)

        hid_hi = split("hid_hi", 0, FM, T)
        hid_lo = split("hid_lo", 0, FM, T)
        w_qkvg_r = [split("hid_hi", i * KT * 4 * D, KT, 4 * D) for i in range(2)]
        hT_r = [split("hid_hi", 2 * KT * 4 * D + i * 2 * KT * P, 2 * KT, P) for i in range(2)]
        qkvg_split = [w.rearrange("p k n -> p (k n)") for w in (w_qkvg, *w_qkvg_r)]
        u_hi = split("u_hi", 0, KT, T)
        down_hi = split("down_hi", 0, FM, D)
        down_lo = split("fc_hi", 0, FM, D)
        u_lo = split("ffw", 0, KT, T)
        u_at = E * EW - FM * D - KT * T
        u_flat = experts[:, u_at:u_at + KT * T]
        wdB = u_flat.rearrange("p (a n) -> p a n", n=D)

        ffw = sb("ffw", 2 * KT * F)
        w_fc1 = [split(name, 0, KT, F) for name in ("fc_hi", "ffw")]
        w_fc2 = [split(name, KT * F, FM, D) for name in ("fc_hi", "ffw")]
        w_ug = [split(name, 0, KT, 2 * F) for name in ("ug_hi", "ug_lo")]
        ug_raw = experts[:, FM * T:FM * T + 2 * KT * F]
        fc_split = ffw, rounded["fc_hi"], rounded["ffw"]
        ug_split = ug_raw, rounded["ug_hi"], rounded["ug_lo"]

        def pieces(c):
            return [c] if c < C - 2 else [c, c + 1] if c == C - 2 else []

        def split_hi(eng, weights, n):
            cols = slice(n * GW, (n + 1) * GW)
            raw, hi, _ = weights
            return eng.activation(hi[:, cols], raw[:, cols], ACT.Copy)

        def split_lo(eng, weights, n):
            cols = slice(n * GW, (n + 1) * GW)
            raw, hi, lo = weights
            return eng.tensor_tensor(lo[:, cols], raw[:, cols], hi[:, cols].bitcast(F32), ALU.subtract)

        qT = ffw[:, 0:KT * T].rearrange("p (k n) -> p k n", k=KT)
        v = ffw[:, KT * T:].rearrange("p (c n) -> p c n", c=C)
        attn = sb("attn", 3 * T)
        prob = attn[:, 0:2 * T].rearrange("p (b n) -> p b n", n=GW)
        probT = attn[:, 2 * T:].rearrange("p (j n) -> p j n", j=C)
        silu_g = sb("silu_g", 2, GW)
        w_qkt = attn[:, 0:T].rearrange("p (a k n) -> p a k n", a=2, k=KT)
        w_vt = silu_g[:, 0, :].rearrange("p (k n) -> p k n", k=KT)
        feat_hi = rounded["featT"]
        feat_lo = split("attn", T, KT, T)
        down_tmp = attn[:, 0:T].rearrange("p (b a n) -> p b a n", b=2, n=D)
        w_o = carve(0, KT, D)
        w_m = sb("w_m", KT, D)
        w_vo = sb("w_vo", KT, D)
        w_r = sb("w_r", KT, E)
        w_spare = u_flat[:, 0:D]
        scpar = sb("scpar", FM)
        scup = sb("scup", FM)
        rmax = sb("rmax", C)
        rsum = sb("rsum", C, 2)
        rmaxp = sb("rmaxp", C)
        rinv = sb("rinv", C)
        flat_y = y[:].rearrange("p c d -> p (c d)")
        zT = flat_y[:, 0:D].rearrange("p (k n) -> p k n", k=KT)
        oh = flat_y[:, D:D + 3 * C * E].rearrange("p (a n) -> p a n", a=3)
        pick = flat_y[:, 4 * D:5 * D].rearrange("p (a n) -> p a n", a=2)
        posn = flat_y[:, 5 * D:5 * D + C * E]
        wparts = flat_y[:, 3 * D + 4 * C:3 * D + 7 * C].bitcast(BF16).rearrange("p (a n) -> p a n", a=3)
        rest = flat_y[:, 3 * D:3 * D + 4 * C].rearrange("p (a n) -> p a n", a=2)
        lgs = sb("lgs", C, E)
        top = sb("top", C, 8)
        topi = sb("topi", C, 8, dt=U32)
        topf = sb("topf", C, 2)
        dv8 = sb("dv8", C)
        ex8 = sb("ex8", C)
        p12 = sb("p12", 2, C)
        ends = sb("ends", 2, E)
        ntile = sb("ntile", E)
        ntile_i = sb("ntile_i", E, dt=I32)
        base = sb("base", E)
        slotf = sb("slotf", 2 * C)
        slot_i = sb("slot_i", 3, 2 * C, dt=I32)
        rowf = sb("rowf", 2 * C)
        tilef = sb("tilef", 2 * C)
        id1, weight, idtmp, source, target, texp, texp_i = (
            flat_y[:, 6 * D + i * 32:6 * D + i * 32 + TILES] for i in range(7))
        source, target, texp_i = source.bitcast(U32), target.bitcast(U32), texp_i.bitcast(I32)
        source_span = flat_y[:, 6 * D + 3 * 32:6 * D + 3 * 32 + TILES + LOADS].bitcast(U32)
        source_t = sb("source_t", LOADS, dt=U32)
        target_t = sb("target_t", 2, dt=U32)
        def two(ap):
            return ap.rearrange("p (b n) -> p b n", b=2)

        mh = two(attn[:, 0:2 * FE])
        mh_hi = two(rounded["attn"][:, 2 * FE:4 * FE])
        mh_lo = two(rounded["attn"][:, 4 * FE:6 * FE])
        mx = xn
        my = two(featT[:].rearrange("p k n -> p (k n)")[:, C * (P + 2 * TILES):C * (P + 2 * TILES) + 2 * D])
        w1 = two(x[:].rearrange("p c d -> p (c d)"))
        w2_hi, w2_lo = (rounded["ffw"][:, at:at + 2 * FEM * D].rearrange("p (b n) -> p b n", b=2)
                        for at in (0, 2 * FEM * D))
        mxT = two(silu_g[:, 0, :])
        tcmp = silu_g[:, 1, 0:TILES * E]
        bits16 = featT[:].rearrange("p k n -> p (k n)").bitcast(BF16)
        onerow = bits16[:, 0:2 * C * P].rearrange("p (a n) -> p a n", n=P)
        idpair = bits16[:, 2 * C * P:2 * C * (P + 2 * TILES)].rearrange("p (a b n) -> p a b n", b=2, n=TILES)
        onetile = ffw[:, 0:2 * C * TILES].rearrange("p (a n) -> p a n", n=TILES)
        wpair = ffw[:, KT * T:].bitcast(BF16)[:, 0:2 * C * 3 * TILES].rearrange("p (a b n) -> p a b n", b=3, n=TILES)

        psum = ctx.enter_context(nc.psum_tensor("psum", [P, 8, 512], F32))

        ztok = nc.dram_tensor("router_input", [T, D], F32, kind="Internal").ap()

        full = [sem(f"psum_full{b}") for b in range(8)]
        drained = [sem(f"psum_drained{b}") for b in range(8)]
        s_cst, s_qkvg, s_outw, s_vec = sem("const_loaded"), sem("qkvg_loaded"), sem("outw_loaded"), sem("vec_loaded")
        s_fc, s_down, s_ug, s_at, s_o = sem("fc_loaded"), sem("down_loaded"), sem("upgate_loaded"), sem("attw_loaded"), sem("o_loaded")
        s_exp = [sem("experts_lo_loaded"), sem("experts_hi_loaded")]
        s_x = [sem(f"x_loaded{n}") for n in range(4)]
        s_fchi, s_fclo = sem("fc_weights_hi"), sem("fc_weights_lo")
        s_ughi, s_uglo = sem("upgate_weights_hi"), sem("upgate_weights_lo")
        s_had = sem("hadamard_rounded")
        s_wqhi, s_wqlo, s_hThi = sem("qkvg_weights_hi"), sem("qkvg_weights_lo"), sem("input_hi")
        s_down_split = sem("down_weights_lo")
        s_fthi, s_uhi = sem("features_hi"), sem("transformed_hi")
        s_hhi, s_hlo = sem("hidden_hi"), sem("hidden_lo")
        s_scale = sem("norm_scales")
        s_spare = sem("spare_rows_zeroed")
        s_ztok = sem("router_input_stored")
        s_x3 = sem("residual_stored")
        s_p = sem("gate_weights_ready")
        s_map = sem("place_factors_ready")
        s_tiles, s_poolmap = sem("one_hot_tiles"), sem("pool_place_factors")
        s_src = sem("tile_sources_ready")
        s_add = sem("tile_added")
        s_dv = sem("vector_steps")
        s_pl = sem("pool_steps")
        s_ac = sem("scalar_steps")
        s_init = sem("buffers_set")
        s_par = sem("ffn_scales_ready")
        s_stat = sem("stats_ready")
        s_xn = [sem(f"normalised{ph}") for ph in range(5)]
        s_y = sem("layernorm_ready")
        s_xr = [sem("ffn_residual"), sem("attn_residual")]
        s_oss = sem("head_squares")
        s_qk = sem("rotated")
        s_va = sem("values_ready")
        s_qx = [sem(f"queries_spread{k}") for k in range(KT)]
        s_state = sem("state_ready")
        s_ors = sem("head_rms_ready")
        s_o3 = sem("gated_ready")
        s_bfly = sem("butterflies")
        s_mx = sem("rowmax_ready")
        s_gap = sem("logit_gap_ready")
        s_e8 = sem("gap_exp_ready")
        s_oh = sem("onehot_ready")
        s_te = sem("tile_experts_ready")
        s_ld = [sem(f"tile_loaded{n}") for n in range(LOADS)]
        s_txf, s_txd = sem("tile_xT_full"), sem("tile_xT_drained")
        s_hf, s_hd = sem("tile_h_full"), sem("tile_h_drained")
        s_w1, s_w2 = sem("tile_w1_ready"), sem("tile_w2_ready")
        s_w2hi = sem("tile_w2_hi")
        s_thi, s_tlo = sem("tile_h_hi"), sem("tile_h_lo")
        s_yf, s_yd = sem("tile_y_full"), sem("tile_y_drained")

        def turned(c):
            return GC * (c % 2) if c < GC else 0

        def bank(job):
            b, _ = plan[job]
            return psum[:, b, :]

        def filled(eng, job):
            b, n = plan[job]
            eng.wait_ge(full[b], n)
            return psum[:, b, :]

        def emptied(eng, job):
            b, n = plan[job]
            eng.wait_ge(drained[b], n)

        gate = E // 2 * EW

        block = ctx.enter_context(nc.Block())

        @block.sync
        def _(sp):
            xs = x_in.rearrange("(c p) d -> p c d", p=P)
            for n in range(4):
                sp.dma_start(x[:, 2 * n:2 * n + 2, :], xs[:, 2 * n:2 * n + 2, :]).then_inc(s_x[n], 16)
                if n == 0:
                    sp.dma_start(cst[:], const_in).then_inc(s_cst, 16)
                    sp.dma_start(w_qkvg, qkvg_in).then_inc(s_qkvg, 16)
            sp.dma_start(w_out, out_w_in).then_inc(s_outw, 16)
            sp.dma_start(wdA, down_in).then_inc(s_down, 16)
            sp.dma_start(w_qkt[:, 0], wqt_in).then_inc(s_at, 16)
            sp.dma_start(w_qkt[:, 1], wkt_in).then_inc(s_at, 16)
            sp.dma_start(w_vt, wvt_in).then_inc(s_at, 16)
            sp.dma_start(w_o, o_in).then_inc(s_at, 16)
            sp.dma_start(ffw[:, 0:KT * F], fc1_in.rearrange("p k n -> p (k n)")).then_inc(s_fc, 16)
            sp.dma_start(ffw[:, KT * F:], fc2_in.rearrange("p m n -> p (m n)")).then_inc(s_fc, 16)
            sp.dma_start(w_r[:], router_in).then_inc(s_o, 16)
            sp.wait_ge(full[plan[("y", C - 1)][0]], plan[("y", C - 1)][1])
            sp.wait_ge(s_xn[1], C)
            sp.dma_start(ug_raw, upgate_in.rearrange("p k n -> p (k n)")).then_inc(s_ug, 16)
            half = E // 4
            sp.wait_ge(full[plan[("up", G - 1, FM - 1)][0]], plan[("up", G - 1, FM - 1)][1])
            for e in range(half, E // 2):
                sp.dma_start(region[0][:, e * EW:(e + 1) * EW], experts_in[e]).then_inc(s_exp[0], 16)
            sp.wait_ge(full[plan[("down", C - 1)][0]], plan[("down", C - 1)][1])
            for e in range(half):
                sp.dma_start(region[0][:, e * EW:(e + 1) * EW], experts_in[e]).then_inc(s_exp[0], 16)
            for e in range(E // 2):
                sp.dma_start(region[1][:, e * EW:(e + 1) * EW], experts_in[E // 2 + e]).then_inc(s_exp[1], 16)
            for c in range(C):
                sp.wait_ge(s_xn[4], c + 1)
                sp.dma_start(ztok[c * P:(c + 1) * P, :], xn[:, c, :]).then_inc(s_ztok, 16)
                sp.dma_start(out[c * P:(c + 1) * P, :], x[:, c, :]).then_inc(s_x3, 16)

        @block.gpsimd
        def _(pool):
            steps = [0]

            def link(ins):
                steps[0] += 1
                ins.then_inc(s_pl, 1)
                pool.wait_ge(s_pl, steps[0])

            def power(dst, src):
                return pool.tensor_tensor(dst, src, halfs[:, 0:dst.shape[1]], ALU.pow)

            def norm(ph, c, double):
                col = slice(c, c + 1)
                pool.wait_ge(s_stat, ph * C + c + 1)
                ins = pool.tensor_scalar(tmp1[:, col], raw[:, c, 1:2], EPS, None, ALU.add)
                if double:
                    ins = pool.tensor_scalar(tmp2[:, col], raw[:, c, 1:2], 1.0 + EPS, EPS * EPS, ALU.mult, ALU.add)
                link(ins)
                ins = power(rstd[:, col], tmp1[:, col])
                if double:
                    ins = power(rs2[:, col], tmp2[:, col])
                link(ins)
                ins = pool.tensor_scalar(shift[:, col], raw[:, c, 0:1], rstd[:, col], -1.0, ALU.mult, ALU.mult)
                if double:
                    ins = pool.tensor_scalar(shift2[:, col], raw[:, c, 0:1], rs2[:, col], -1.0, ALU.mult, ALU.mult)
                ins.then_inc(s_scale, 1)

            def attention_residual(c):
                pool.wait_ge(s_y, C + c + 1)
                pool.tensor_tensor(x[:, c, :], x[:, c, :], y[:, c, :], ALU.add).then_inc(s_xr[1], 1)

            def head_rms(c):
                pool.wait_ge(s_oss, c + 1)
                link(pool.tensor_scalar(oss, oss, 1.0 / DH, EPS, ALU.mult, ALU.add))
                pool.tensor_tensor(ors, oss, halfs[:], ALU.pow).then_inc(s_ors, 1)

            def ffn_norm(c):
                col = slice(c, c + 1)
                pool.wait_ge(s_ac, c + 1)
                link(pool.tensor_scalar(tmp1[:, col], ssq[:, col], 1.0 / D, EPS, ALU.mult, ALU.add))
                power(rs2f[:, col], tmp1[:, col]).then_inc(s_scale, 1)
                link(pool.tensor_tensor(x[:, c, :], x[:, c, :], x1i[:, c, :], ALU.add))
                pool.tensor_tensor(x[:, c, :], x[:, c, :], vector("fc2_b"), ALU.add).then_inc(s_xr[0], 1)

            def butterfly(stage, half):
                src, dst = ((wdA, wdB), (wdB, wdA), (wdA, wdB))[stage]
                a = src.rearrange("p (o t i) n -> p o t (i n)", t=2, i=1 << stage)
                b = dst.rearrange("p (o t i) n -> p o t (i n)", t=2, i=1 << stage)
                return pool.tensor_tensor(b[:, :, half], a[:, :, 0], a[:, :, 1], (ALU.add, ALU.subtract)[half])

            def half_stage(n):
                if n == 0:
                    pool.wait_ge(s_spare, 16)
                    pool.wait_ge(s_down, 16)
                ins = butterfly(n // 2, n % 2)
                if n == 5:
                    ins.then_inc(s_bfly, 1)
                else:
                    link(ins)

            link(pool.memset(halfs[:], -0.5))
            link(pool.memset(state, 0.0))
            pool.memset(w_spare, 0.0).then_inc(s_init, 1)
            norm(0, 0, True)
            norm(0, 1, True)
            pool.wait_ge(s_cst, 16)
            for n in range(2):
                va_n = va[:, n].rearrange("p (h e) -> p h e", e=DH + 1)
                pool.tensor_copy(va_n[:, :, DH], growth).then_inc(s_init, 1)
            norm(0, 2, True)
            pool.wait_ge(s_init, 3)
            pool.dma_start(out[T:T + P, :], w_spare).then_inc(s_spare, 16)

            def rotated(c):
                emptied(pool, ("qk", c))
                if c >= 2:
                    filled(pool, ("st", c - 2))
                pool.tensor_tensor(qk[:, c % 2, :], rotc, rots, ALU.add).then_inc(s_qk, 1)

            pool.wait_ge(s_vec, 16)
            rotated(0)
            rotated(1)
            norm(0, 3, True)
            for c in range(C):
                if c:
                    head_rms(c - 1)
                if c + 4 < C:
                    norm(0, c + 4, True)
                if c >= 2:
                    ffn_norm(c - 2)
                if c + 2 < C:
                    rotated(c + 2)
                for n in pieces(c):
                    pool.wait_ge(s_fchi, n + 1)
                    split_lo(pool, fc_split, n).then_inc(s_fclo, 1)
                if 1 <= c <= 6:
                    half_stage(c - 1)
            head_rms(C - 1)
            ffn_norm(C - 2)
            ffn_norm(C - 1)
            for c in range(C):
                norm(1, c, False)
            for c in range(C):
                norm(2, c, True)
                if c:
                    attention_residual(c - 1)
            attention_residual(C - 1)
            for c in range(C):
                norm(3, c, False)
            pool.wait_ge(s_tiles, 1)
            chunk_at = const("chunk_at").unsqueeze(2).to_broadcast([P, 2 * C, TILES])
            pool.tensor_tensor(idpair[:, :, 1, :], onetile, chunk_at, ALU.mult).then_inc(s_poolmap, 1)
            pool.wait_ge(s_ztok, 16 * C)
            pool.wait_ge(s_x3, 16 * C)
            pool.wait_ge(s_spare, 16)

            def gather(t, n):
                pool.wait_ge(s_src, t + 1)
                pool.indirect_dma_start(
                    out=mx[:, n, :], out_offset=None, in_=ztok,
                    in_offset=bass.IndirectOffsetOnAxis(ap=source_t[:, n:n + 1], axis=0)).then_inc(s_ld[n], 16)

            def step(t, u, last=False):
                par, n = u % 2, u % LOADS
                if not last:
                    pool.wait_ge(s_txf, t + 1)
                    gather(t + LOADS, n)
                pool.wait_ge(s_yd, t + 1)
                if t:
                    pool.wait_ge(s_add, t * 16)
                pool.indirect_dma_start(
                    out=out, out_offset=bass.IndirectOffsetOnAxis(ap=target_t[:, par:par + 1], axis=0),
                    in_=my[:, par, :], in_offset=None, compute_op=ALU.add, bounds_check=T + P - 1
                ).then_inc(s_add, 16)

            for n in range(LOADS):
                gather(n, n)
            for t in range(TILES):
                step(t, t, last=t + LOADS >= TILES)
            pool.wait_ge(s_add, 16 * TILES)

        @block.scalar
        def _(act):
            act.dma_start(vec[:], vec_in).then_inc(s_vec, 16)
            act.wait_ge(s_vec, 16)
            act.activation(unread[:, 0:1], vec[:, 0:1], ACT.Silu)

            def drain(job, dst, scale=1.0, func=ACT.Copy, src=None):
                b, _ = plan[job]
                p_ = filled(act, job)
                act.activation(dst, src(p_) if src else p_[:, 0:dst.free_size()], func, scale=scale).then_inc(drained[b], 1)

            def drain2(job, dst, name, bias=None):
                b, _ = plan[job]
                p_ = filled(act, job)
                for k in range(KT):
                    kw = {"bias": vector(bias)[:, k:k + 1]} if bias else {}
                    ins = act.activation(dst[:, k, :], p_[:, k * P:(k + 1) * P], ACT.Identity,
                                         scale=vector(name)[:, k:k + 1], **kw)
                ins.then_inc(drained[b], 1)

            def normal(ph, c, n, double):
                col = slice(c, c + 1)
                act.wait_ge(s_scale, n)
                a, b = (rs2, shift2) if double else (rstd, shift)
                act.activation(xn[:, c, :], x[:, c, :], ACT.Identity, scale=a[:, col], bias=b[:, col]
                               ).then_inc(s_xn[ph], 1)
                if double:
                    act.activation(y[:, c, :], x[:, c, :], ACT.Identity, scale=rstd[:, col], bias=shift[:, col]
                                   ).then_inc(s_y, 1)

            def xt(c):
                if c < WHOLE:
                    drain2(("xt", c), hT[:, c % 2], "retn_w")
                    return
                p_ = filled(act, ("xt", c))
                for k in range(KT):
                    ins = act.activation(hT_r[0][:, c % 2 * KT + k, :], p_[:, k * P:(k + 1) * P], ACT.Copy,
                                         scale=vector("retn_w")[:, k:k + 1])
                ins.then_inc(s_hThi, 1)

            def ffn_in(c):
                act.wait_ge(s_scale, min(C, c + 7) + c + 1)
                act.activation(xn[:, c, :], x1i[:, c, :], ACT.Copy, scale=rs2f[:, c:c + 1]).then_inc(s_xn[1], 1)

            def gate_g(c):
                act.wait_ge(s_va, c + 1)
                if c >= 3:
                    act.wait_ge(s_o3, c - 2)
                b, _ = plan[("vg", c)]
                act.activation(sg[:, c % 3, :], bank(("vg", c))[:, D:2 * D], ACT.Silu).then_inc(drained[b], 1)

            def ot(c):
                drain(("ot", c), oT.rearrange("p k n -> p (k n)"))

            def square(c):
                emptied(act, ("y", c))
                act.activation(sqj, x1i[:, c, :], ACT.Square, accum_out=ssq[:, c:c + 1]).then_inc(s_ac, 1)

            def qkt(c):
                drain(("qkt", c), qkT[:, c % 2].rearrange("p a n -> p (a n)"))
                emptied(act, ("qkt", c))
                for h in range(HT):
                    ins = act.activation(qx[:, 1, h * P:(h + 1) * P], qkT[:, c % 2, 1, :], ACT.Copy,
                                         scale=headmask[:, h:h + 1])
                ins.then_inc(s_qx[1], 1)

            def features_hi(job, name):
                c = job[1]
                p_ = filled(act, job)
                for k in range(KT):
                    ins = act.activation(feat_hi[:, k, c * P:(c + 1) * P], p_[:, k * P:(k + 1) * P], ACT.Copy,
                                         scale=vector(name)[:, k:k + 1])
                ins.then_inc(s_fthi, 1)

            def bt(c):
                features_hi(("bt", c), "final_w")

            def block_input(c):
                normal(0, c, c + 1 + max(0, c - 6), True)

            block_input(0)
            xt(0)
            block_input(1)
            xt(1)
            block_input(2)
            act.wait_ge(s_cst, 16)
            qkt(0)
            gate_g(0)
            gate_g(1)
            for n in range(GC):
                split_hi(act, qkvg_split, n).then_inc(s_wqhi, 1)
            xt(2)
            for c in range(C):
                if c >= 2:
                    square(c - 2)
                if c + 3 < C:
                    block_input(c + 3)
                if c + 1 < C:
                    qkt(c + 1)
                if c >= 3:
                    ffn_in(c - 3)
                if c == C - 1:
                    act.activation(unread[:, 1:2], vec[:, 0:1], ACT.Gelu_apprx_tanh)
                    bt(2)
                if c:
                    ot(c - 1)
                if c + 2 < C:
                    gate_g(c + 2)
                elif c == C - 2:
                    for m in range(KT):
                        drain(("m", m), w_m[:, m, :], scale=float(D) ** -0.5)
                else:
                    for m in range(KT):
                        drain(("vo", m), w_vo[:, m, :])
                if c + 3 < C:
                    xt(c + 3)
                elif c < C - 1:
                    bt(c + 3 - C)
                else:
                    bt(3)
                if c == 0:
                    act.wait_ge(s_fc, 32)
                for n in pieces(c):
                    split_hi(act, fc_split, n).then_inc(s_fchi, 1)

            def ct(c):
                features_hi(("ct", c), "su_ug")

            def dt(c):
                drain2(("dt", c), featT[:, :, c * P:(c + 1) * P], "gamma", "beta")

            def hadamard(g):
                for m in range(KT):
                    act.activation(u_hi[:, m, g * GW:(g + 1) * GW], filled(act, ("had", g, m)), ACT.Copy
                                   ).then_inc(s_uhi, 1)

            def queries(g):
                for m in range(KT):
                    drain(("qm", g, m), qT[:, m, g * GW:(g + 1) * GW])

            square(C - 2)
            ffn_in(C - 3)
            for g in range(G):
                for m in range(FM):
                    b, _ = plan[("fc1", g, m)]
                    n = g * FM + m
                    if (g, m) == (0, LAST_TURN):
                        bt(TURNS[m])
                    if n >= 2:
                        act.wait_ge(s_hlo, n - 1)
                    act.activation(silu_g[:, n % 2, :], filled(act, ("fc1", g, m)),
                                   ACT.Gelu_apprx_tanh, bias=vector("fc1_b")[:, m:m + 1]).then_inc(drained[b], 1)
                    emptied(act, ("fc1", g, m))
                    if g:
                        act.activation(hid_hi[:, m, g * GW:(g + 1) * GW], silu_g[:, n % 2, :], ACT.Copy
                                       ).then_inc(s_hhi, 1)
                    if (g, m) == (0, 1):
                        ffn_in(C - 2)
                    if (g, m) == (0, 2):
                        ot(C - 1)
                    if (g, m) == (0, 3):
                        square(C - 1)
                    if (g, m) == (0, 4):
                        ffn_in(C - 1)
                    if g == 0 and m in TURNS and m != LAST_TURN:
                        bt(TURNS[m])
            act.wait_ge(s_ug, 16)
            act.wait_ge(s_bfly, 1)
            for n in range(C):
                split_hi(act, ug_split, n).then_inc(s_ughi, 1)
            for c in range(C):
                if c >= AHEAD:
                    ct(c - AHEAD)
                if c == C - 2:
                    hadamard(0)
                normal(2, c, 2 * C + c + 1, False)
            act.wait_ge(s_par, 2)
            for g in range(G):
                for m in range(FM):
                    if g == 0 and m < AHEAD:
                        ct(C - AHEAD + m)
                    n = g * FM + m
                    act.wait_ge(s_hlo, G * FM + n - 1)
                    b, _ = plan[("gate", g, m)]
                    act.activation(silu_g[:, n % 2, :], filled(act, ("gate", g, m)), ACT.Silu,
                                   scale=scpar[:, m:m + 1]).then_inc(drained[b], 1)
                    if g == 0 and m == FM - 2:
                        hadamard(1)
            for c in range(C):
                if c >= AHEAD:
                    dt(c - AHEAD)
                normal(3, c, 3 * C + c + 1, True)
            queries(0)
            for c in range(GC):
                drain(("v", c), v[:, c, :])
            dt(C - 2)
            dt(C - 1)

            def exps(c):
                act.wait_ge(s_mx, c + 1)
                if c >= GC + 2:
                    for b_ in range(2):
                        filled(act, ("pt", c - 2, b_))
                elif c >= GC:
                    for c_ in score_banks(c):
                        filled(act, ("pt", c_, 0))
                for b_ in range(c // GC + 1):
                    n = min(GW, (c + 1) * P - b_ * GW)
                    act.activation(prob[:, score_banks(c)[b_], 0:n], bank(("sc", c, b_))[:, 0:n], ACT.Exp,
                                   bias=rmax[:, c:c + 1], accum_out=rsum[:, c, b_:b_ + 1]
                                   ).then_inc(drained[plan[("sc", c, b_)][0]], 1)

            def zt(c):
                normal(4, c, 4 * C + c + 1, False)
                if c == 0:
                    act.wait_ge(s_xr[1], C)
                drain(("zt", c), zT.rearrange("p k n -> p (k n)"))

            exps(0)
            queries(1)
            for c in range(C):
                if c + 1 < C:
                    exps(c + 1)
                if c < GC:
                    drain(("v", c + GC), v[:, c + GC, :])
                if c:
                    zt(c - 1)
            zt(C - 1)
            act.wait_ge(s_gap, 1)
            act.activation(ex8[:], dv8[:], ACT.Exp).then_inc(s_e8, 1)

            act.wait_ge(s_te, 1)
            act.wait_ge(s_x3, 16 * C)
            for n in range(2):
                act.wait_ge(s_exp[n], 16 * (E // 2))

            def tile_w1(t, par):
                at = act.value_load(texp_i[0:1, bass.ds(t, 1)], min_val=0, max_val=(E - 1) * EW)
                act.activation(w1[:, par, :], experts[:, bass.ds(at, KT * FE)], ACT.Copy).then_inc(s_w1, 1)

            def tile_xT(t, par):
                act.wait_ge(s_txf, t + 1)
                act.activation(mxT[:, par, :], psum[:, par, 0:KT * P], ACT.Copy).then_inc(s_txd, 1)

            def tile_silu(t, par):
                act.wait_ge(s_hf, t + 1)
                if not (isinstance(t, int) and t < 2):
                    act.wait_ge(s_tlo, t - 1)
                act.activation(mh[:, par, :], psum[:, 2 + par, :], ACT.Silu).then_inc(s_hd, 1)

            def tile_hi(t, par):
                act.wait_ge(s_hd, t + 1)
                if not (isinstance(t, int) and t < 2):
                    act.wait_ge(s_yf, t - 1)
                act.activation(mh_hi[:, par, :], mh[:, par, :], ACT.Copy).then_inc(s_thi, 1)

            def step(t, par):
                tile_w1(t + 2, par)
                tile_silu(t + 1, 1 - par)
                tile_xT(t + 2, par)
                tile_hi(t + 1, 1 - par)

            tile_w1(0, 0)
            tile_xT(0, 0)
            tile_w1(1, 1)
            tile_silu(0, 0)
            tile_xT(1, 1)
            tile_hi(0, 0)
            step(0, 0)
            step(1, 1)
            with act.Fori(2, TILES - 3, 2) as t:
                step(t, 0)
                step(t + 1, 1)
            step(TILES - 3, 0)
            tile_silu(TILES - 1, 0)
            tile_hi(TILES - 1, 0)

        @block.tensor
        def _(pe):
            def fill(job):
                b, n = plan[job]
                if n > 1:
                    pe.wait_ge(drained[b], n - 1)
                return psum[:, b, :]

            def done(ins, job):
                ins.then_inc(full[plan[job][0]], 1)

            def turn(job, src):
                d = fill(job)
                for k in range(src.shape[1] // P):
                    ins = pe.transpose(d[:, k * P:(k + 1) * P], src[:, k * P:(k + 1) * P], ident)
                done(ins, job)

            def product(job, pairs, n):
                d = fill(job)
                for i, (w, m) in enumerate(pairs):
                    ins = pe.matmul(d[:, 0:n], w, m, start=(i == 0), stop=(i == len(pairs) - 1))
                done(ins, job)

            def product3(job, pairs, n):
                d = fill(job)
                for i, ((w_hi, w_lo), (m_hi, m_lo)) in enumerate(pairs):
                    pe.matmul(d[:, 0:n], w_hi, m_hi, start=(i == 0), stop=False)
                    pe.matmul(d[:, 0:n], w_hi, m_lo, start=False, stop=False)
                    ins = pe.matmul(d[:, 0:n], w_lo, m_hi, start=False, stop=(i == len(pairs) - 1))
                done(ins, job)

            def xt(c):
                pe.wait_ge(s_xn[0], c + 1)
                turn(("xt", c), xn[:, c, :])

            def features(name, phase, c):
                pe.wait_ge(s_xn[phase], c + 1)
                turn((name, c), xn[:, c, :])

            def project(c):
                emptied(pe, ("xt", c))
                if c == WHOLE:
                    pe.wait_ge(s_wqlo, GC)
                for half, name in enumerate(("qk", "vg")):
                    d = fill((name, c))
                    for k in range(KT):
                        cols = slice(half * 2 * D, (half + 1) * 2 * D)
                        if c < WHOLE:
                            ins = pe.matmul(d, hT[:, c % 2, k, :], w_qkvg[:, k, cols],
                                            start=(k == 0), stop=(k == KT - 1))
                        else:
                            for i, (a, b) in enumerate(((0, 0), (0, 1), (1, 0))):
                                ins = pe.matmul(d, hT_r[a][:, c % 2 * KT + k, :], w_qkvg_r[b][:, k, cols],
                                                start=(k == 0 and i == 0), stop=(k == KT - 1 and i == 2))
                        if k == KT - 1:
                            done(ins, (name, c))
                        yield

            def weight_product(name, left, right):
                if name == "m":
                    pe.wait_ge(s_at, 64)
                for m in range(KT):
                    d = fill((name, m))
                    for k in range(KT):
                        ins = pe.matmul(d[:, 0:D], left[:, k, m * P:(m + 1) * P], right[:, k, :],
                                        start=(k == 0), stop=(k == KT - 1))
                        if k == KT - 1:
                            done(ins, (name, m))
                        yield

            def qkt(c):
                pe.wait_ge(s_qk, c + 1)
                turn(("qkt", c), qk[:, c % 2, :])

            def scores(c):
                for k in range(KT):
                    pe.wait_ge(s_qx[k], c + 1)
                for n in range(4):
                    k, h = n // 2, (n % 2) * 4
                    product(("p", c, n), [(qkT[:, c % 2, 2 + k, :], qx[:, k, h * P:(h + 4) * P])], 4 * P)

            def retain(c, others):
                w = DH + 1
                d = fill(("o", c))
                if c == 0:
                    pe.wait_ge(s_init, 3)
                for h in range(H):
                    if h % 4 == 0:
                        next(others)
                        emptied(pe, ("p", c, h // 4))
                    if h == 0:
                        pe.wait_ge(s_va, c + 1)
                    pe.matmul(d[:, h * w:(h + 1) * w], pT[:, h, :], va[:, c % 2, h * w:(h + 1) * w],
                              start=(h == 0), stop=False, skip_group_check=True)
                if c:
                    pe.wait_ge(s_state, c)
                for k in range(KT):
                    ins = pe.matmul(d[:, k * HT * w:(k + 1) * HT * w], qkT[:, c % 2, k, :], state[:, k, :],
                                    start=False, stop=(k == KT - 1), skip_group_check=True)
                done(ins, ("o", c))
                if c == C - 1:
                    return
                d = fill(("st", c))
                for k in range(KT):
                    ins = pe.matmul(d[:, k * HT * w:(k + 1) * HT * w], qk[:, c % 2, D + k * P:D + (k + 1) * P],
                                    va[:, c % 2, k * HT * w:(k + 1) * HT * w], start=True, stop=True)
                done(ins, ("st", c))

            def ot(c):
                pe.wait_ge(s_o3, c + 1)
                turn(("ot", c), o3[:, c % 2, :])

            def yproj(c):
                emptied(pe, ("ot", c))
                product(("y", c), [(oT[:, k, :], w_out[:, k, :]) for k in range(KT)], D)

            pe.wait_ge(s_cst, 16)
            xt(0)
            pe.wait_ge(s_qkvg, 16)
            for _ in project(0):
                pass
            xt(1)
            qkt(0)
            for _ in project(1):
                pass
            xt(2)
            for c in range(C):
                scores(c)
                if c + 1 < C:
                    qkt(c + 1)
                if c == C - 1:
                    features("bt", 1, 2)
                if c + 2 < C:
                    retain(c, project(c + 2))
                elif c == C - 2:
                    retain(c, weight_product("m", w_qkt[:, 0], w_qkt[:, 1]))
                else:
                    retain(c, weight_product("vo", w_vt, w_o))
                if c:
                    ot(c - 1)
                if c + 3 < C:
                    xt(c + 3)
                elif c < C - 1:
                    features("bt", 1, c + 3 - C)
                else:
                    features("bt", 1, 3)
                if c:
                    if c == 1:
                        pe.wait_ge(s_outw, 16)
                    yproj(c - 1)

            def group(g):
                return slice(g * GW, (g + 1) * GW)

            def transform_down(n):
                product(("wd", n), [(had_r.bitcast(F32), wdB[:, 2 * n:2 * n + 2, :].rearrange("p a n -> p (a n)"))], 512)

            pe.wait_ge(s_had, 2)
            pe.wait_ge(s_bfly, 1)
            transform_down(0)
            pe.wait_ge(s_fclo, C)
            for g in range(G):
                for c in range(GC * g, GC * g + GC):
                    emptied(pe, ("bt", c))
                for m in range(FM):
                    product3(("fc1", g, m), [([w[:, k, m * P:(m + 1) * P] for w in w_fc1],
                                              [f[:, k, group(g)] for f in (feat_hi, feat_lo)])
                                             for k in range(KT)], GW)
                    if (g, m) == (0, 2):
                        transform_down(1)
                        ot(C - 1)
                    if (g, m) == (0, 3):
                        yproj(C - 1)
                    if g == 0 and m in TURNS:
                        features("bt", 1, TURNS[m])
            transform_down(2)
            transform_down(3)

            def hadamard(g):
                for c in (GC * g + GC - 2, GC * g + GC - 1):
                    emptied(pe, ("ct", c))
                for m in range(KT):
                    d = fill(("had", g, m))
                    for k in range(KT):
                        w = had_r if (k, m) != (1, 1) else hadneg_r
                        for f in (feat_hi, feat_lo):
                            ins = pe.matmul(d, w, f[:, k, group(g)], start=(k == 0 and f is feat_hi),
                                            stop=(k == KT - 1 and f is feat_lo))
                    done(ins, ("had", g, m))

            for c in range(C):
                pe.wait_ge(s_hlo, (c // GC + 1) * FM)
                product3(("fc2", c), [([h[:, m, c * P:(c + 1) * P] for h in (hid_hi, hid_lo)],
                                       [w[:, m, :] for w in w_fc2]) for m in range(FM)], D)
                if c >= AHEAD:
                    features("ct", 2, c - AHEAD)
                if c == C - 2:
                    hadamard(0)
            pe.wait_ge(s_uglo, 8)
            for g in range(G):
                for m in range(FM):
                    if g == 0 and m < AHEAD:
                        features("ct", 2, C - AHEAD + m)
                    if m == 0:
                        for k in range(KT):
                            emptied(pe, ("had", g, k))
                    for name, at in (("gate", F), ("up", 0)):
                        product3((name, g, m), [([w[:, k, at + m * P:at + (m + 1) * P] for w in w_ug],
                                                 [u[:, k, group(g)] for u in (u_hi, u_lo)])
                                                for k in range(KT)], GW)
                    if g == 0 and m == FM - 2:
                        hadamard(1)
            for c in range(C):
                pe.wait_ge(s_hlo, (G + c // GC + 1) * FM)
                if c == 0:
                    pe.wait_ge(s_down_split, 4)
                product3(("down", c), [([h[:, m, c * P:(c + 1) * P] for h in (hid_hi, hid_lo)],
                                        [w[:, m, :] for w in (down_hi, down_lo)]) for m in range(FM)], D)
                if c >= AHEAD:
                    features("dt", 3, c - AHEAD)
            def queries(g):
                for c in range(GC * g, GC * g + GC):
                    emptied(pe, ("dt", c))
                for m in range(KT):
                    product(("qm", g, m), [(w_m[:, k, m * P:(m + 1) * P], featT[:, k, group(g)])
                                           for k in range(KT)], GW)

            def values(c):
                product(("v", c), [(featT[:, k, c * P:(c + 1) * P], w_vo[:, k, :]) for k in range(KT)], D)

            def att_scores(c):
                if c % GC == 0:
                    for m in range(KT):
                        emptied(pe, ("qm", c // GC, m))
                for b in range(c // GC + 1):
                    n = min(GW, (c + 1) * P - b * GW)
                    product(("sc", c, b), [(qT[:, k, c * P:(c + 1) * P], featT[:, k, b * GW:b * GW + n])
                                           for k in range(KT)], n)

            def prob_turn(c):
                for b in range(c // GC + 1):
                    emptied(pe, ("sc", c, b))
                    n = min(GW, (c + 1) * P - b * GW)
                    turn(("pt", c, b), prob[:, score_banks(c)[b], 0:n])

            def att_out(c):
                for b in range(c // GC + 1):
                    emptied(pe, ("pt", c, b))
                if c % GC == 0:
                    for cc in range(c, c + GC):
                        emptied(pe, ("v", cc))
                product(("pv", c), [(probT[:, turned(c) + j, :], v[:, j, :]) for j in range(c + 1)], D)

            def zt(c):
                pe.wait_ge(s_xn[4], c + 1)
                turn(("zt", c), xn[:, c, :])

            def logits(c):
                emptied(pe, ("zt", c))
                product(("lg", c), [(zT[:, k, :], w_r[:, k, :]) for k in range(KT)], E)

            queries(0)
            for c in range(GC):
                values(c)
            features("dt", 3, C - 2)
            features("dt", 3, C - 1)
            att_scores(0)
            att_scores(1)
            queries(1)
            for c in range(C):
                prob_turn(c)
                if c == 2:
                    pe.wait_ge(s_o, 16)
                if c >= 2:
                    logits(c - 2)
                if c + 2 < C:
                    att_scores(c + 2)
                if c < GC:
                    values(c + GC)
                att_out(c)
                if c:
                    zt(c - 1)
            logits(C - 2)
            d = fill(("rank",))

            def count_pairs(c):
                pe.wait_ge(s_oh, c + 1)
                here = oh[:, 2, c * E:(c + 1) * E]
                later = d[:, (c + 1) * E:(C + 1) * E].rearrange("p (n e) -> p n e", e=E)
                pe.matmul(later, ones, here.unsqueeze(1).to_broadcast([P, C - c, E]),
                          start=(c == 0), stop=False, skip_group_check=True)
                return pe.matmul(d[:, c * E:(c + 1) * E], strict, here,
                                 start=False, stop=(c == C - 1), skip_group_check=True)

            for c in range(C - 2):
                count_pairs(c)
            zt(C - 1)
            logits(C - 1)
            count_pairs(C - 2)
            done(count_pairs(C - 1), ("rank",))

            d = fill(("map",))
            for a in range(2 * C):
                if a % 4 == 0:
                    pe.wait_ge(s_map, a // 4 + 1)
                    if a == 0:
                        pe.wait_ge(s_poolmap, 1)
                ins = pe.matmul(d[:, 0:2 * TILES], onerow[:, a, :], idpair[:, a].rearrange("p b n -> p (b n)"),
                                start=(a == 0), stop=(a == 2 * C - 1))
            done(ins, ("map",))
            for b in range(7):
                pe.wait_ge(drained[b], fills[b])
            def tile_turn(t, u, loads):
                par, n = u % 2, u % LOADS
                pe.wait_ge(s_ld[n], loads)
                for k in range(KT):
                    ins = pe.transpose(psum[:, par, k * P:(k + 1) * P], mx[:, n, k * P:(k + 1) * P], ident)
                ins.then_inc(s_txf, 1)

            def tile_up(t, par):
                pe.wait_ge(s_txd, t + 1)
                pe.wait_ge(s_w1, t + 1)
                if not (isinstance(t, int) and t < 2):
                    pe.wait_ge(s_hd, t - 1)
                for m in range(FEM):
                    for k in range(KT):
                        ins = pe.matmul(psum[:, 2 + par, m * P:(m + 1) * P],
                                        w1[:, par, k * FE + m * P:k * FE + (m + 1) * P],
                                        mxT[:, par, k * P:(k + 1) * P], start=(k == 0), stop=(k == KT - 1))
                ins.then_inc(s_hf, 1)

            def tile_down(t, par):
                pe.wait_ge(s_tlo, t + 1)
                pe.wait_ge(s_w2, t + 1)
                if not (isinstance(t, int) and t < 2):
                    pe.wait_ge(s_yd, t - 1)
                for m in range(FEM):
                    h_hi, h_lo = (h[:, par, m * P:(m + 1) * P] for h in (mh_hi, mh_lo))
                    w_hi, w_lo = (w[:, par, m * D:(m + 1) * D] for w in (w2_hi, w2_lo))
                    pe.matmul(psum[:, 6 + par, 0:D], h_hi, w_hi, start=(m == 0), stop=False)
                    pe.matmul(psum[:, 6 + par, 0:D], h_hi, w_lo, start=False, stop=False)
                    ins = pe.matmul(psum[:, 6 + par, 0:D], h_lo, w_hi, start=False, stop=(m == FEM - 1))
                ins.then_inc(s_yf, 1)

            def step(t, u, loads):
                par = u % 2
                tile_up(t + 1, 1 - par)
                if loads is not None:
                    tile_turn(t + 2, u + 2, loads)
                tile_down(t, par)

            def load_count(t):
                return (t // LOADS + 1) * 16

            tile_turn(0, 0, 16)
            tile_up(0, 0)
            tile_turn(1, 1, 16)
            pe.wait_ge(s_p, 1)
            d = fill(("weights",))
            for a in range(2 * C):
                ins = pe.matmul(d[:, 0:3 * TILES], onerow[:, a, :], wpair[:, a].rearrange("p b n -> p (b n)"),
                                start=(a == 0), stop=(a == 2 * C - 1))
            done(ins, ("weights",))
            for t in range(HEAD):
                if t == 1:
                    emptied(pe, ("weights",))
                step(t, t, load_count(t + 2))
            with pe.Fori(HEAD, LOOPED, LOADS) as t:
                for n in range(HEAD, HEAD + LOADS):
                    step(t + (n - HEAD), n, t * (16 // LOADS) + (load_count(n + 2) - HEAD * 16 // LOADS))
            for t in range(LOOPED, TILES - 1):
                step(t, t, load_count(t + 2) if t + 2 < TILES else None)
            tile_down(TILES - 1, 0)

        @block.vector
        def _(dve):
            steps = [0]

            def link(ins):
                steps[0] += 1
                ins.then_inc(s_dv, 1)
                dve.wait_ge(s_dv, steps[0])

            def wide(ap, n):
                return ap.unsqueeze(2).to_broadcast([P, ap.shape[1], n])

            def over(ap, n):
                return ap.unsqueeze(1).to_broadcast([P, n, ap.shape[1]])

            def input_lo(c):
                job = ("xt", c)
                dve.wait_ge(s_hThi, c - WHOLE + 1)
                for k in range(KT):
                    part = c % 2 * KT + k
                    ins = dve.scalar_tensor_tensor(hT_r[1][:, part, :], bank(job)[:, k * P:(k + 1) * P],
                                                   vector("retn_w")[:, k:k + 1], hT_r[0][:, part, :].bitcast(F32),
                                                   ALU.mult, ALU.subtract)
                ins.then_inc(drained[plan[job][0]], 1)

            counts = {"features": 0}

            def features_lo(job, name):
                c = job[1]
                counts["features"] += 1
                dve.wait_ge(s_fthi, counts["features"])
                for k in range(KT):
                    cols = slice(c * P, (c + 1) * P)
                    ins = dve.scalar_tensor_tensor(feat_lo[:, k, cols], bank(job)[:, k * P:(k + 1) * P],
                                                   vector(name)[:, k:k + 1], feat_hi[:, k, cols].bitcast(F32),
                                                   ALU.mult, ALU.subtract)
                ins.then_inc(drained[plan[job][0]], 1)

            def stats(c):
                link(dve.bn_stats(bn[:, c % 2, :], x[:, c, :]))
                dve.bn_aggr(raw[:, c, :], bn[:, c % 2, :]).then_inc(s_stat, 1)

            def rotate(c):
                if c:
                    dve.wait_ge(s_qk, c)
                q = filled(dve, ("qk", c)).rearrange("p (h d) -> p h d", d=DH)
                dve.tensor_tensor(rotc.rearrange("p (h d) -> p h d", d=DH), q, over(cos[:, c, :], 2 * H), ALU.mult)
                q2 = q.rearrange("p h (i two) -> p h i two", two=2)
                r2 = rots.rearrange("p (h i two) -> p h i two", two=2, i=DH // 2)
                s2 = sin[:, c, :].rearrange("p (i two) -> p i two", two=2)
                for side in range(2):
                    ins = dve.tensor_tensor(r2[:, :, :, side], q2[:, :, :, 1 - side],
                                            over(s2[:, :, side], 2 * H), ALU.mult)
                ins.then_inc(drained[plan[("qk", c)][0]], 1)

            def values(c):
                if c >= 2:
                    filled(dve, ("st", c - 2))
                src = filled(dve, ("vg", c))[:, 0:D].rearrange("p (h d) -> p h d", d=DH)
                dst = va[:, c % 2, :].rearrange("p (h e) -> p h e", e=DH + 1)[:, :, 0:DH]
                dve.tensor_tensor(dst, src, wide(growth, DH), ALU.mult).then_inc(s_va, 1)

            def causal(c):
                if c:
                    filled(dve, ("o", c - 1))
                for n in range(4):
                    src = filled(dve, ("p", c, n)).rearrange("p (h s) -> p h s", s=P)
                    dve.tensor_tensor(pT[:, 4 * n:4 * n + 4, :], src, over(tril, 4), ALU.mult
                                      ).then_inc(drained[plan[("p", c, n)][0]], 1)

            def spread(c):
                emptied(dve, ("qkt", c))
                dve.tensor_tensor(qx[:, 0, :].rearrange("p (h s) -> p h s", s=P), over(qkT[:, c % 2, 0, :], HT),
                                  wide(headmask, P), ALU.mult).then_inc(s_qx[0], 1)

            def inner_residual(c):
                dve.wait_ge(s_y, c + 1)
                dve.tensor_tensor(x1i[:, c, :], y[:, c, :], filled(dve, ("y", c))[:, 0:D], ALU.add
                                  ).then_inc(drained[plan[("y", c)][0]], 1)

            def update_state(c):
                n = KT * HT * (DH + 1)
                src = filled(dve, ("st", c))[:, 0:n]
                flat = statetmp.rearrange("p k n -> p (k n)")
                dve.tensor_tensor(flat, src, stateblock, ALU.mult).then_inc(drained[plan[("st", c)][0]], 1)
                emptied(dve, ("st", c))
                for k in range(KT):
                    ins = dve.scalar_tensor_tensor(state[:, k, :], state[:, k, :], statedecay[:, k:k + 1],
                                                   statetmp[:, k, :], ALU.mult, ALU.add)
                ins.then_inc(s_state, 1)

            def weigh(c):
                d = filled(dve, ("o", c))[:, 0:H * (DH + 1)].rearrange("p (h e) -> p h e", e=DH + 1)
                link(dve.tensor_tensor(den, d[:, :, DH], rowscale[:, c, :], ALU.mult))
                link(dve.scalar_tensor_tensor(den, den, -1.0, den, ALU.mult, ALU.max))
                link(dve.tensor_scalar(den, den, 1.0, None, ALU.max))
                link(dve.reciprocal(rden, den))
                link(dve.tensor_tensor(wrow, rden, rowscale[:, c, :], ALU.mult))
                dve.tensor_tensor(o1.rearrange("p (h d) -> p h d", d=DH), d[:, :, 0:DH], wide(wrow, DH), ALU.mult
                                  ).then_inc(drained[plan[("o", c)][0]], 1)
                if c + 3 < C:
                    input_lo(c + 3)
                else:
                    features_lo(("bt", (0, 1, 3)[c + 3 - C]), "final_w")
                if c:
                    inner_residual(c - 1)
                emptied(dve, ("o", c))
                link(dve.tensor_tensor(osq, o1, o1, ALU.mult))
                if c:
                    dve.wait_ge(s_ors, c)
                dve.tensor_reduce(oss, osq.rearrange("p (h d) -> p h d", d=DH), AX.X, ALU.add).then_inc(s_oss, 1)

            def gated(c):
                dve.wait_ge(s_ors, c + 1)
                link(dve.tensor_tensor(o2.rearrange("p (h d) -> p h d", d=DH),
                                       o1.rearrange("p (h d) -> p h d", d=DH), wide(ors, DH), ALU.mult))
                emptied(dve, ("vg", c))
                dve.tensor_tensor(o3[:, c % 2, :], o2, sg[:, c % 3, :], ALU.mult).then_inc(s_o3, 1)

            for c in range(C):
                if c % 2 == 0:
                    dve.wait_ge(s_x[c // 2], 16)
                stats(c)
            dve.wait_ge(s_vec, 16)
            dve.wait_ge(s_cst, 16)
            for h, h_r in ((had, had_r), (hadneg, hadneg_r)):
                dve.tensor_copy(h_r, h).then_inc(s_had, 1)
            dve.scalar_tensor_tensor(scup[:], vector("scale_up"), D ** -0.5, vector("su_dp"), ALU.mult, ALU.mult
                                     ).then_inc(s_par, 1)
            dve.tensor_scalar(scpar[:], vector("scale_gate"), D ** -0.5, None, ALU.mult).then_inc(s_par, 1)
            for c in range(2):
                rotate(c)
                values(c)
                if c == 0:
                    spread(0)
            for n in range(GC):
                dve.wait_ge(s_wqhi, n + 1)
                split_lo(dve, qkvg_split, n).then_inc(s_wqlo, 1)
            input_lo(2)
            for c in range(C):
                if c:
                    weigh(c - 1)
                causal(c)
                if c:
                    update_state(c - 1)
                    gated(c - 1)
                if c == C - 1:
                    features_lo(("bt", 2), "final_w")
                if c + 1 < C:
                    spread(c + 1)
                if c + 2 < C:
                    rotate(c + 2)
                    values(c + 2)

            def hidden_lo(g, m):
                n, cols = g * FM + m, slice(g * GW, (g + 1) * GW)
                if g:
                    dve.wait_ge(s_hhi, n - FM + 1)
                else:
                    emptied(dve, ("fc1", g, m))
                    link(dve.tensor_copy(hid_hi[:, m, cols], silu_g[:, n % 2, :]))
                dve.tensor_tensor(hid_lo[:, m, cols], silu_g[:, n % 2, :], hid_hi[:, m, cols].bitcast(F32),
                                  ALU.subtract).then_inc(s_hlo, 1)

            def add_residual(job, c):
                dve.tensor_tensor(x[:, c, :], x[:, c, :], filled(dve, job)[:, 0:D], ALU.add
                                  ).then_inc(drained[plan[job][0]], 1)
                emptied(dve, job)
                stats(c)

            def scale_down(n):
                src = filled(dve, ("wd", n)).rearrange("p (a n) -> p a n", n=D)
                dve.scalar_tensor_tensor(down_tmp[:, n % 2], src, F ** -0.5, over(vector("scale_dp"), 2),
                                         ALU.mult, ALU.mult).then_inc(drained[plan[("wd", n)][0]], 1)
                emptied(dve, ("wd", n))
                link(dve.tensor_copy(down_hi[:, 2 * n:2 * n + 2, :], down_tmp[:, n % 2]))

            weigh(C - 1)
            for g in range(G):
                for m in range(FM):
                    if (g, m) == (0, LAST_TURN):
                        features_lo(("bt", TURNS[m]), "final_w")
                    hidden_lo(g, m)
                    if (g, m) == (0, 0):
                        gated(C - 1)
                    if (g, m) == (0, 3):
                        inner_residual(C - 1)
                    if g == 0 and m in TURNS and m != LAST_TURN:
                        features_lo(("bt", TURNS[m]), "final_w")
                    if g == 1 and m in (2, 4):
                        scale_down(m // 2 - 1)
            filled(dve, ("wd", 2))
            for n in range(4):
                if n >= 2:
                    dve.wait_ge(s_down_split, n - 1)
                    scale_down(n)
                dve.tensor_tensor(down_lo[:, 2 * n:2 * n + 2, :], down_tmp[:, n % 2],
                                  down_hi[:, 2 * n:2 * n + 2, :].bitcast(F32), ALU.subtract).then_inc(s_down_split, 1)
            def transformed_lo(g):
                for m in range(KT):
                    cols = slice(g * GW, (g + 1) * GW)
                    job = ("had", g, m)
                    dve.wait_ge(s_uhi, g * KT + m + 1)
                    dve.tensor_tensor(u_lo[:, m, cols], bank(job), u_hi[:, m, cols].bitcast(F32), ALU.subtract
                                      ).then_inc(drained[plan[job][0]], 1)

            for c in range(C):
                for n in pieces(c):
                    dve.wait_ge(s_ughi, n + 1)
                    split_lo(dve, ug_split, n).then_inc(s_uglo, 1)
                dve.wait_ge(s_xr[0], c + 1)
                add_residual(("fc2", c), c)
                if c >= AHEAD:
                    features_lo(("ct", c - AHEAD), "su_ug")
                if c == C - 2:
                    transformed_lo(0)

            for g in range(G):
                for m in range(FM):
                    if g == 0 and m < AHEAD:
                        features_lo(("ct", C - AHEAD + m), "su_ug")
                    n, cols = g * FM + m, slice(g * GW, (g + 1) * GW)
                    emptied(dve, ("gate", g, m))
                    h = silu_g[:, n % 2, :]
                    dve.scalar_tensor_tensor(h, filled(dve, ("up", g, m)), scup[:, m:m + 1], h, ALU.mult, ALU.mult
                                             ).then_inc(drained[plan[("up", g, m)][0]], 1)
                    emptied(dve, ("up", g, m))
                    link(dve.tensor_copy(hid_hi[:, m, cols], h))
                    dve.tensor_tensor(hid_lo[:, m, cols], h, hid_hi[:, m, cols].bitcast(F32), ALU.subtract
                                      ).then_inc(s_hlo, 1)
                    if g == 0 and m == FM - 2:
                        transformed_lo(1)
            for c in range(C):
                add_residual(("down", c), c)

            def row_max(c):
                for b in range(c // GC + 1):
                    filled(dve, ("sc", c, b))
                banks = score_banks(c)
                flat = psum[:, banks[0]:banks[-1] + 1, :].rearrange("p b n -> p (b n)")
                diag = flat[:, c * P:(c + 1) * P]
                link(dve.tensor_tensor(diag, diag, below, ALU.add))
                link(dve.tensor_reduce(rmaxp[:, c:c + 1], flat[:, 0:(c + 1) * P], AX.X, ALU.max))
                dve.tensor_scalar(rmax[:, c:c + 1], rmaxp[:, c:c + 1], -1.0, None, ALU.mult
                                  ).then_inc(s_mx, 1)

            def probs_out(c):
                for b in range(c // GC + 1):
                    n = min(GW, (c + 1) * P - b * GW)
                    at = turned(c) + b * GC
                    dst = probT[:, at:at + n // P, :].rearrange("p j n -> p (j n)")
                    dve.tensor_copy(dst, filled(dve, ("pt", c, b))[:, 0:n]).then_inc(drained[plan[("pt", c, b)][0]], 1)

            def attended(c):
                col = slice(c, c + 1)
                if c >= GC:
                    link(dve.tensor_tensor(rsum[:, c, 0:1], rsum[:, c, 0:1], rsum[:, c, 1:2], ALU.add))
                link(dve.reciprocal(rinv[:, col], rsum[:, c, 0:1]))
                dve.wait_ge(s_xr[1], c + 1)
                job = ("pv", c)
                dve.scalar_tensor_tensor(x[:, c, :], filled(dve, job)[:, 0:D], rinv[:, col], x[:, c, :],
                                         ALU.mult, ALU.add).then_inc(drained[plan[job][0]], 1)
                emptied(dve, job)
                stats(c)

            def choose(c):
                job = ("lg", c)
                if c == 0:
                    dve.wait_ge(s_xr[1], C)
                dve.tensor_copy(lgs[:, c, :], filled(dve, job)[:, 0:E]).then_inc(drained[plan[job][0]], 1)
                emptied(dve, job)
                link(dve.max(top[:, c, :], lgs[:, c, :]))
                link(dve.max_index(topi[:, c, :], top[:, c, :], lgs[:, c, :]))
                link(dve.tensor_copy(topf[:, c, :], topi[:, c, 0:2]))
                cols = slice(c * E, (c + 1) * E)
                for k in range(2):
                    ins = dve.tensor_scalar(oh[:, k, cols], const("iota")[:, 0:E], topf[:, c, k:k + 1], None, ALU.is_equal)
                link(ins)
                dve.tensor_tensor(oh[:, 2, cols], oh[:, 0, cols], oh[:, 1, cols], ALU.add).then_inc(s_oh, 1)

            row_max(0)
            row_max(1)
            for c in range(C):
                probs_out(c)
                if c >= 2:
                    choose(c - 2)
                if c + 2 < C:
                    row_max(c + 2)
                attended(c)
            choose(C - 2)
            choose(C - 1)
            dve.tensor_tensor(dv8[:], top[:, :, 1], top[:, :, 0], ALU.subtract).then_inc(s_gap, 1)
            n = C * E
            job = ("rank",)
            before = filled(dve, job)
            link(dve.tensor_scalar(ntile_i[:], before[:, n:n + E], float(P - 1), None, ALU.add))
            link(dve.tensor_scalar(ntile_i[:], ntile_i[:], 7, None, ALU.logical_shift_right))
            dve.tensor_copy(ntile[:], ntile_i[:])
            link(dve.tensor_copy(ends[:, 0, :], ntile_i[:]))
            for i, sh in enumerate((1, 2, 4, 8)):
                a, b = ends[:, i % 2, :], ends[:, 1 - i % 2, :]
                dve.tensor_copy(b[:, 0:sh], a[:, 0:sh])
                link(dve.tensor_tensor(b[:, sh:E], a[:, sh:E], a[:, 0:E - sh], ALU.add))
            last = ends[:, 0, :]
            link(dve.tensor_tensor(base[:], last, ntile[:], ALU.subtract))
            dve.scalar_tensor_tensor(posn.rearrange("p (c e) -> p c e", e=E), over(base[:], C), float(P),
                                     before[:, 0:n].rearrange("p (c e) -> p c e", e=E), ALU.mult, ALU.add
                                     ).then_inc(drained[plan[job][0]], 1)
            emptied(dve, job)
            link(dve.tensor_tensor(pick, over(posn, 2), oh[:, 0:2, :], ALU.mult))
            link(dve.tensor_reduce(slotf[:], pick.rearrange("p k (c e) -> p (k c) e", e=E), AX.X, ALU.add))
            link(dve.tensor_copy(slot_i[:, 0, :], slotf[:]))
            dve.tensor_scalar(slot_i[:, 1, :], slot_i[:, 0, :], P - 1, None, ALU.bitwise_and)
            link(dve.tensor_scalar(slot_i[:, 2, :], slot_i[:, 0, :], 7, None, ALU.logical_shift_right))
            dve.tensor_copy(rowf[:], slot_i[:, 1, :])
            link(dve.tensor_copy(tilef[:], slot_i[:, 2, :]))
            dve.tensor_tensor(onetile, over(const("tileno"), 2 * C), wide(tilef[:], TILES), ALU.is_equal
                              ).then_inc(s_tiles, 1)
            dve.wait_ge(s_tiles, 1)
            dve.tensor_scalar(idpair[:, :, 0, :], onetile, const("row1"), None, ALU.mult)
            for n in range(4):
                dve.tensor_tensor(onerow[:, 4 * n:4 * n + 4, :], over(const("iota"), 4),
                                  wide(rowf[:, 4 * n:4 * n + 4], P), ALU.is_equal).then_inc(s_map, 1)
            job = ("map",)
            src = filled(dve, job)
            link(dve.tensor_copy(idtmp, src[:, TILES:2 * TILES]))
            dve.tensor_tensor(id1, src[:, 0:TILES], idtmp, ALU.add).then_inc(drained[plan[job][0]], 1)
            emptied(dve, job)
            link(dve.tensor_scalar(source, id1, -1.0, 0.0, ALU.add, ALU.max))
            for t in range(LOADS):
                dve.tensor_copy(source_t[:, t:t + 1], source[:, t:t + 1]).then_inc(s_src, 1)
            tc = tcmp.rearrange("p (t e) -> p t e", e=E)
            link(dve.tensor_tensor(tc, over(last, TILES), wide(const("tileno"), E), ALU.is_le))
            link(dve.tensor_reduce(texp, tc, AX.X, ALU.add))
            dve.tensor_scalar(texp_i, texp, float(E - 1), float(EW), ALU.min, ALU.mult).then_inc(s_te, 1)
            dve.wait_ge(s_e8, 1)
            link(dve.tensor_scalar(p12[:, 1, :], ex8[:], 1.0, None, ALU.add))
            link(dve.reciprocal(p12[:, 0, :], p12[:, 1, :]))
            link(dve.tensor_tensor(p12[:, 1, :], ex8[:], p12[:, 0, :], ALU.mult))
            left = p12[:].rearrange("p k c -> p (k c)")
            for i in range(3):
                part = wparts[:, i, :]
                link(dve.tensor_copy(part, left))
                if i < 2:
                    link(dve.tensor_tensor(rest[:, i, :], left, part, ALU.subtract))
                    left = rest[:, i, :]
            for i in range(3):
                ins = dve.tensor_tensor(wpair[:, :, i, :], onetile, wide(wparts[:, i, :], TILES), ALU.mult)
            ins.then_inc(s_p, 1)
            link(dve.tensor_scalar(idtmp, id1, 0.0, const("spare"), ALU.is_equal, ALU.mult))
            link(dve.scalar_tensor_tensor(target, idtmp, -1.0, id1, ALU.add, ALU.add))
            job = ("weights",)
            src = filled(dve, job)
            link(dve.tensor_copy(idtmp, src[:, 0:TILES]))
            link(dve.tensor_tensor(weight, src[:, TILES:2 * TILES], idtmp, ALU.add))
            dve.tensor_tensor(weight, src[:, 2 * TILES:3 * TILES], weight, ALU.add
                              ).then_inc(drained[plan[job][0]], 1)
            emptied(dve, job)

            for n in range(2):
                dve.wait_ge(s_exp[n], 16 * (E // 2))

            def tile_w2(t, par):
                if not (isinstance(t, int) and t < 2):
                    dve.wait_ge(s_yf, t - 1)
                at = dve.value_load(texp_i[0:1, bass.ds(t, 1)], min_val=0, max_val=(E - 1) * EW)
                raw = experts[:, bass.ds(at + KT * FE, FEM * D)]
                dve.tensor_copy(w2_hi[:, par, :], raw).then_inc(s_w2hi, 1)
                dve.wait_ge(s_w2hi, t + 1)
                dve.tensor_tensor(w2_lo[:, par, :], raw, w2_hi[:, par, :].bitcast(F32), ALU.subtract).then_inc(s_w2, 1)

            def tile_lo(t, par):
                dve.wait_ge(s_thi, t + 1)
                dve.tensor_tensor(mh_lo[:, par, :], mh[:, par, :], mh_hi[:, par, :].bitcast(F32), ALU.subtract
                                  ).then_inc(s_tlo, 1)

            def step(t, u, load=True, last=False):
                par, n = u % 2, u % LOADS
                if not last:
                    tile_w2(t + 1, 1 - par)
                if not (isinstance(t, int) and t < 2):
                    dve.wait_ge(s_add, t * 16 - 16)
                dve.tensor_copy(target_t[:, par:par + 1], target[:, bass.ds(t, 1)])
                dve.wait_ge(s_yf, t + 1)
                dve.tensor_scalar(my[:, par, :], psum[:, 6 + par, 0:D], weight[:, bass.ds(t, 1)], None, ALU.mult
                                  ).then_inc(s_yd, 1)
                if load:
                    dve.tensor_copy(source_t[:, n:n + 1], source_span[:, bass.ds(t + LOADS, 1)]).then_inc(s_src, 1)
                if not last:
                    tile_lo(t + 1, 1 - par)

            tile_w2(0, 0)
            tile_lo(0, 0)
            for t in range(HEAD):
                step(t, t)
            with dve.Fori(HEAD, LOOPED, LOADS) as t:
                for n in range(HEAD, HEAD + LOADS):
                    step(t + (n - HEAD), n)
            for t in range(LOOPED, TILES):
                step(t, t, load=t + LOADS < TILES, last=t == TILES - 1)



def kernel(**inputs):
    import numpy as _np
    import concourse.bacc as _bacc
    from concourse import mybir as _mybir
    from concourse.bass_utils import run_bass_kernel_spmd as _run

    a = {k: _np.asarray(v) for k, v in inputs.items()}

    def rows(w):
        return _np.ascontiguousarray(w.reshape(-1, P, w.shape[-1]).transpose(1, 0, 2))

    def column(vec):
        return vec.reshape(-1, P).T

    def spread_row(vec):
        return _np.broadcast_to(vec[None, :], (P, vec.shape[0]))

    qkv = a["L1_attn_qkv"]
    su_ug, ws_ug = a["L0_ffn_SU_ug"], a["L0_ffn_Wscale_ug"]
    vectors = _np.concatenate([
        column(a["L0_attn_retn_norm_w"]), column(a["L0_attn_final_norm_w"]), column(a["L0_attn_fc1_b"]),
        column(su_ug), column(ws_ug[:F]), column(ws_ug[F:]), column(a["L0_ffn_SU_dp"]),
        column(a["L1_attn_gamma"]), column(a["L1_attn_beta"]), spread_row(a["L0_attn_fc2_b"]),
        spread_row(a["L0_ffn_Wscale_dp"])], axis=1)
    arrays = {
        "x_in": a["L0_attn_x"].reshape(T, D),
        "const_in": constants(),
        "vec_in": vectors,
        "qkvg_in": rows(_np.concatenate([a["L0_attn_q_w"], a["L0_attn_k_w"], a["L0_attn_v_w"], a["L0_attn_g_w"]], axis=1)),
        "out_w_in": rows(a["L0_attn_out_w"]),
        "fc1_in": rows(a["L0_attn_fc1_w"]),
        "fc2_in": rows(a["L0_attn_fc2_w"]),
        "upgate_in": rows(_np.concatenate([a["L0_ffn_W_up"].T, a["L0_ffn_W_gate"].T], axis=1)),
        "down_in": rows(a["L0_ffn_W_down"].T),
        "wqt_in": rows(qkv[:, :D].T),
        "wkt_in": rows(qkv[:, D:2 * D].T),
        "wvt_in": rows(qkv[:, 2 * D:].T),
        "o_in": rows(a["L1_attn_o_proj"]),
        "router_in": rows(a["L1_ffn_router_w"]),
        "experts_in": _np.concatenate([
            a["L1_ffn_W1"].reshape(E, KT, P, FE).transpose(0, 2, 1, 3).reshape(E, P, KT * FE),
            a["L1_ffn_W2"].reshape(E, FEM, P, D).transpose(0, 2, 1, 3).reshape(E, P, FEM * D)], axis=2),
    }
    nc = _bacc.Bacc("TRN2", target_bir_lowering=False, num_devices=1)
    arrays = {k: _np.ascontiguousarray(v) for k, v in arrays.items()}
    args = {k: nc.dram_tensor(k, v.shape, _mybir.dt.from_np(v.dtype), kind="ExternalInput").ap()
            for k, v in arrays.items()}
    out = nc.dram_tensor("out", (T + P, D), F32, kind="ExternalOutput").ap()
    build(nc, out=out, **args)
    r = _run(nc, [arrays], core_ids=[0])
    return r.results[0]["out"][:T].reshape(1, T, D)
```
